# Optimizing a Trainium2 kernel written in Bass

```python
import numpy as np
import jax
import jax.numpy as jnp

def _softmax(x, axis=-1):
    return jax.nn.softmax(x, axis=axis)

def _gelu(x):
    return jax.nn.gelu(x, approximate=True)

def _silu(x):
    return jax.nn.silu(x)

def _sigmoid(x):
    return jax.nn.sigmoid(x)

def _layernorm(x, axis=-1, eps=1e-05):
    m = jnp.mean(x, axis=axis, keepdims=True)
    v = jnp.var(x, axis=axis, keepdims=True)
    return (x - m) / jnp.sqrt(v + eps)

def _scatter_add(tgt, idx, src, axis=0):
    return tgt.at[idx].add(src)

def _segment_sum(src, seg, n):
    return jax.ops.segment_sum(src, seg, n)
kernel_name = 'mk_hybrid_d1_jaxref_r8_c8e238'

def setup_inputs(seed: int=0):
    np.random.seed(seed)
    _w = jnp.asarray

    def _L0_attn_a_setup():
        import jax, jax.numpy as jnp
        import numpy as np
        BATCH, SEQ, D_MODEL, N_HEADS, D_HEAD = (2, 256, 256, 16, 128)
        ATTN_SCALE = np.sqrt(D_HEAD).astype(np.float32)
        IGNORE = jnp.float32(-100000.0)
        key = jax.random.key(seed)
        ks = jax.random.split(key, 5)
        init = 1.0 / np.sqrt(D_MODEL)
        return {'x': jax.random.normal(ks[0], (BATCH, SEQ, D_MODEL), jnp.float32), 'W_Q': jax.random.normal(ks[1], (N_HEADS, D_MODEL, D_HEAD), jnp.float32) * init, 'W_K': jax.random.normal(ks[2], (N_HEADS, D_MODEL, D_HEAD), jnp.float32) * init, 'W_V': jax.random.normal(ks[3], (N_HEADS, D_MODEL, D_HEAD), jnp.float32) * init, 'W_O': jax.random.normal(ks[4], (N_HEADS, D_HEAD, D_MODEL), jnp.float32) * init, 'b_Q': jnp.zeros((N_HEADS, D_HEAD), jnp.float32), 'b_K': jnp.zeros((N_HEADS, D_HEAD), jnp.float32), 'b_V': jnp.zeros((N_HEADS, D_HEAD), jnp.float32), 'b_O': jnp.zeros((D_MODEL,), jnp.float32)}
    _L0_attn_a_in = _L0_attn_a_setup()

    def _L0_attn_b_setup():
        import jax, jax.numpy as jnp
        import numpy as np
        EMBED = 256
        HEADS = 16
        NOPE = 128
        VDIM = 128
        ROPE = 64
        Q_HEAD = NOPE + ROPE
        KV_RANK = 64
        BASE = 10000.0

        def _rope(x, offset=0):
            d = x.shape[-1]
            n = x.shape[-2]
            theta = BASE ** (-2.0 * jnp.arange(d // 2, dtype=jnp.float32) / d)
            pos = jnp.arange(n, dtype=jnp.float32) + offset
            ang = pos[:, None] * theta[None, :]
            cos, sin = (jnp.cos(ang), jnp.sin(ang))
            x1 = x[..., 0::2]
            x2 = x[..., 1::2]
            o1 = x1 * cos - x2 * sin
            o2 = x1 * sin + x2 * cos
            return jnp.stack([o1, o2], axis=-1).reshape(x.shape)
        key = jax.random.key(seed)
        ks = jax.random.split(key, 6)
        b, n = (2, 256)
        s = lambda fin: 1.0 / np.sqrt(fin)
        return {'x': jax.random.normal(ks[0], (b, n, EMBED), jnp.float32), 'Wqa': jax.random.normal(ks[1], (EMBED, 64), jnp.float32) * s(EMBED), 'Wqb': jax.random.normal(ks[2], (64, HEADS * Q_HEAD), jnp.float32) * s(64), 'Wkva': jax.random.normal(ks[3], (EMBED, KV_RANK + ROPE), jnp.float32) * s(EMBED), 'Wkvb': jax.random.normal(ks[4], (KV_RANK, HEADS * (NOPE + VDIM)), jnp.float32) * s(KV_RANK), 'Wout': jax.random.normal(ks[5], (HEADS * VDIM, EMBED), jnp.float32) * s(HEADS * VDIM)}
    _L0_attn_b_in = _L0_attn_b_setup()

    def _L0_ffn_setup():
        import jax, jax.numpy as jnp
        import numpy as np
        L, B, D = (256, 1, 256)
        H = 16
        DK, DV = (D // 2, D)
        HDK, HDV = (DK // H, DV // H)
        RATIO = 2
        BASE = 10000.0
        EPS = 1e-05

        def _apply_rotary(x, cos, sin):
            d2 = x.shape[-1] // 2
            x1, x2 = (x[..., :d2], x[..., d2:])
            return jnp.concatenate([x1 * cos - x2 * sin, x2 * cos + x1 * sin], axis=-1)
        key = jax.random.key(seed)
        ks = jax.random.split(key, 8)
        s = 0.02
        return {'x': jax.random.normal(ks[0], (L, B, D), jnp.float32), 'conv_w': jax.random.normal(ks[1], (D, 2), jnp.float32) * 0.5, 'Wq': jax.random.normal(ks[2], (D, DK), jnp.float32) * s, 'Wk': jax.random.normal(ks[3], (D, DK), jnp.float32) * s, 'Wv': jax.random.normal(ks[4], (D, DV), jnp.float32) * s, 'Wg': jax.random.normal(ks[5], (D, DV), jnp.float32) * s, 'router_w': jax.random.normal(ks[6], (H, HDV, RATIO), jnp.float32) * s, 'Wout': jax.random.normal(ks[7], (DV, D), jnp.float32) * s}
    _L0_ffn_in = _L0_ffn_setup()
    _d = {'L0_attn_a_x': _L0_attn_a_in['x'], 'L0_attn_a_W_Q': _L0_attn_a_in['W_Q'], 'L0_attn_a_W_K': _L0_attn_a_in['W_K'], 'L0_attn_a_W_V': _L0_attn_a_in['W_V'], 'L0_attn_a_W_O': _L0_attn_a_in['W_O'], 'L0_attn_a_b_Q': _L0_attn_a_in['b_Q'], 'L0_attn_a_b_K': _L0_attn_a_in['b_K'], 'L0_attn_a_b_V': _L0_attn_a_in['b_V'], 'L0_attn_a_b_O': _L0_attn_a_in['b_O'], 'L0_attn_b_Wqa': _L0_attn_b_in['Wqa'], 'L0_attn_b_Wqb': _L0_attn_b_in['Wqb'], 'L0_attn_b_Wkva': _L0_attn_b_in['Wkva'], 'L0_attn_b_Wkvb': _L0_attn_b_in['Wkvb'], 'L0_attn_b_Wout': _L0_attn_b_in['Wout'], 'L0_ffn_conv_w': _L0_ffn_in['conv_w'], 'L0_ffn_Wq': _L0_ffn_in['Wq'], 'L0_ffn_Wk': _L0_ffn_in['Wk'], 'L0_ffn_Wv': _L0_ffn_in['Wv'], 'L0_ffn_Wg': _L0_ffn_in['Wg'], 'L0_ffn_router_w': _L0_ffn_in['router_w'], 'L0_ffn_Wout': _L0_ffn_in['Wout']}
    _x0 = _d['L0_attn_a_x']
    _d['L0_attn_a_x'] = jax.random.normal(jax.random.fold_in(jax.random.key(seed), 1), (4, 512, 256), dtype=_x0.dtype)
    del _x0
    return _d

def reference(L0_attn_a_x, L0_attn_a_W_Q, L0_attn_a_W_K, L0_attn_a_W_V, L0_attn_a_W_O, L0_attn_a_b_Q, L0_attn_a_b_K, L0_attn_a_b_V, L0_attn_a_b_O, L0_attn_b_Wqa, L0_attn_b_Wqb, L0_attn_b_Wkva, L0_attn_b_Wkvb, L0_attn_b_Wout, L0_ffn_conv_w, L0_ffn_Wq, L0_ffn_Wk, L0_ffn_Wv, L0_ffn_Wg, L0_ffn_router_w, L0_ffn_Wout):

    def _L0_attn_a_ref(x, W_Q, W_K, W_V, W_O, b_Q, b_K, b_V, b_O):
        import jax, jax.numpy as jnp
        import numpy as np
        BATCH, SEQ, D_MODEL, N_HEADS, D_HEAD = (2, 256, 256, 16, 128)
        ATTN_SCALE = np.sqrt(D_HEAD).astype(np.float32)
        IGNORE = jnp.float32(-100000.0)
        q = jnp.einsum('bpd,hde->bphe', x, W_Q) + b_Q
        k = jnp.einsum('bpd,hde->bphe', x, W_K) + b_K
        v = jnp.einsum('bpd,hde->bphe', x, W_V) + b_V
        scores = jnp.einsum('bqhe,bkhe->bhqk', q, k) / ATTN_SCALE
        S = x.shape[1]
        causal = jnp.tril(jnp.ones((S, S), bool))
        scores = jnp.where(causal, scores, IGNORE)
        attn = jax.nn.softmax(scores, axis=-1)
        z = jnp.einsum('bkhe,bhqk->bqhe', v, attn)
        out = jnp.einsum('bqhe,hed->bqd', z, W_O) + b_O
        return out

    def _L0_attn_b_ref(x, Wqa, Wqb, Wkva, Wkvb, Wout):
        import jax, jax.numpy as jnp
        import numpy as np
        EMBED = 256
        HEADS = 16
        NOPE = 128
        VDIM = 128
        ROPE = 64
        Q_HEAD = NOPE + ROPE
        KV_RANK = 64
        BASE = 10000.0

        def _rope(x, offset=0):
            d = x.shape[-1]
            n = x.shape[-2]
            theta = BASE ** (-2.0 * jnp.arange(d // 2, dtype=jnp.float32) / d)
            pos = jnp.arange(n, dtype=jnp.float32) + offset
            ang = pos[:, None] * theta[None, :]
            cos, sin = (jnp.cos(ang), jnp.sin(ang))
            x1 = x[..., 0::2]
            x2 = x[..., 1::2]
            o1 = x1 * cos - x2 * sin
            o2 = x1 * sin + x2 * cos
            return jnp.stack([o1, o2], axis=-1).reshape(x.shape)
        b, n, _ = x.shape
        q = x @ Wqa @ Wqb
        q = q.reshape(b, n, HEADS, Q_HEAD).transpose(0, 2, 1, 3)
        q_nope, q_pe = (q[..., :NOPE], q[..., NOPE:])
        ckv = x @ Wkva
        compressed, k_pe = (ckv[..., :KV_RANK], ckv[..., KV_RANK:])
        k_pe = jnp.broadcast_to(k_pe[:, None], (b, HEADS, n, ROPE))
        kv = compressed @ Wkvb
        kv = kv.reshape(b, n, HEADS, NOPE + VDIM).transpose(0, 2, 1, 3)
        k_nope, v = (kv[..., :NOPE], kv[..., NOPE:])
        q_pe = _rope(q_pe)
        k_pe = _rope(k_pe)
        qf = jnp.concatenate([q_nope, q_pe], axis=-1)
        kf = jnp.concatenate([k_nope, k_pe], axis=-1)
        scale = 1.0 / np.sqrt(Q_HEAD)
        scores = jnp.einsum('bhnd,bhmd->bhnm', qf, kf) * scale
        causal = jnp.tril(jnp.ones((n, n), dtype=bool))
        scores = jnp.where(causal, scores, jnp.finfo(scores.dtype).min)
        attn = jax.nn.softmax(scores, axis=-1)
        out = jnp.einsum('bhnm,bhmd->bhnd', attn, v)
        out = out.transpose(0, 2, 1, 3).reshape(b, n, HEADS * VDIM)
        return out @ Wout

    def _L0_ffn_ref(x, conv_w, Wq, Wk, Wv, Wg, router_w, Wout):
        import jax, jax.numpy as jnp
        import numpy as np
        L, B, D = (256, 1, 256)
        H = 16
        DK, DV = (D // 2, D)
        HDK, HDV = (DK // H, DV // H)
        RATIO = 2
        BASE = 10000.0
        EPS = 1e-05

        def _apply_rotary(x, cos, sin):
            d2 = x.shape[-1] // 2
            x1, x2 = (x[..., :d2], x[..., d2:])
            return jnp.concatenate([x1 * cos - x2 * sin, x2 * cos + x1 * sin], axis=-1)
        x = jnp.transpose(x, (1, 0, 2))
        b, l, d = x.shape
        x_prev = jnp.pad(x, ((0, 0), (1, 0), (0, 0)))[:, :l]
        x = jax.nn.silu(x_prev * conv_w[:, 0] + x * conv_w[:, 1])
        q = jax.nn.silu(x @ Wq)
        k = x @ Wk
        v = x @ Wv
        g = x @ Wg
        q = q.reshape(b, l, H, HDK).transpose(0, 2, 1, 3)
        k = k.reshape(b, l, H, HDK).transpose(0, 2, 1, 3)
        v = v.reshape(b, l, H, HDV).transpose(0, 2, 1, 3)
        inv_freq = 1.0 / BASE ** (jnp.arange(0, HDK, 2, dtype=jnp.float32) / HDK)
        freqs = jnp.arange(l, dtype=jnp.float32)[:, None] * inv_freq[None, :]
        cos, sin = (jnp.cos(freqs), jnp.sin(freqs))
        q = _apply_rotary(q, cos, sin)
        k = _apply_rotary(k, cos, sin)
        logits = jnp.einsum('bhld,hdr->bhlr', v, router_w)
        scores = jax.nn.softmax(logits, axis=-1)
        onehot = jax.nn.one_hot(jnp.argmax(scores, axis=-1), RATIO, dtype=scores.dtype)
        masked_scores = scores * onehot
        masked_ind = onehot
        sum_ind = jnp.cumsum(masked_ind, axis=2)
        norm = jnp.where(sum_ind > 0, 1.0 / jnp.maximum(sum_ind, 1.0), 0.0)[..., None]
        q_exp = q[:, :, :, None, :] * masked_scores[..., None] * norm
        k_exp = k[:, :, :, None, :] * masked_ind[..., None]
        q_exp = q_exp.reshape(b, H, l, RATIO * HDK)
        k_exp = k_exp.reshape(b, H, l, RATIO * HDK)
        qk = jnp.einsum('bhld,bhmd->bhlm', q_exp, k_exp) * HDK ** (-0.5)
        mask = jnp.tril(jnp.ones((l, l), dtype=qk.dtype))
        qk = qk * mask
        o = jnp.einsum('bhlm,bhmd->bhld', qk, v)
        o = o.transpose(0, 2, 1, 3)
        mu = jnp.mean(o, axis=-1, keepdims=True)
        var = jnp.var(o, axis=-1, keepdims=True)
        o = (o - mu) / jnp.sqrt(var + EPS)
        out = jax.nn.silu(g) * o.reshape(b, l, d)
        out = out @ Wout
        return jnp.transpose(out, (1, 0, 2))
    x = L0_attn_a_x
    x = x + _L0_attn_a_ref(_layernorm(x, axis=-1), L0_attn_a_W_Q, L0_attn_a_W_K, L0_attn_a_W_V, L0_attn_a_W_O, L0_attn_a_b_Q, L0_attn_a_b_K, L0_attn_a_b_V, L0_attn_a_b_O)
    x = x + _L0_ffn_ref(_layernorm(x, axis=-1), L0_ffn_conv_w, L0_ffn_Wq, L0_ffn_Wk, L0_ffn_Wv, L0_ffn_Wg, L0_ffn_router_w, L0_ffn_Wout)
    x = x + _L0_attn_b_ref(_layernorm(x, axis=-1), L0_attn_b_Wqa, L0_attn_b_Wqb, L0_attn_b_Wkva, L0_attn_b_Wkvb, L0_attn_b_Wout)
    x = x + _L0_ffn_ref(_layernorm(x, axis=-1), L0_ffn_conv_w, L0_ffn_Wq, L0_ffn_Wk, L0_ffn_Wv, L0_ffn_Wg, L0_ffn_router_w, L0_ffn_Wout)
    return x

_drawn_inputs = setup_inputs


def setup_inputs(seed=0):
    import zlib

    import numpy as np

    out = dict(_drawn_inputs(seed))
    spreads = {'L0_attn_a_b_Q': (0.0, 0.1),
     'L0_attn_a_b_K': (0.0, 0.8),
     'L0_attn_a_b_V': (0.0, 0.1),
     'L0_attn_a_b_O': (0.0, 0.1)}
    factors = {'L0_ffn_conv_w': 8.0,
     'L0_ffn_Wq': 8.0,
     'L0_ffn_Wk': 8.0,
     'L0_ffn_Wv': 8.0,
     'L0_ffn_Wg': 8.0,
     'L0_ffn_router_w': 8.0,
     'L0_ffn_Wout': 8.0}
    for name, (base, spread) in spreads.items():
        noise = np.random.default_rng([zlib.crc32(name.encode()), seed]).standard_normal(out[name].shape)
        drawn = base * np.exp(spread * noise) if base else spread * noise
        out[name] = jnp.asarray(drawn.astype(out[name].dtype))
    for name, factor in factors.items():
        out[name] = (out[name] * factor).astype(out[name].dtype)
    return out
```

```python
from contextlib import ExitStack

import numpy as np
import concourse.bass as bass
from concourse import mybir

F32 = mybir.dt.float32
F32R = mybir.dt.float32r
BF16 = mybir.dt.bfloat16
ALU = mybir.AluOpType
ACT = mybir.ActivationFunctionType
AX = mybir.AxisListType

P = 128
BATCH, SEQ, DM = 4, 512, 256
TOK = BATCH * SEQ
NT = TOK // P
TPB = SEQ // P
KT = DM // P
HEADS = 16
DH = 128
GH = 2
NG = HEADS // GH
GW = GH * DH
ROPE = 64
RANK = 64
NOPE = 128
MIX_DK, MIX_DV, MIX_H = 128, 256, 16
MIX_HDK, MIX_HDV = MIX_DK // MIX_H, MIX_DV // MIX_H
EPS = 1e-5
MASKED = -1.0e30
SCALE_A = float(DH) ** -0.5
SCALE_B = float(NOPE + ROPE) ** -0.5
ROT_COLS = BATCH * 2 * MIX_DK


class Stream:

    def __init__(self, sem):
        self.sem, self.count, self.steps, self.passed = sem, 0, [], {}

    def wait(self, *marks):
        for sem, value in marks:
            if self.passed.get(id(sem), 0) < value:
                self.passed[id(sem)] = value
                self.steps.append(lambda e, s=sem, v=value: e.wait_ge(s, v))

    def do(self, step):
        self.steps.append(step)

    def counted(self, step):
        self.steps.append(lambda e: step(e).then_inc(self.sem, 1))
        self.count += 1
        return (self.sem, self.count)

    def last(self):
        return (self.sem, self.count)

    def dma(self, out, in_, sem):
        self.steps.append(lambda e: e.dma_start(out, in_).then_inc(sem, 16))

    def play(self, engine):
        for step in self.steps:
            step(engine)


def before(marks, n, *rest):
    return marks[(n, *rest) if rest else n] if n >= 0 else ()


def three_pass(pe, out, w_hi, w_lo, x_hi, x_lo, start, stop, skip=False):
    pe.do(lambda e: e.matmul(out, w_hi, x_hi, start=start, stop=False, skip_group_check=skip))
    pe.do(lambda e: e.matmul(out, w_hi, x_lo, start=False, stop=False, skip_group_check=skip))
    return lambda e: e.matmul(out, w_lo, x_hi, start=False, stop=stop, skip_group_check=skip)


def hybrid_program(nc, x, wa, ba, bo, ident, mask, wqa, wqb_t, wqb_pe, wqb_sw, wkva, wkvbk_t, wkvbv_t,
                   wout_b, rope_tab, conv_w, wmix, wv_t, router, wmix_out, rot_tab, tri, out):
    top = ExitStack()
    with top:
        def sem(name):
            return top.enter_context(nc.semaphore(name))

        def allocator(stack):
            return lambda name, shape, dt=F32: stack.enter_context(nc.sbuf_tensor(name, shape, dt))

        keep = allocator(top)
        pe, act, dve, pool, sp = (Stream(sem(n)) for n in
                                  ("pe_steps", "act_steps", "dve_steps", "pool_steps", "sp_steps"))
        engines = (pe, act, dve, pool)
        bank = [top.enter_context(nc.psum_tensor(f"bank{i}", [P, 512], F32)) for i in range(8)]

        X = keep("X", [P, NT, DM])
        XT_hi = keep("XT_hi", [P, KT, TOK], F32R)
        XT_lo = keep("XT_lo", [P, KT, TOK], F32R)
        ident_f = keep("ident_f", [P, P])
        ident_b = keep("ident_b", [P, P], BF16)
        mask_b = keep("mask_b", [P, P], BF16)
        stats = keep("stats", [P, NT, 6])
        moments = keep("moments", [P, NT, 2])
        std = keep("std", [P, NT])
        rstd = keep("rstd", [P, NT])
        xn = keep("xn", [P, 4, DM])

        dma_x = [sem(f"dma_x{b}") for b in range(BATCH)]
        dma_const = sem("dma_const")
        dma_out = sem("dma_out")

        x_tiles = x.rearrange("(t p) d -> p t d", p=P)
        out_tiles = out.rearrange("(t p) d -> p t d", p=P)
        for b in range(BATCH):
            sp.dma(X[:, 4 * b:4 * b + 4, :], x_tiles[:, 4 * b:4 * b + 4, :], dma_x[b])
            if b == 0:
                sp.dma(ident_f[:, :], ident, dma_const)

        def barrier():
            marks = [s.last() for s in engines if s.count]
            for s in (*engines, sp):
                s.wait(*marks)

        xn_free = {}

        def norm_stats(tile_marks):
            for t in range(NT):
                dve.wait(tile_marks[t])
                m = dve.counted(lambda e, t=t: e.bn_stats(stats[:, t, :], X[:, t, :]))
                if t % 4 == 3:
                    dve.wait(m)
                    for u in range(t - 3, t + 1):
                        m = dve.counted(lambda e, u=u: e.bn_aggr(moments[:, u, :], stats[:, u, :]))
            dve.wait(m)
            m = dve.counted(lambda e: e.tensor_scalar(std[:, :], moments[:, :, 1], EPS, None, ALU.add))
            act.wait(m)
            m = act.counted(lambda e: e.activation(std[:, :], std[:, :], ACT.Sqrt))
            dve.wait(m)
            return dve.counted(lambda e: e.reciprocal(rstd[:, :], std[:, :]))

        def norm_tile(t, k, free):
            dve.wait(*free)
            return dve.counted(lambda e: e.tensor_scalar(xn[:, k, :], X[:, t, :], moments[:, t, 0:1],
                                                        rstd[:, t:t + 1], ALU.subtract, ALU.mult))

        def transpose_four(tiles, ready, banks, free):
            marks = []
            pe.wait(*ready)
            for f in range(KT):
                pe.wait(*free[f])
                for k in range(4):
                    step = (lambda e, f=f, k=k: e.transpose(bank[banks[f]][:, k * P:(k + 1) * P],
                                                            xn[:, k, f * P:(f + 1) * P], ident_f[:, :]))
                    if k < 3:
                        pe.do(step)
                marks.append(pe.counted(step))
            return marks

        def split_from(psum_ap, hi, lo, ready, free=(), bias=None, scale=None):
            act.wait(ready, *free)
            if bias is None:
                m_hi = act.counted(lambda e: e.activation(hi, psum_ap, ACT.Copy))
            else:
                m_hi = act.counted(lambda e: e.activation(hi, psum_ap, ACT.Identity, bias=bias))
            dve.wait(m_hi)
            if bias is None:
                m_lo = dve.counted(lambda e: e.tensor_tensor(lo, psum_ap, hi.bitcast(F32), ALU.subtract))
            else:
                m_lo = dve.counted(lambda e: e.scalar_tensor_tensor(
                    out=lo, in0=psum_ap, scalar=bias, in1=hi.bitcast(F32), op0=ALU.add, op1=ALU.subtract))
            return m_hi, m_lo

        def norm_transposed(tile_marks):
            m_stats = norm_stats(tile_marks)
            dve.wait(m_stats)
            ready_at, prev_t, freed = [], None, {0: (), 1: (), 2: (), 3: ()}
            for b in range(BATCH):
                ms = [norm_tile(4 * b + k, k, [prev_t] if prev_t else []) for k in range(4)]
                bks = (0, 1) if b % 2 == 0 else (2, 3)
                mt = transpose_four(range(4 * b, 4 * b + 4), ms, bks, [freed[bks[0]], freed[bks[1]]])
                prev_t = mt[-1]
                los = []
                for f in range(KT):
                    cols = slice(b * SEQ, (b + 1) * SEQ)
                    _, lo = split_from(bank[bks[f]][:, :], XT_hi[:, f, cols], XT_lo[:, f, cols], mt[f])
                    freed[bks[f]] = (lo,)
                    los.append(lo)
                ready_at.append(los[-1])
            return ready_at

        class Core:

            def __init__(self, al, tag, split):
                self.split = split
                self.negmax = al(f"{tag}_negmax", [P, 8, TPB])
                self.rowsum = al(f"{tag}_rowsum", [P, 8, TPB])
                self.rinv = al(f"{tag}_rinv", [P, 8, TPB])
                self.probs = al(f"{tag}_probs", [P, TPB, SEQ])
                self.s_banks, self.t_banks, self.acc_banks = (0, 1, 2), (3, 4), (5, 6, 7)
                self.s_free, self.t_free, self.acc_free = {}, {}, {}
                self.n_s = self.n_t = self.n_acc = 0
                self.norm, self.transposed, self.pt = {}, {}, {}

            def next_acc(self):
                k = self.acc_banks[self.n_acc % 3]
                self.n_acc += 1
                pe.wait(*self.acc_free.get(k, ()))
                return k

            def scores(self, n, i, q_hi, q_lo, k_hi, k_lo, ready):
                k = self.s_banks[self.n_s % 3]
                self.n_s += 1
                cols = P * (i + 1)
                s_ap, diag = bank[k][:, 0:cols], bank[k][:, P * i:cols]
                slot = n % 8
                pe.wait(*ready, *self.s_free.get(k, ()))
                qs = slice(P * i, P * i + P)
                pe.do(lambda e: e.matmul(s_ap, q_hi[:, qs], k_hi[:, 0:cols], start=True, stop=False))
                pe.do(lambda e: e.matmul(diag, ident_b[:, :], mask_b[:, :], start=False, stop=False))
                pe.do(lambda e: e.matmul(s_ap, q_hi[:, qs], k_lo[:, 0:cols], start=False, stop=False))
                done = pe.counted(lambda e: e.matmul(s_ap, q_lo[:, qs], k_hi[:, 0:cols],
                                                    start=False, stop=True))
                nm = self.negmax[:, slot, i:i + 1]
                rs = self.rowsum[:, slot, i:i + 1]
                ri = self.rinv[:, slot, i:i + 1]
                pr = self.probs[:, i, 0:cols]
                dve.wait(done)
                m = dve.counted(lambda e: e.tensor_reduce(nm, s_ap, AX.X, ALU.max, negate=True))
                act.wait(m, *(before(self.transposed, n - 1, i)))
                m = act.counted(lambda e: e.activation(pr, s_ap, ACT.Exp, bias=nm, accum_out=rs))
                self.s_free[k] = (m,)
                self.pending = (n, i, m, ri, rs, pr, cols)
                return done

            def normalise(self, pending):
                n, i, m, ri, rs, pr, cols = pending
                dve.wait(m)
                m = dve.counted(lambda e: e.reciprocal(ri, rs))
                pool.wait(m, pool.last())
                self.norm[n, i] = pool.counted(
                    lambda e: e.tensor_tensor(pr, pr, ri.to_broadcast([P, cols]), ALU.mult))

            def transposes(self, n, i, dst, free):
                k = self.t_banks[self.n_t % 2]
                self.n_t += 1
                pe.wait(self.norm[n, i], *self.t_free.get(k, ()))
                for j in range(i + 1):
                    step = (lambda e, j=j: e.transpose(bank[k][:, P * j:P * j + P],
                                                       self.probs[:, i, P * j:P * j + P], ident_f[:, :]))
                    if j < i:
                        pe.do(step)
                done = pe.counted(step)
                self.transposed[n, i] = (done,)
                src = bank[k][:, 0:P * (i + 1)].rearrange("p (j q) -> p j q", q=P)
                qs = slice(P * i, P * i + P)
                if self.split:
                    hi, lo = dst
                    _, m = split_from(src, hi[:, 0:i + 1, qs], lo[:, 0:i + 1, qs], done, free)
                elif i % 2:
                    act.wait(done, *free)
                    m = act.counted(lambda e: e.activation(dst[:, 0:i + 1, qs], src, ACT.Copy))
                else:
                    dve.wait(done, *free)
                    m = dve.counted(lambda e: e.tensor_copy(dst[:, 0:i + 1, qs], src))
                self.t_free[k] = (m,)
                self.pt[n, i] = m

        def attention_a():
            ctx = ExitStack()
            al = allocator(ctx)
            GWORDS = 2048
            raw = al("a_raw", [P, GWORDS])
            W_hi = al("a_W_hi", [P, 2, GWORDS], F32R)
            W_lo = al("a_W_lo", [P, 2, GWORDS], F32R)
            bias = al("a_bias", [P, 3, HEADS])
            bo_bc = al("a_bo", [P, DM])
            mask_f = al("a_mask_f", [P, P])
            Q_hi, Q_lo, K_hi, K_lo = (al(f"a_{n}", [P, 2, SEQ], F32R) for n in ("Qh", "Ql", "Kh", "Kl"))
            V_hi, V_lo = (al(f"a_{n}", [P, 2, TPB, GW], F32R) for n in ("Vh", "Vl"))
            PT_hi, PT_lo = (al(f"a_{n}", [P, 2, TPB, SEQ], F32R) for n in ("PTh", "PTl"))
            Z_hi, Z_lo = (al(f"a_{n}", [P, 2, GH, SEQ], F32R) for n in ("Zh", "Zl"))
            core = Core(al, "a", split=True)
            dma_w = [sem(f"dma_wa{g}") for g in range(NG)]
            dma_b = sem("dma_ba")

            def wq(t, s): return t[:, s, 0:512].rearrange("p (k h e) -> p k h e", k=KT, h=GH)
            def wk(t, s): return t[:, s, 512:1024].rearrange("p (k h e) -> p k h e", k=KT, h=GH)
            def wv(t, s): return t[:, s, 1024:1536].rearrange("p (k n) -> p k n", k=KT)
            def wo(t, s): return t[:, s, 1536:2048].rearrange("p (h d) -> p h d", h=GH)

            sp.dma(raw[:, :], wa[0], dma_w[0])
            sp.dma(bias[:, :, :], ba, dma_b)
            sp.dma(bo_bc[:, :], bo.to_broadcast([P, DM]), dma_b)
            sp.dma(mask_f[:, :], mask, dma_b)

            dve.wait((dma_const, 16), (dma_b, 48))
            dve.do(lambda e: e.tensor_copy(ident_b[:, :], ident_f[:, :]))
            dve.do(lambda e: e.tensor_copy(mask_b[:, :], mask_f[:, :]))
            consts = dve.counted(lambda e: e.tensor_scalar(bias[:, 0, :], bias[:, 0, :], SCALE_A, None,
                                                          ALU.mult))
            act.wait(consts)
            pe.wait(consts)
            dve.wait(consts)

            xt_ready = norm_transposed([(dma_x[t // 4], 16) for t in range(NT)])

            pool.wait(xt_ready[-1], consts)
            bias_in = pool.counted(lambda e: e.tensor_tensor(
                X[:, :, :], X[:, :, :], bo_bc[:, :].unsqueeze(1).to_broadcast([P, NT, DM]), ALU.add))

            w_ready, w_read = {}, {}
            raw_free = None

            def split_weights(g):
                nonlocal raw_free
                s = g % 2
                pool.wait((dma_w[g], 16), *before(w_read, g - 2))
                m = pool.counted(lambda e: e.tensor_scalar(raw[:, 0:512], raw[:, 0:512], SCALE_A, None,
                                                          ALU.mult))
                pool.wait(m)
                m = pool.counted(lambda e: e.tensor_scalar(W_hi[:, s, :], raw[:, :], 1.0, None, ALU.mult))
                pool.wait(m)
                m = pool.counted(lambda e: e.tensor_tensor(W_lo[:, s, :], raw[:, :],
                                                          W_hi[:, s, :].bitcast(F32), ALU.subtract))
                w_ready[g] = m
                if g + 1 < NG:
                    sp.wait(m)
                    sp.dma(raw[:, :], wa[g + 1], dma_w[g + 1])

            units = NG * BATCH * GH
            qk_ready, s_done, v_ready, av_done, z_ready, o_done = {}, {}, {}, {}, {}, {}

            def place(n):
                return n // 8, (n % 8) // 2, n % 2

            def project(n, which):
                g, b, hh = place(n)
                s, cols = g % 2, slice(b * SEQ, (b + 1) * SEQ)
                view = (wq, wk)[which]
                hi, lo = ((Q_hi, Q_lo), (K_hi, K_lo))[which]
                k = core.next_acc()
                pe.wait(w_ready[g], xt_ready[b])
                for kt in range(KT):
                    step = three_pass(pe, bank[k][:, :], view(W_hi, s)[:, kt, hh, :],
                                      view(W_lo, s)[:, kt, hh, :], XT_hi[:, kt, cols],
                                      XT_lo[:, kt, cols], kt == 0, kt == KT - 1)
                    if kt < KT - 1:
                        pe.do(step)
                m = pe.counted(step)
                h = g * GH + hh
                _, m = split_from(bank[k][:, :], hi[:, n % 2, :], lo[:, n % 2, :], m,
                                  before(s_done, n - 2), bias=bias[:, which, h:h + 1])
                core.acc_free[k] = (m,)
                qk_ready[n, which] = m

            def project_v(u, half):
                g, b = u // BATCH, u % BATCH
                s = g % 2
                k = core.next_acc()
                pe.wait(w_ready[g], xt_ready[b])
                for tt in range(2):
                    cols = slice(b * SEQ + (2 * half + tt) * P, b * SEQ + (2 * half + tt + 1) * P)
                    for kt in range(KT):
                        step = three_pass(pe, bank[k][:, tt * GW:(tt + 1) * GW], XT_hi[:, kt, cols],
                                          XT_lo[:, kt, cols], wv(W_hi, s)[:, kt, :],
                                          wv(W_lo, s)[:, kt, :], kt == 0, kt == KT - 1)
                        if tt == 0 or kt < KT - 1:
                            pe.do(step)
                m = pe.counted(step)
                src = bank[k][:, :].rearrange("p (t n) -> p t n", t=2)
                tts = slice(2 * half, 2 * half + 2)
                _, m = split_from(src, V_hi[:, u % 2, tts, :], V_lo[:, u % 2, tts, :], m,
                                  before(av_done, 2 * (u - 2) + 1))
                core.acc_free[k] = (m,)
                v_ready[u, half] = m

            def scores(n, i):
                q = n % 2
                m = core.scores(n, i, Q_hi[:, q, :], Q_lo[:, q, :], K_hi[:, q, :], K_lo[:, q, :],
                                [qk_ready[n, 0], qk_ready[n, 1]])
                s_done[n] = (m,)
                return core.pending

            def values(n):
                g, b, hh = place(n)
                u, q = n // 2, n % 2
                k = core.next_acc()
                pe.wait(v_ready[u, 0], v_ready[u, 1], core.pt[n, TPB - 1])
                for i in range(TPB):
                    pe.wait(core.pt[n, i])
                hs = slice(hh * DH, (hh + 1) * DH)
                for j in range(TPB):
                    qs = slice(P * j, SEQ)
                    step = three_pass(pe, bank[k][:, qs], V_hi[:, u % 2, j, hs], V_lo[:, u % 2, j, hs],
                                      PT_hi[:, q, j, qs], PT_lo[:, q, j, qs], j == 0, j == TPB - 1)
                    if j < TPB - 1:
                        pe.do(step)
                m = pe.counted(step)
                av_done[n] = (m,)
                h = g * GH + hh
                _, m = split_from(bank[k][:, :], Z_hi[:, u % 2, hh, :], Z_lo[:, u % 2, hh, :], m,
                                  before(o_done, u - 2), bias=bias[:, 2, h:h + 1])
                core.acc_free[k] = (m,)
                z_ready[u, hh] = m

            def output(u, half):
                g, b = u // BATCH, u % BATCH
                s = g % 2
                k = core.next_acc()
                pe.wait(z_ready[u, 0], z_ready[u, 1])
                for tt in range(2):
                    cols = slice((2 * half + tt) * P, (2 * half + tt + 1) * P)
                    for hh in range(GH):
                        step = three_pass(pe, bank[k][:, tt * DM:(tt + 1) * DM],
                                          Z_hi[:, u % 2, hh, cols], Z_lo[:, u % 2, hh, cols],
                                          wo(W_hi, s)[:, hh, :], wo(W_lo, s)[:, hh, :],
                                          hh == 0, hh == GH - 1)
                        if tt == 0 or hh < GH - 1:
                            pe.do(step)
                m = pe.counted(step)
                if half == 1:
                    o_done[u] = (m,)
                    if b == BATCH - 1:
                        w_read[g] = (m,)
                t0 = 4 * b + 2 * half
                dve.wait(m, bias_in, *x_added.get(t0, ()))
                m = dve.counted(lambda e: e.tensor_tensor(
                    X[:, t0:t0 + 2, :], X[:, t0:t0 + 2, :],
                    bank[k][:, :].rearrange("p (t d) -> p t d", t=2), ALU.add))
                x_added[t0] = x_added[t0 + 1] = (m,)
                core.acc_free[k] = (m,)

            x_added = {}
            split_weights(0)
            pool_todo = []
            project(0, 0)
            project(0, 1)
            split_weights(1)
            for n in range(units + 5):
                g, b, hh = place(n)
                if n % 8 == 5 and n > 8 and g + 1 < NG:
                    split_weights(g + 1)
                u = n // 2
                for i in range(TPB):
                    if 1 <= n <= units:
                        core.transposes(n - 1, i, (PT_hi[:, (n - 1) % 2, :, :], PT_lo[:, (n - 1) % 2, :, :]),
                                        before(av_done, n - 3))
                    pend = scores(n, i) if n < units else None
                    if pool_todo:
                        core.normalise(pool_todo.pop())
                    if pend:
                        pool_todo.append(pend)
                    if i == 0 and n + 1 < units:
                        project(n + 1, 0)
                    if i == 1 and n + 1 < units:
                        project(n + 1, 1)
                    if i == 2 and n < units:
                        project_v(u, hh)
                    if i == 2 and n >= 2 and n - 2 < units:
                        values(n - 2)
                    if i == 3 and n >= 4 and (n - 4) // 2 < units // 2:
                        output((n - 4) // 2, hh)
            barrier()
            ctx.close()
            return [x_added[t][0] for t in range(NT)]

        def mixture(tag, tile_marks, last):
            ctx = ExitStack()
            al0 = allocator(ctx)
            al = lambda name, shape, dt=F32: al0(f"{tag}_{name}", shape, dt)
            NW = 2 * MIX_DK + 2 * MIX_DV
            NL = 2 * MIX_H
            raw = al("raw", [P, KT, NW + NL])
            W_hi, W_lo = (al(n, [P, KT, NW + NL], F32R) for n in ("W_hi", "W_lo"))
            wvt = al("wvt", [P, KT, DM])
            rt = al("rt", [P, KT, NL])
            wor = al("wor", [P, KT, DM])
            WO_hi, WO_lo = (al(n, [P, KT, DM], F32R) for n in ("WO_hi", "WO_lo"))
            cw = al("cw", [P, KT, 2])
            rot = al("rot", [P, 2, ROT_COLS])
            tri_sb = al("tri", [P, BATCH, BATCH, MIX_H])
            xt = al("xt", [P, KT, SEQ])
            conv = al("conv", [P, KT, SEQ])
            sil = al("sil", [P, KT, SEQ])
            C_hi, C_lo = (al(n, [P, 2, KT, SEQ], F32R) for n in ("C_hi", "C_lo"))
            qk = al("qk", [P, 2, BATCH, 2 * MIX_DK])
            vv = al("vv", [P, 2, BATCH, MIX_DV])
            sg = al("sg", [P, 2, BATCH, MIX_DV])
            lg = al("lg", [P, 2, BATCH, NL])
            t1 = al("t1", [P, BATCH, 2 * MIX_DK])
            t2 = al("t2", [P, BATCH, 2 * MIX_DK])
            small = [al(f"sm{i}", [P, BATCH, MIX_H]) for i in range(8)]
            same = al("same", [P, BATCH, BATCH, MIX_H])
            prod = al("prod", [P, 10, MIX_DK])
            dots = al("dots", [P, 10, MIX_H])
            coef = al("coef", [P, 10, MIX_H])
            ov = al("ov", [P, 4, MIX_DV])
            oo = al("oo", [P, BATCH, MIX_DV])
            sq = al("sq", [P, BATCH, MIX_DV])
            yy = al("yy", [P, BATCH, MIX_DV])
            Y_hi, Y_lo = (al(n, [P, KT, SEQ], F32R) for n in ("Y_hi", "Y_lo"))
            dma_w = sem(f"dma_{tag}")

            loads = [(raw[:, :, 0:NW], wmix), (wvt[:, :, :], wv_t), (rt[:, :, :], router),
                     (wor[:, :, :], wmix_out), (cw[:, :, :], conv_w), (rot[:, :, :], rot_tab),
                     (tri_sb[:, :, :, :], tri)]
            for dst, src in loads:
                sp.dma(dst, src, dma_w)
            loaded = (dma_w, 16 * len(loads))

            m_stats = norm_stats(tile_marks)
            dve.wait(m_stats)

            pe.wait(loaded)
            for f in range(KT):
                for kt in range(KT):
                    step = (lambda e, f=f, kt=kt: e.matmul(bank[7][:, f * NL:(f + 1) * NL],
                                                           wvt[:, kt, f * P:(f + 1) * P], rt[:, kt, :],
                                                           start=(kt == 0), stop=(kt == KT - 1)))
                    if f < KT - 1 or kt < KT - 1:
                        pe.do(step)
            m = pe.counted(step)
            act.wait(m, loaded)
            m = act.counted(lambda e: e.activation(
                raw[:, :, NW:NW + NL], bank[7][:, 0:KT * NL].rearrange("p (f n) -> p f n", f=KT), ACT.Copy))
            wr_free = m
            pool.wait(m, loaded)
            pool.do(lambda e: e.tensor_scalar(W_hi[:, :, :], raw[:, :, :], 1.0, None, ALU.mult))
            m = pool.counted(lambda e: e.tensor_scalar(WO_hi[:, :, :], wor[:, :, :], 1.0, None, ALU.mult))
            pool.wait(m)
            pool.do(lambda e: e.tensor_tensor(W_lo[:, :, :], raw[:, :, :], W_hi[:, :, :].bitcast(F32),
                                              ALU.subtract))
            w_ready = pool.counted(lambda e: e.tensor_tensor(WO_lo[:, :, :], wor[:, :, :],
                                                            WO_hi[:, :, :].bitcast(F32), ALU.subtract))

            free = {k: () for k in range(8)}
            free[7] = (wr_free,)
            marks = {}

            def earlier(kind, c):
                return marks[kind, c] if c >= 0 else ()

            def front(c):
                ms = []
                for l in range(BATCH):
                    ms.append(norm_tile(4 * l + c, l, earlier("t", c - 1)))
                mt = transpose_four([4 * l + c for l in range(BATCH)], ms, (0, 1), [free[0], free[1]])
                marks["t", c] = (mt[-1],)
                for f in range(KT):
                    act.wait(mt[f], loaded, *earlier("conv", c - 1))
                    act.do(lambda e, f=f: e.activation(xt[:, f, :], bank[f][:, :], ACT.Copy))
                    m = act.counted(lambda e, f=f: e.activation(conv[:, f, :], bank[f][:, :], ACT.Copy,
                                                               scale=cw[:, f, 1:2]))
                    free[f] = (m,)
                    dve.wait(m)
                    m = dve.counted(lambda e, f=f: e.scalar_tensor_tensor(
                        out=conv[:, f, P:SEQ], in0=xt[:, f, 0:SEQ - P], scalar=cw[:, f, 0:1],
                        in1=conv[:, f, P:SEQ], op0=ALU.mult, op1=ALU.add))
                act.wait(m, *earlier("proj", c - 2), *earlier("lo", c - 1))
                act.do(lambda e: e.activation(sil[:, :, :], conv[:, :, :], ACT.Silu))
                m = act.counted(lambda e: e.activation(C_hi[:, c % 2, :, :], conv[:, :, :], ACT.Silu))
                marks["conv", c] = (m,)
                dve.wait(m)
                m = dve.counted(lambda e: e.tensor_tensor(C_lo[:, c % 2, :, :], sil[:, :, :],
                                                         C_hi[:, c % 2, :, :].bitcast(F32), ALU.subtract))
                marks["lo", c] = (m,)

            def project(c):
                q = c % 2
                for l in range(BATCH):
                    cols = slice(l * P, (l + 1) * P)
                    for part, (a, z) in enumerate(((0, 512), (512, NW + NL))):
                        k = 4 + (2 * l + part) % 4
                        pe.wait(*marks["lo", c], w_ready, *free[k])
                        for kt in range(KT):
                            step = three_pass(pe, bank[k][:, 0:z - a], C_hi[:, q, kt, cols],
                                              C_lo[:, q, kt, cols], W_hi[:, kt, a:z], W_lo[:, kt, a:z],
                                              kt == 0, kt == KT - 1)
                            if kt < KT - 1:
                                pe.do(step)
                        m = pe.counted(step)
                        act.wait(m, *earlier("mix", c - 2))
                        if part == 0:
                            act.do(lambda e, l=l, k=k: e.activation(qk[:, q, l, 0:MIX_DK],
                                                                    bank[k][:, 0:MIX_DK], ACT.Silu))
                            act.do(lambda e, l=l, k=k: e.activation(qk[:, q, l, MIX_DK:2 * MIX_DK],
                                                                    bank[k][:, MIX_DK:2 * MIX_DK], ACT.Copy))
                            m = act.counted(lambda e, l=l, k=k: e.activation(
                                vv[:, q, l, :], bank[k][:, 2 * MIX_DK:512], ACT.Copy))
                        else:
                            act.do(lambda e, l=l, k=k: e.activation(sg[:, q, l, :], bank[k][:, 0:MIX_DV],
                                                                    ACT.Silu))
                            m = act.counted(lambda e, l=l, k=k: e.activation(
                                lg[:, q, l, :], bank[k][:, MIX_DV:MIX_DV + NL], ACT.Copy))
                        free[k] = (m,)
                marks["proj", c] = (pe.last(),)
                marks["evac", c] = (m,)

            def chain(step):
                m = dve.counted(step)
                dve.wait(m)
                return m

            def mix(c):
                q = c % 2
                QK, V, SG, LG = qk[:, q, :, :], vv[:, q, :, :], sg[:, q, :, :], lg[:, q, :, :]
                halves = lambda ap: ap.rearrange("p l (n a f) -> p (l n) a f", a=2, f=MIX_HDK // 2)
                sin_t = rot[:, 1, :].rearrange("p (n a f) -> p n a f", a=2, f=MIX_HDK // 2)
                diff, first, mag, prob, cnt, rcnt, tmp, pw = (s[:, :, :] for s in small)
                pool.wait(*marks["evac", c], loaded, *earlier("rot", c - 1))
                pool.do(lambda e: e.tensor_tensor(halves(t2[:, :, :])[:, :, 0, :], halves(QK)[:, :, 1, :],
                                                  sin_t[:, :, 0, :], ALU.mult))
                m2 = pool.counted(lambda e: e.tensor_tensor(
                    halves(t2[:, :, :])[:, :, 1, :], halves(QK)[:, :, 0, :], sin_t[:, :, 1, :], ALU.mult))
                dve.wait(*marks["evac", c], loaded)
                chain(lambda e: e.tensor_tensor(diff, LG[:, :, 0:MIX_H], LG[:, :, MIX_H:2 * MIX_H],
                                                ALU.subtract))
                dve.do(lambda e: e.tensor_scalar(first, diff, 0.0, None, ALU.is_ge))
                chain(lambda e: e.tensor_scalar(tmp, diff, -1.0, None, ALU.mult))
                m = chain(lambda e: e.tensor_tensor(mag, diff, tmp, ALU.max))
                act.wait(m)
                mp = act.counted(lambda e: e.activation(prob, mag, ACT.Tanh, scale=0.5))
                chain(lambda e: e.tensor_tensor(same[:, :, :, :],
                                                first.unsqueeze(2).to_broadcast([P, BATCH, BATCH, MIX_H]),
                                                first.unsqueeze(1).to_broadcast([P, BATCH, BATCH, MIX_H]),
                                                ALU.is_equal))
                chain(lambda e: e.tensor_tensor(same[:, :, :, :], same[:, :, :, :], tri_sb[:, :, :, :],
                                                ALU.mult))
                chain(lambda e: e.tensor_reduce(cnt, same[:, :, :, :].rearrange("p l m h -> p l h m"),
                                                AX.X, ALU.add))
                dve.do(lambda e: e.reciprocal(rcnt, cnt))
                dve.wait(mp)
                chain(lambda e: e.tensor_scalar(tmp, prob, 0.5 * MIX_HDK ** -0.5, 0.5 * MIX_HDK ** -0.5,
                                                ALU.mult, ALU.add))
                chain(lambda e: e.tensor_tensor(pw, tmp, rcnt, ALU.mult))
                chain(lambda e: e.tensor_tensor(
                    t1[:, :, :].rearrange("p l n -> p (l n)"), QK.rearrange("p l n -> p (l n)"),
                    rot[:, 0, :], ALU.mult))
                dve.wait(m2)
                m = chain(lambda e: e.tensor_tensor(t1[:, :, :], t1[:, :, :], t2[:, :, :], ALU.add))
                marks["rot", c] = (m,)
                at = 0
                for l in range(BATCH):
                    n = l + 1
                    dve.do(lambda e, l=l, n=n, at=at: e.tensor_tensor(
                        prod[:, at:at + n, :],
                        t1[:, l, 0:MIX_DK].unsqueeze(1).to_broadcast([P, n, MIX_DK]),
                        t1[:, 0:n, MIX_DK:2 * MIX_DK], ALU.mult))
                    m = dve.counted(lambda e, l=l, n=n, at=at: e.tensor_tensor(
                        coef[:, at:at + n, :], same[:, l, 0:n, :],
                        pw[:, l, :].unsqueeze(1).to_broadcast([P, n, MIX_H]), ALU.mult))
                    at += n
                dve.wait(m)
                chain(lambda e: e.tensor_reduce(
                    dots[:, :, :].rearrange("p n h -> p (n h)"),
                    prod[:, :, :].rearrange("p n (h f) -> p (n h) f", f=MIX_HDK), AX.X, ALU.add))
                chain(lambda e: e.tensor_tensor(coef[:, :, :], coef[:, :, :], dots[:, :, :], ALU.mult))
                at = 0
                for l in range(BATCH):
                    n = l + 1
                    dst = oo[:, 0:1, :] if l == 0 else ov[:, 0:n, :]
                    heads = lambda ap: ap.rearrange("p m (h d) -> p (m h) d", d=MIX_HDV)
                    chain(lambda e, n=n, at=at, dst=dst: e.tensor_tensor(
                        heads(dst), heads(V[:, 0:n, :]),
                        coef[:, at:at + n, :].rearrange("p m h -> p (m h)").unsqueeze(2)
                        .to_broadcast([P, n * MIX_H, MIX_HDV]), ALU.mult))
                    if l:
                        chain(lambda e, l=l, n=n: e.tensor_reduce(
                            oo[:, l, :], ov[:, 0:n, :].rearrange("p m x -> p x m"), AX.X, ALU.add))
                    at += n
                groups = oo[:, :, :].rearrange("p l (h d) -> p (l h) d", d=MIX_HDV)
                flat = lambda ap: ap.rearrange("p l h -> p (l h)")
                wide = lambda ap: flat(ap).unsqueeze(2).to_broadcast([P, BATCH * MIX_H, MIX_HDV])
                chain(lambda e: e.tensor_reduce(flat(tmp), groups, AX.X, ALU.add))
                chain(lambda e: e.tensor_scalar(tmp, tmp, 1.0 / MIX_HDV, None, ALU.mult))
                m = chain(lambda e: e.tensor_tensor(groups, groups, wide(tmp), ALU.subtract))
                act.wait(m)
                m_sq = act.counted(lambda e: e.activation(sq[:, :, :], oo[:, :, :], ACT.Square))
                pool.wait(m, *earlier("yt", c - 1))
                m_y = pool.counted(lambda e: e.tensor_tensor(yy[:, :, :], oo[:, :, :], SG, ALU.mult))
                dve.wait(m_sq)
                chain(lambda e: e.tensor_reduce(
                    flat(cnt), sq[:, :, :].rearrange("p l (h d) -> p (l h) d", d=MIX_HDV), AX.X, ALU.add))
                m = chain(lambda e: e.tensor_scalar(cnt, cnt, 1.0 / MIX_HDV, EPS, ALU.mult, ALU.add))
                act.wait(m)
                m = act.counted(lambda e: e.activation(mag, cnt, ACT.Sqrt))
                dve.wait(m)
                chain(lambda e: e.reciprocal(rcnt, mag))
                dve.wait(m_y)
                ygroups = yy[:, :, :].rearrange("p l (h d) -> p (l h) d", d=MIX_HDV)
                m = chain(lambda e: e.tensor_tensor(ygroups, ygroups, wide(rcnt), ALU.mult))
                marks["mix", c] = (m,)

            def finish(c):
                pe.wait(*marks["mix", c])
                for f in range(KT):
                    k = 2 + f
                    pe.wait(*free[k])
                    for l in range(BATCH):
                        step = (lambda e, l=l, f=f, k=k: e.transpose(
                            bank[k][:, l * P:(l + 1) * P], yy[:, l, f * P:(f + 1) * P], ident_f[:, :]))
                        if l < BATCH - 1:
                            pe.do(step)
                    m = pe.counted(step)
                    _, lo = split_from(bank[k][:, :], Y_hi[:, f, :], Y_lo[:, f, :], m,
                                       earlier("out", c - 1))
                    free[k] = (lo,)
                marks["yt", c] = (pe.last(),)
                for half in range(2):
                    k = 2 + half
                    pe.wait(lo, *free[k])
                    for a in range(2):
                        l = 2 * half + a
                        cols = slice(l * P, (l + 1) * P)
                        for kt in range(KT):
                            step = three_pass(pe, bank[k][:, a * DM:(a + 1) * DM], Y_hi[:, kt, cols],
                                              Y_lo[:, kt, cols], WO_hi[:, kt, :], WO_lo[:, kt, :],
                                              kt == 0, kt == KT - 1)
                            if a == 0 or kt < KT - 1:
                                pe.do(step)
                    m = pe.counted(step)
                    tiles = X[:, 8 * half:8 * half + 8, :].rearrange("p (a r) d -> p a r d", r=4)[:, :, c, :]
                    dve.wait(m)
                    m = dve.counted(lambda e, tiles=tiles, k=k: e.tensor_tensor(
                        tiles, tiles, bank[k][:, :].rearrange("p (a d) -> p a d", a=2), ALU.add))
                    free[k] = (m,)
                    for a in range(2):
                        done[4 * (2 * half + a) + c] = m
                marks["out", c] = (pe.last(),)
                if last:
                    sp.wait(m)
                    for l in range(BATCH):
                        sp.dma(out_tiles[:, 4 * l + c, :], X[:, 4 * l + c, :], dma_out)

            done = {}
            front(0)
            project(0)
            for c in range(4):
                if c + 1 < 4:
                    front(c + 1)
                    project(c + 1)
                mix(c)
                finish(c)
            if not last:
                barrier()
            ctx.close()
            return [done[t] for t in range(NT)]

        def attention_b(tile_marks):
            ctx = ExitStack()
            al = allocator(ctx)
            Wq = al("b_Wq", [P, HEADS, P], F32R)
            Wsw = al("b_Wsw", [P, HEADS // 2, P], F32R)
            Nw_hi, Nw_lo = (al(f"b_{n}", [P, HEADS // 2, DM], F32R) for n in ("Nh", "Nl"))
            QA_hi, QA_lo = (al(f"b_{n}", [P, TOK], F32R) for n in ("QAh", "QAl"))
            KC_hi, KC_lo = (al(f"b_{n}", [P, 2, TOK], F32R) for n in ("KCh", "KCl"))
            CT = al("b_CT", [P, NT, RANK])
            tabs = al("b_tabs", [P, 3, SEQ])
            dma_w1, dma_w2 = sem("dma_b1"), sem("dma_b2")
            pro = ExitStack()
            ap_ = allocator(pro)
            wsrc = ap_("b_wsrc", [P, KT, 5, P])
            Wc_hi, Wc_lo = (ap_(f"b_{n}", [P, KT, 4, P], F32R) for n in ("Wch", "Wcl"))
            qbt = ap_("b_qbt", [P, 4, 2, RANK])
            kbt = ap_("b_kbt", [P, 4, RANK])
            vbt = ap_("b_vbt", [P, 4, RANK])
            wo = ap_("b_wo", [P, 4, DM])
            wq_raw = ap_("b_wqraw", [P, 4, P])
            wsw_raw = ap_("b_wswraw", [P, HEADS // 2, P])
            kk = ap_("b_kk", [P, 2, SEQ])
            kt_ = ap_("b_kt", [P, SEQ])

            for j, dst in enumerate((0, 1, 2, 3)):
                sp.dma(wsrc[:, :, dst, :], wqa[:, :, :] if j == 0 else wkva[:, :, (j - 1) * P:j * P], dma_w1)
            sp.dma(tabs[:, :, :], rope_tab, dma_w1)
            for half in range(2):
                rows = slice(64 * half, 64 * half + 64)
                sp.dma(wsw_raw[rows, :, :], wqb_sw, dma_w1)
            w1 = (dma_w1, 16 * 7)

            xt_ready = norm_transposed(tile_marks)

            pool.wait(w1)
            m = pool.counted(lambda e: e.tensor_scalar(Wc_hi[:, :, :, :], wsrc[:, :, 0:4, :], 1.0, None,
                                                      ALU.mult))
            pool.wait(m)
            wc_ready = pool.counted(lambda e: e.tensor_tensor(
                Wc_lo[:, :, :, :], wsrc[:, :, 0:4, :], Wc_hi[:, :, :, :].bitcast(F32), ALU.subtract))

            free = {k: () for k in range(8)}
            for k in range(4):
                free[k] = (dve.last(),)

            sent, read = 0, None
            for r in range(4):
                if read:
                    sp.wait(*read)
                hs = slice(4 * r, 4 * r + 4)
                for rep in range(2):
                    sp.dma(qbt[:, :, rep, :], wqb_t[:, hs, :], dma_w2)
                sp.dma(kbt[:, :, :], wkvbk_t[:, hs, :], dma_w2)
                sp.dma(vbt[:, :, :], wkvbv_t[:, hs, :], dma_w2)
                sp.dma(wo[:, :, :], wout_b[:, hs, :], dma_w2)
                for half in range(2):
                    rows = slice(64 * half, 64 * half + 64)
                    for par in range(2):
                        c0 = 64 if par == 0 else 0
                        sp.dma(wq_raw[rows, par:4:2, c0:c0 + 64], wqb_pe[:, 4 * r + par:4 * r + 4:2, :],
                               dma_w2)
                sent += 9
                w2 = (dma_w2, 16 * sent)
                pe.wait(w2, *free[4])
                for j in range(4):
                    step = (lambda e, j=j: e.matmul(bank[4][:, j * 64:(j + 1) * 64],
                                                    qbt[:, j, :, :].rearrange("p a r -> p (a r)"),
                                                    kbt[:, j, :], start=True, stop=True))
                    if j < 3:
                        pe.do(step)
                m_abs = pe.counted(step)
                dve.wait(m_abs, w2)
                absv = bank[4][:, 0:256].rearrange("p (j c) -> p j c", c=64)
                for par in range(2):
                    c0 = 0 if par == 0 else 64
                    m = dve.counted(lambda e, par=par, c0=c0: e.tensor_copy(
                        wq_raw[:, par:4:2, c0:c0 + 64], absv[:, par:4:2, :]))
                free[4] = (m,)
                dve.wait(m)
                m = dve.counted(lambda e: e.tensor_scalar(wq_raw[:, :, :], wq_raw[:, :, :], SCALE_B, None,
                                                         ALU.mult))
                dve.wait(m)
                m = dve.counted(lambda e, hs=hs: e.tensor_copy(Wq[:, hs, :], wq_raw[:, :, :]))
                dve.wait(m)
                wq_done = dve.counted(lambda e, hs=hs: e.tensor_tensor(
                    Wq[64:128, hs, :], wq_raw[64:128, :, :], Wq[64:128, hs, :].bitcast(F32), ALU.subtract))
                for pr in range(2):
                    k = 5 + pr
                    pe.wait(*free[k])
                    for par in range(2):
                        j = 2 * pr + par
                        step = (lambda e, j=j, par=par, k=k: e.matmul(
                            bank[k][64 * par:64 * par + 64, 0:DM], vbt[:, j, :], wo[:, j, :],
                            start=True, stop=True))
                        if par == 0:
                            pe.do(step)
                    m = pe.counted(step)
                    _, lo = split_from(bank[k][:, 0:DM], Nw_hi[:, 2 * r + pr, :], Nw_lo[:, 2 * r + pr, :], m)
                    free[k] = (lo,)
                read = (pe.last(), wq_done)
            dve.wait(w1)
            m = dve.counted(lambda e: e.tensor_scalar(wsw_raw[:, :, :], wsw_raw[:, :, :], SCALE_B, None,
                                                     ALU.mult))
            dve.wait(m)
            m = dve.counted(lambda e: e.tensor_copy(Wsw[:, :, :], wsw_raw[:, :, :]))
            dve.wait(m)
            w_ready = dve.counted(lambda e: e.tensor_tensor(
                Wsw[64:128, :, :], wsw_raw[64:128, :, :], Wsw[64:128, :, :].bitcast(F32), ALU.subtract))

            kc_ready = {}
            kk_read = ()
            for b in range(BATCH):
                cols = slice(b * SEQ, (b + 1) * SEQ)
                res = []
                for j in range(4):
                    pe.wait(wc_ready, xt_ready[b], *free[j])
                    for kt in range(KT):
                        step = three_pass(pe, bank[j][:, :], Wc_hi[:, kt, j, :], Wc_lo[:, kt, j, :],
                                          XT_hi[:, kt, cols], XT_lo[:, kt, cols], kt == 0, kt == KT - 1)
                        if kt < KT - 1:
                            pe.do(step)
                    res.append(pe.counted(step))
                _, lo = split_from(bank[0][:, :], QA_hi[:, cols], QA_lo[:, cols], res[0])
                free[0] = (lo,)
                dve.wait(res[3], w1)
                m = dve.counted(lambda e: e.tensor_tensor(kt_[:, :], bank[3][:, :], tabs[:, 2, :], ALU.mult))
                free[3] = (m,)
                dve.wait(m)
                for v in range(2):
                    dve.wait(res[1 + v], *kk_read)
                    m = dve.counted(lambda e, v=v: e.tensor_tensor(kk[:, v, :], bank[1 + v][:, :],
                                                                  tabs[:, v, :], ALU.mult))
                    free[1 + v] = (m,)
                    dve.wait(m)
                    rows = slice(64, 128) if v == 0 else slice(0, 64)
                    m = dve.counted(lambda e, v=v, rows=rows: e.tensor_tensor(
                        kk[rows, v, :], kk[rows, v, :], kt_[rows, :], ALU.add))
                    dve.wait(m)
                    m = dve.counted(lambda e, v=v, cols=cols: e.tensor_copy(KC_hi[:, v, cols], kk[:, v, :]))
                    dve.wait(m)
                    m = dve.counted(lambda e, v=v, cols=cols: e.tensor_tensor(
                        KC_lo[:, v, cols], kk[:, v, :], KC_hi[:, v, cols].bitcast(F32), ALU.subtract))
                kc_ready[b] = m
                pe.wait(m, *free[7])
                for t in range(TPB):
                    step = (lambda e, t=t: e.transpose(bank[7][:, t * RANK:(t + 1) * RANK],
                                                       kk[0:64, 0, t * P:(t + 1) * P], ident_f[0:64, 0:64]))
                    if t < TPB - 1:
                        pe.do(step)
                m = pe.counted(step)
                kk_read = (m,)
                act.wait(m)
                ct_ready = act.counted(lambda e, b=b: e.activation(
                    CT[:, 4 * b:4 * b + 4, :], bank[7][:, 0:TPB * RANK].rearrange("p (t c) -> p t c", c=RANK),
                    ACT.Copy))
                free[7] = (ct_ready,)
            barrier()
            pro.close()

            qt = al("b_qt", [P, 2, SEQ])
            qr = al("b_qr", [P, 2, SEQ])
            Q_hi, Q_lo = (al(f"b_{n}", [P, 2, SEQ], F32R) for n in ("Qh", "Ql"))
            PT = al("b_PT", [P, 4, TPB, SEQ])
            U_hi, U_lo = (al(f"b_{n}", [P, 2, SEQ], F32R) for n in ("Uh", "Ul"))
            core = Core(al, "b", split=False)
            pairs = BATCH * HEADS // 2
            units = 2 * pairs
            q_ready, s_done, av_done, u_ready, o_done, sw_ready, sw_read = {}, {}, {}, {}, {}, {}, {}
            x_added = {}

            def two_pass(out, w, b):
                cols = slice(b * SEQ, (b + 1) * SEQ)
                pe.do(lambda e: e.matmul(out, w, QA_hi[:, cols], start=True, stop=False))
                return pe.counted(lambda e: e.matmul(out, w, QA_lo[:, cols], start=False, stop=True))

            def swapped(p):
                b, hp = p // 8, p % 8
                k = core.next_acc()
                m = two_pass(bank[k][:, :], Wsw[:, hp, :], b)
                dve.wait(m, *before(sw_read, p - 2))
                m = dve.counted(lambda e: e.tensor_tensor(qt[:, p % 2, :], bank[k][:, :], tabs[:, 2, :],
                                                         ALU.mult))
                core.acc_free[k] = (m,)
                sw_ready[p] = m

            def query(n):
                p, par = n // 2, n % 2
                b, h = p // 8, 2 * (p % 8) + par
                q = n % 2
                k = core.next_acc()
                m = two_pass(bank[k][:, :], Wq[:, h, :], b)
                dve.wait(m, *before(q_ready, n - 2))
                m = dve.counted(lambda e: e.tensor_tensor(qr[:, q, :], bank[k][:, :], tabs[:, par, :],
                                                         ALU.mult))
                core.acc_free[k] = (m,)
                rows = slice(64, 128) if par == 0 else slice(0, 64)
                pool.wait(m, sw_ready[p], pool.last())
                m = pool.counted(lambda e: e.tensor_tensor(qr[rows, q, :], qr[rows, q, :],
                                                          qt[rows, p % 2, :], ALU.add))
                sw_read[p] = (m,)
                act.wait(m, *before(s_done, n - 2))
                m = act.counted(lambda e: e.activation(Q_hi[:, q, :], qr[:, q, :], ACT.Copy))
                dve.wait(m)
                m = dve.counted(lambda e: e.tensor_tensor(Q_lo[:, q, :], qr[:, q, :],
                                                         Q_hi[:, q, :].bitcast(F32), ALU.subtract))
                q_ready[n] = (m,)

            def scores(n, i):
                p, par = n // 2, n % 2
                b, q = p // 8, n % 2
                cols = slice(b * SEQ, (b + 1) * SEQ)
                m = core.scores(n, i, Q_hi[:, q, :], Q_lo[:, q, :], KC_hi[:, par, cols], KC_lo[:, par, cols],
                                q_ready[n])
                s_done[n] = (m,)
                return core.pending

            def values(p):
                b = p // 8
                k = core.next_acc()
                for n in (2 * p, 2 * p + 1):
                    for i in range(TPB):
                        pe.wait(core.pt[n, i])
                for j in range(TPB):
                    for par in range(2):
                        qs = slice(P * j, SEQ)
                        step = (lambda e, j=j, par=par, qs=qs: e.matmul(
                            bank[k][64 * par:64 * par + 64, qs], CT[:, 4 * b + j, :],
                            PT[:, (2 * p + par) % 4, j, qs], start=(j == 0), stop=(j == TPB - 1)))
                        if j < TPB - 1 or par == 0:
                            pe.do(step)
                m = pe.counted(step)
                av_done[2 * p] = av_done[2 * p + 1] = (m,)
                _, m = split_from(bank[k][:, :], U_hi[:, p % 2, :], U_lo[:, p % 2, :], m,
                                  before(o_done, p - 2))
                core.acc_free[k] = (m,)
                u_ready[p] = m

            def output(p, half):
                b, hp = p // 8, p % 8
                k = core.next_acc()
                pe.wait(u_ready[p])
                for tt in range(2):
                    cols = slice((2 * half + tt) * P, (2 * half + tt + 1) * P)
                    step = three_pass(pe, bank[k][:, tt * DM:(tt + 1) * DM], U_hi[:, p % 2, cols],
                                      U_lo[:, p % 2, cols], Nw_hi[:, hp, :], Nw_lo[:, hp, :], True, True)
                    if tt == 0:
                        pe.do(step)
                m = pe.counted(step)
                if half == 1:
                    o_done[p] = (m,)
                t0 = 4 * b + 2 * half
                dve.wait(m, *x_added.get(t0, ()))
                m = dve.counted(lambda e: e.tensor_tensor(
                    X[:, t0:t0 + 2, :], X[:, t0:t0 + 2, :],
                    bank[k][:, :].rearrange("p (t d) -> p t d", t=2), ALU.add))
                x_added[t0] = x_added[t0 + 1] = (m,)
                core.acc_free[k] = (m,)

            pool_todo = []
            swapped(0)
            query(0)
            for n in range(units + 5):
                for i in range(TPB):
                    if 1 <= n <= units:
                        core.transposes(n - 1, i, PT[:, (n - 1) % 4, :, :], before(av_done, n - 5))
                    pend = scores(n, i) if n < units else None
                    if pool_todo:
                        core.normalise(pool_todo.pop())
                    if pend:
                        pool_todo.append(pend)
                    if i == 0 and n + 1 < units:
                        if (n + 1) % 2 == 0:
                            swapped((n + 1) // 2)
                        query(n + 1)
                    if i == 2 and n % 2 == 1 and 3 <= n and (n - 3) // 2 < pairs:
                        values((n - 3) // 2)
                    if i == 3 and n >= 4 and (n - 4) // 2 < pairs:
                        output((n - 4) // 2, n % 2)
            barrier()
            ctx.close()
            return [x_added[t][0] for t in range(NT)]

        ready = attention_a()
        ready = mixture("m1", ready, last=False)
        ready = attention_b(ready)
        ready = mixture("m2", ready, last=True)
        sp.wait((dma_out, 16 * NT))

        block = top.enter_context(nc.Block())

        @block.sync
        def _(e):
            sp.play(e)

        @block.tensor
        def _(e):
            pe.play(e)

        @block.scalar
        def _(e):
            act.play(e)

        @block.vector
        def _(e):
            dve.play(e)

        @block.gpsimd
        def _(e):
            pool.play(e)


def kernel(**inputs):
    from concourse import bacc
    from concourse.bass_utils import run_bass_kernel_spmd

    f = {n.removeprefix("L0_"): np.asarray(a) for n, a in inputs.items()}

    def rows(a):
        return a.reshape(-1, P, a.shape[-1]).transpose(1, 0, 2)

    def group(w):
        return w.reshape(NG, GH, KT, P, DH).transpose(0, 3, 2, 1, 4).reshape(NG, P, KT * GH * DH)

    wo = f["attn_a_W_O"].reshape(NG, GH, DH, DM).transpose(0, 2, 1, 3).reshape(NG, P, GH * DM)
    swap = np.arange(ROPE) ^ 1
    wqb = f["attn_b_Wqb"].reshape(RANK, HEADS, NOPE + ROPE)
    wkvb = f["attn_b_Wkvb"].reshape(RANK, HEADS, 2 * NOPE)
    pe_sw = wqb[:, :, NOPE:][:, :, swap].reshape(RANK, HEADS // 2, 2, ROPE)
    wkva = rows(f["attn_b_Wkva"])
    c_, pe_ = wkva[:, :, :RANK], wkva[:, :, RANK:]
    wqa = rows(f["attn_b_Wqa"])
    router = np.zeros((MIX_DV, 2, MIX_H), f["ffn_router_w"].dtype)
    for h in range(MIX_H):
        router[h * MIX_HDV:(h + 1) * MIX_HDV, :, h] = f["ffn_router_w"][h]

    theta = (np.float32(10000.0) ** (-2.0 * np.arange(ROPE // 2, dtype=np.float32) / ROPE)).astype(np.float32)
    angle = np.repeat(theta, 2)[:, None] * np.arange(SEQ, dtype=np.float32)[None, :]
    cos, sin = np.cos(angle), np.sin(angle)
    sin[0::2] *= -1
    one = np.ones_like(cos)
    rope_tab = np.stack([np.concatenate([one, cos]), np.concatenate([cos, one]),
                         np.concatenate([sin, sin])], axis=1).astype(np.float32)
    inv = (1.0 / np.float32(10000.0) ** (np.arange(0, MIX_HDK, 2, dtype=np.float32) / MIX_HDK)).astype(np.float32)
    fr = np.arange(BATCH, dtype=np.float32)[:, None] * inv[None, :]
    mc = np.tile(np.concatenate([np.cos(fr), np.cos(fr)], 1), (1, 2 * MIX_H))
    ms = np.tile(np.concatenate([-np.sin(fr), np.sin(fr)], 1), (1, 2 * MIX_H))
    rot_tab = np.broadcast_to(np.stack([mc, ms]).reshape(1, 2, ROT_COLS), (P, 2, ROT_COLS)).astype(np.float32)
    tri = np.broadcast_to(np.tril(np.ones((BATCH, BATCH), np.float32))[None, :, :, None],
                          (P, BATCH, BATCH, MIX_H))
    arrays = {
        "x": f["attn_a_x"].reshape(TOK, DM),
        "wa": np.concatenate([group(f["attn_a_W_Q"]), group(f["attn_a_W_K"]), group(f["attn_a_W_V"]), wo], 2),
        "ba": np.stack([f["attn_a_b_Q"].T, f["attn_a_b_K"].T, f["attn_a_b_V"].T], axis=1),
        "bo": f["attn_a_b_O"].reshape(1, DM),
        "ident": np.eye(P, dtype=np.float32),
        "mask": np.triu(np.full((P, P), MASKED, np.float32), 1),
        "wqa": np.concatenate([wqa, wqa], 2),
        "wqb_t": wqb[:, :, :NOPE].transpose(2, 1, 0),
        "wqb_pe": wqb[:, :, NOPE:],
        "wqb_sw": pe_sw[:, :, ::-1, :].reshape(RANK, HEADS // 2, P),
        "wkva": np.concatenate([c_, pe_, pe_, c_, pe_[:, :, swap], pe_[:, :, swap]], 2),
        "wkvbk_t": wkvb[:, :, :NOPE].transpose(2, 1, 0),
        "wkvbv_t": wkvb[:, :, NOPE:].transpose(2, 1, 0),
        "wout_b": f["attn_b_Wout"].reshape(HEADS, NOPE, DM).transpose(1, 0, 2),
        "rope_tab": rope_tab,
        "conv_w": rows(f["ffn_conv_w"]),
        "wmix": np.concatenate([rows(f[f"ffn_{n}"]) for n in ("Wq", "Wk", "Wv", "Wg")], 2),
        "wv_t": rows(f["ffn_Wv"].T),
        "router": rows(router.reshape(MIX_DV, 2 * MIX_H)),
        "wmix_out": rows(f["ffn_Wout"]),
        "rot_tab": rot_tab,
        "tri": tri,
    }
    arrays = {n: np.ascontiguousarray(a) for n, a in arrays.items()}
    nc = bacc.Bacc("TRN2", target_bir_lowering=False, num_devices=1)
    args = [nc.dram_tensor(n, a.shape, mybir.dt.from_np(a.dtype), kind="ExternalInput").ap()
            for n, a in arrays.items()]
    out = nc.dram_tensor("out", [TOK, DM], F32, kind="ExternalOutput").ap()
    hybrid_program(nc, *args, out)
    result = run_bass_kernel_spmd(nc, [arrays], core_ids=[0])
    return result.results[0]["out"].reshape(BATCH, SEQ, DM)
```

```python
from contextlib import ExitStack

import numpy as np
import concourse.bass as bass
from concourse import mybir

F32 = mybir.dt.float32
F32R = mybir.dt.float32r
BF16 = mybir.dt.bfloat16
ALU = mybir.AluOpType
ACT = mybir.ActivationFunctionType
AX = mybir.AxisListType

P = 128
BATCH, SEQ, DM = 4, 512, 256
TOK = BATCH * SEQ
NT = TOK // P
TPB = SEQ // P
KT = DM // P
HEADS = 16
DH = 128
GH = 2
NG = HEADS // GH
GW = GH * DH
ROPE = 64
RANK = 64
NOPE = 128
MIX_DK, MIX_DV, MIX_H = 128, 256, 16
MIX_HDK, MIX_HDV = MIX_DK // MIX_H, MIX_DV // MIX_H
EPS = 1e-5
MASKED = -1.0e30
SCALE_A = float(DH) ** -0.5
SCALE_B = float(NOPE + ROPE) ** -0.5
MIX_LOGIT = MIX_DK + MIX_DV
MIX_K = MIX_LOGIT + 2 * MIX_H
MIX_V = MIX_K + BATCH * MIX_DK
MIX_COLS = MIX_V + MIX_DV
MIX_WORDS = KT * MIX_COLS + KT * DM
SKEW = 2
PAIRS = BATCH * (BATCH + 1) // 2


class Stream:

    def __init__(self, sem):
        self.sem, self.count, self.steps, self.passed = sem, 0, [], {}

    def wait(self, *marks):
        for sem, value in marks:
            if self.passed.get(id(sem), 0) < value:
                self.passed[id(sem)] = value
                self.steps.append(lambda e, s=sem, v=value: e.wait_ge(s, v))

    def do(self, step):
        self.steps.append(step)

    def counted(self, step):
        self.steps.append(lambda e: step(e).then_inc(self.sem, 1))
        self.count += 1
        return (self.sem, self.count)

    def last(self):
        return (self.sem, self.count)

    def dma(self, out, in_, sem):
        self.steps.append(lambda e: e.dma_start(out, in_).then_inc(sem, 16))

    def play(self, engine):
        for step in self.steps:
            step(engine)


def before(marks, n, *rest):
    return marks[(n, *rest) if rest else n] if n >= 0 else ()


def three_pass(pe, out, w_hi, w_lo, x_hi, x_lo, start, stop, skip=False):
    pe.do(lambda e: e.matmul(out, w_hi, x_hi, start=start, stop=False, skip_group_check=skip))
    pe.do(lambda e: e.matmul(out, w_hi, x_lo, start=False, stop=False, skip_group_check=skip))
    return lambda e: e.matmul(out, w_lo, x_hi, start=False, stop=stop, skip_group_check=skip)


def hybrid_program(nc, x, wa, ba, bo, ident, mask_tri, wqa, wqb_t, wqb_pe, wqb_sw, wkva, wkvbk_t, wkvbv_t,
                   wout_b, rope_tab, conv_w, wmix, wv_t, router, wmix_out, rot_tab, out):
    top = ExitStack()
    with top:
        def sem(name):
            return top.enter_context(nc.semaphore(name))

        def allocator(stack):
            return lambda name, shape, dt=F32: stack.enter_context(nc.sbuf_tensor(name, shape, dt))

        keep = allocator(top)
        pe, act, dve, pool, sp = (Stream(sem(n)) for n in
                                  ("pe_steps", "act_steps", "dve_steps", "pool_steps", "sp_steps"))
        engines = (pe, act, dve, pool)
        bank = [top.enter_context(nc.psum_tensor(f"bank{i}", [P, 512], F32)) for i in range(8)]

        X = keep("X", [P, NT, DM])
        OP_hi = keep("OP_hi", [P, KT * TOK], F32R)
        OP_lo = keep("OP_lo", [P, KT * TOK], F32R)
        ident_f = keep("ident_f", [P, P])
        mask = keep("mask", [P, SEQ])
        stats = keep("stats", [P, NT, 6])
        moments = keep("moments", [P, NT, 2])
        std = keep("std", [P, NT])
        rstd = keep("rstd", [P, NT])
        xn = keep("xn", [P, 4, DM])
        raw = keep("raw", [P, MIX_WORDS])
        wv_t_sb = keep("wv_t_sb", [P, KT, DM])
        router_sb = keep("router_sb", [P, KT, 2 * MIX_H])
        conv_sb = keep("conv_sb", [P, KT, 2])
        rot_sb = keep("rot_sb", [P, BATCH - 1, 2, MIX_HDK])
        k_tmp = keep("k_tmp", [P, KT, MIX_DK])
        v_mean = keep("v_mean", [P, KT, MIX_H])

        dma_x = [sem(f"dma_x{b}") for b in range(BATCH)]
        dma_const = sem("dma_const")
        dma_small = sem("dma_small")
        dma_mix = [sem("dma_mix0"), sem("dma_mix1")]
        dma_out = sem("dma_out")

        x_tiles = x.rearrange("(t p) d -> p t d", p=P)
        out_tiles = out.rearrange("(t p) d -> p t d", p=P)

        def load_x(b):
            sp.dma(X[:, 4 * b:4 * b + 4, :], x_tiles[:, 4 * b:4 * b + 4, :], dma_x[b])

        def barrier():
            marks = [s.last() for s in engines if s.count]
            for s in (*engines, sp):
                s.wait(*marks)

        def tile_stats(tiles, *ready):
            dve.wait(*ready)
            for t in tiles:
                m = dve.counted(lambda e, t=t: e.bn_stats(stats[:, t, :], X[:, t, :]))
            dve.wait(m)
            for t in tiles:
                m = dve.counted(lambda e, t=t: e.bn_aggr(moments[:, t, :], stats[:, t, :]))
            return m

        def inverse_std(a, z):
            dve.wait(dve.last())
            m = dve.counted(lambda e: e.tensor_scalar(std[:, a:z], moments[:, a:z, 1], EPS, None, ALU.add))
            act.wait(m)
            m = act.counted(lambda e: e.activation(std[:, a:z], std[:, a:z], ACT.Sqrt))
            dve.wait(m)
            m = dve.counted(lambda e: e.reciprocal(rstd[:, a:z], std[:, a:z]))
            dve.wait(m)

        xn_read = [()]

        def normalise_four(tiles):
            dve.wait(*xn_read[0])
            for k, t in enumerate(tiles):
                m = dve.counted(lambda e, k=k, t=t: e.tensor_scalar(
                    xn[:, k, :], X[:, t, :], moments[:, t, 0:1], rstd[:, t:t + 1],
                    ALU.subtract, ALU.mult))
            return m

        def transpose_half(f, k, ready, *free):
            pe.wait(ready, *free)
            for j in range(4):
                step = (lambda e, j=j: e.transpose(bank[k][:, j * P:(j + 1) * P],
                                                   xn[:, j, f * P:(f + 1) * P], ident_f[:, :]))
                if j < 3:
                    pe.do(step)
            m = pe.counted(step)
            xn_read[0] = (m,)
            return m

        def split_from(psum_ap, hi, lo, ready, free=(), bias=None, later=None):
            act.wait(ready, *free)
            if bias is None:
                m = act.counted(lambda e: e.activation(hi, psum_ap, ACT.Copy))
            else:
                m = act.counted(lambda e: e.activation(hi, psum_ap, ACT.Identity, bias=bias))

            def remainder():
                dve.wait(m)
                if bias is None:
                    return dve.counted(lambda e: e.tensor_tensor(lo, psum_ap, hi.bitcast(F32),
                                                                 ALU.subtract))
                return dve.counted(lambda e: e.scalar_tensor_tensor(
                    out=lo, in0=psum_ap, scalar=bias, in1=hi.bitcast(F32), op0=ALU.add,
                    op1=ALU.subtract))

            return remainder if later else remainder()

        def mix_cols(t, a, z):
            return t[:, 0:KT * MIX_COLS].rearrange("p (k n) -> p k n", k=KT)[:, :, a:z]

        def mix_out_w(t):
            return t[:, KT * MIX_COLS:MIX_WORDS].rearrange("p (k n) -> p k n", k=KT)

        def load_mix(which, *free):
            sp.wait(*free)
            sp.dma(mix_cols(raw, 0, MIX_LOGIT), wmix[:, :, 0:MIX_LOGIT], dma_mix[which])
            sp.dma(mix_cols(raw, MIX_K, MIX_K + MIX_DK), wmix[:, :, MIX_LOGIT:MIX_LOGIT + MIX_DK],
                   dma_mix[which])
            sp.dma(mix_cols(raw, MIX_V, MIX_COLS), wmix[:, :, MIX_LOGIT + MIX_DK:], dma_mix[which])
            sp.dma(mix_out_w(raw), wmix_out, dma_mix[which])

        def prepare_mix(which, take, give):
            loaded = ((dma_mix[which], 64), (dma_small, 64))
            k = take()
            pe.wait(*loaded)
            for f in range(KT):
                for kt in range(KT):
                    step = (lambda e, f=f, kt=kt: e.matmul(
                        bank[k][:, f * 32:(f + 1) * 32], wv_t_sb[:, kt, f * P:(f + 1) * P],
                        router_sb[:, kt, :], start=(kt == 0), stop=(kt == KT - 1)))
                    if f < KT - 1 or kt < KT - 1:
                        pe.do(step)
            m = pe.counted(step)
            act.wait(m, *loaded)
            m_logit = act.counted(lambda e: e.activation(
                mix_cols(raw, MIX_LOGIT, MIX_K),
                bank[k][:, 0:KT * 32].rearrange("p (f n) -> p f n", f=KT), ACT.Copy))
            give(k, m_logit)
            pool.wait(*loaded, pool.last())
            heads = lambda ap: ap.rearrange("p k (h f) -> p k h f", f=MIX_HDK)
            k0 = heads(mix_cols(raw, MIX_K, MIX_K + MIX_DK))
            half = MIX_HDK // 2
            for d in range(1, BATCH):
                kd = heads(mix_cols(raw, MIX_K + d * MIX_DK, MIX_K + (d + 1) * MIX_DK))
                tab = lambda j, a, z, d=d: (rot_sb[:, d - 1, j, a:z].unsqueeze(1)
                                            .to_broadcast([P, MIX_H, z - a]))
                for kt in range(KT):
                    for a in range(2):
                        o, i = slice(a * half, (a + 1) * half), slice((1 - a) * half, (2 - a) * half)
                        pool.do(lambda e, o=o, i=i, kd=kd, tab=tab, kt=kt: e.tensor_tensor(
                            kd[:, kt, :, o], k0[:, kt, :, i], tab(1, o.start, o.stop), ALU.mult))
                    m = pool.counted(lambda e, kt=kt, tab=tab: e.tensor_tensor(
                        heads(k_tmp[:, :, :])[:, kt], k0[:, kt], tab(0, 0, MIX_HDK), ALU.mult))
                pool.wait(m)
                m = pool.counted(lambda e, kd=kd: e.tensor_tensor(kd, kd, heads(k_tmp[:, :, :]), ALU.add))
                pool.wait(m)
            dve.wait(*loaded)
            vh = mix_cols(raw, MIX_V, MIX_COLS).rearrange("p k (h d) -> p k h d", d=MIX_HDV)
            m_v = dve.counted(lambda e: e.tensor_reduce(v_mean[:, :, :], vh, AX.X, ALU.add))
            dve.wait(m_v)
            m_v = dve.counted(lambda e: e.tensor_scalar(v_mean[:, :, :], v_mean[:, :, :], 1.0 / MIX_HDV,
                                                        None, ALU.mult))
            dve.wait(m_v)
            for kt in range(KT):
                m_v = dve.counted(lambda e, kt=kt: e.tensor_tensor(
                    vh[:, kt], vh[:, kt],
                    v_mean[:, kt, :].unsqueeze(2).to_broadcast([P, MIX_H, MIX_HDV]), ALU.subtract))
            return (m, m_v, m_logit, *loaded)

        def split_mix(ready, *free):
            act.wait(*ready, *free)
            m = act.counted(lambda e: e.activation(OP_hi[:, 0:MIX_WORDS], raw[:, :], ACT.Copy))
            dve.wait(m)
            return dve.counted(lambda e: e.tensor_tensor(
                OP_lo[:, 0:MIX_WORDS], raw[:, :], OP_hi[:, 0:MIX_WORDS].bitcast(F32), ALU.subtract))

        class Core:

            def __init__(self, al, tag, split, ring):
                self.split, self.ring = split, ring
                self.negmax = al(f"{tag}_negmax", [P, 8, TPB])
                self.rowsum = al(f"{tag}_rowsum", [P, 8, TPB])
                self.rinv = al(f"{tag}_rinv", [P, 8, TPB])
                self.probs = al(f"{tag}_probs", [P, ring, TPB, SEQ])
                self.s_banks, self.t_banks, self.acc_banks = (0, 1, 2), (3, 4), (5, 6, 7)
                self.free = {k: () for k in range(8)}
                self.n_s = self.n_t = self.n_acc = 0
                self.norm, self.transposed, self.pt = {}, {}, {}
                self.substep, self.due = 0, []

            def after(self, delay, step):
                self.due.append((self.substep + delay, step))

            def flush(self):
                self.substep += 1
                now = [f for t, f in self.due if t <= self.substep]
                self.due = [(t, f) for t, f in self.due if t > self.substep]
                for step in now:
                    step()

            def take(self):
                k = self.acc_banks[self.n_acc % 3]
                self.n_acc += 1
                pe.wait(*self.free[k])
                return k

            def give(self, k, mark):
                self.free[k] = (mark,)

            def scores(self, n, i, q_hi, q_lo, k_hi, k_lo, ready):
                k = self.s_banks[self.n_s % 3]
                self.n_s += 1
                cols = P * (i + 1)
                s_ap = bank[k][:, 0:cols]
                slot = n % 8
                pe.wait(*ready, *self.free[k])
                qs = slice(P * i, P * i + P)
                done = pe.counted(three_pass(pe, s_ap, q_hi[:, qs], q_lo[:, qs], k_hi[:, 0:cols],
                                             k_lo[:, 0:cols], True, True))
                nm = self.negmax[:, slot, i:i + 1]
                rs = self.rowsum[:, slot, i:i + 1]
                ri = self.rinv[:, slot, i:i + 1]
                pr = self.probs[:, n % self.ring, i, 0:cols]
                dve.wait(done)
                m = dve.counted(lambda e: e.tensor_tensor_reduce(
                    s_ap, s_ap, mask[:, SEQ - cols:SEQ], -1.0, 3.0e38, ALU.add, ALU.min, nm))
                act.wait(m, *before(self.transposed, n - self.ring, i))
                m = act.counted(lambda e: e.activation(pr, s_ap, ACT.Exp, bias=nm, scale=-1.0,
                                                       accum_out=rs))
                self.free[k] = (m,)
                self.pending = (n, i, m, ri, rs, pr, cols)
                return done

            def normalise(self, pending):
                n, i, m, ri, rs, pr, cols = pending
                dve.wait(m)
                m = dve.counted(lambda e: e.reciprocal(ri, rs))
                pool.wait(m, pool.last())
                self.norm[n, i] = pool.counted(
                    lambda e: e.tensor_tensor(pr, pr, ri.to_broadcast([P, cols]), ALU.mult))

            def transposes(self, n, i, dst, free):
                k = self.t_banks[self.n_t % 2]
                self.n_t += 1
                pe.wait(self.norm[n, i], *self.free[k])
                for j in range(i + 1):
                    step = (lambda e, j=j: e.transpose(bank[k][:, P * j:P * j + P],
                                                       self.probs[:, n % self.ring, i, P * j:P * j + P], ident_f[:, :]))
                    if j < i:
                        pe.do(step)
                done = pe.counted(step)
                self.transposed[n, i] = (done,)
                src = bank[k][:, 0:P * (i + 1)].rearrange("p (j q) -> p j q", q=P)
                qs = slice(P * i, P * i + P)
                if self.split:
                    hi, lo = dst
                    lo_step = split_from(src, hi[:, 0:i + 1, qs], lo[:, 0:i + 1, qs], done, free,
                                         later=True)

                    def finish():
                        self.pt[n, i] = lo_step()
                        self.free[k] = (self.pt[n, i],)
                    return finish
                elif i % 2:
                    act.wait(done, *free)
                    m = act.counted(lambda e: e.activation(dst[:, 0:i + 1, qs], src, ACT.Copy))
                else:
                    dve.wait(done, *free)
                    m = dve.counted(lambda e: e.tensor_copy(dst[:, 0:i + 1, qs], src))
                self.free[k] = (m,)
                self.pt[n, i] = m
                return lambda: None

        def attention_a():
            ctx = ExitStack()
            al = allocator(ctx)
            GWORDS = 2048
            XT_hi, XT_lo = (t[:, :].rearrange("p (k n) -> p k n", k=KT) for t in (OP_hi, OP_lo))
            W_hi = al("a_W_hi", [P, 2, GWORDS], F32R)
            W_lo = al("a_W_lo", [P, 2, GWORDS], F32R)
            bias = al("a_bias", [P, 3, HEADS])
            bo_bc = al("a_bo", [P, DM])
            Q_hi, Q_lo, K_hi, K_lo = (al(f"a_{n}", [P, 2, SEQ], F32R) for n in ("Qh", "Ql", "Kh", "Kl"))
            V_hi, V_lo = (al(f"a_{n}", [P, 2, TPB, GW], F32R) for n in ("Vh", "Vl"))
            PT_hi, PT_lo = (al(f"a_{n}", [P, 2, TPB, SEQ], F32R) for n in ("PTh", "PTl"))
            Z_hi, Z_lo = (al(f"a_{n}", [P, 2, GH, SEQ], F32R) for n in ("Zh", "Zl"))
            core = Core(al, "a", split=True, ring=1)
            dma_w = [sem(f"dma_wa{g}") for g in range(NG)]
            dma_b = sem("dma_ba")

            def wq(t, s): return t[:, s, 0:512].rearrange("p (k h e) -> p k h e", k=KT, h=GH)
            def wk(t, s): return t[:, s, 512:1024].rearrange("p (k h e) -> p k h e", k=KT, h=GH)
            def wv(t, s): return t[:, s, 1024:1536].rearrange("p (k n) -> p k n", k=KT)
            def wo(t, s): return t[:, s, 1536:2048].rearrange("p (h d) -> p h d", h=GH)

            load_x(0)
            sp.dma(ident_f[:, :], ident, dma_const)
            sp.dma(raw[:, 0:GWORDS], wa[0], dma_w[0])
            sp.dma(bias[:, :, :], ba, dma_b)
            for b in range(1, BATCH):
                load_x(b)
            sp.dma(mask[:, SEQ - P:SEQ], mask_tri, dma_const)
            sp.dma(bo_bc[:, :], bo.to_broadcast([P, DM]), dma_b)
            for dst, src in ((wv_t_sb, wv_t), (router_sb, router), (conv_sb, conv_w)):
                sp.dma(dst[:, :, :], src, dma_small)
            sp.dma(rot_sb[:, :, :, :], rot_tab, dma_small)

            pool.do(lambda e: e.memset(mask[:, 0:SEQ - P], 0.0))
            pool.wait((dma_b, 32), (dma_w[0], 16))
            pool.do(lambda e: e.tensor_scalar(bias[:, 0, :], bias[:, 0, :], SCALE_A, None, ALU.mult))
            consts = pool.counted(lambda e: e.tensor_scalar(raw[:, 0:512], raw[:, 0:512], SCALE_A, None,
                                                            ALU.mult))
            tile_stats(range(0, 4), (dma_x[0], 16))
            inverse_std(0, 4)
            pe.wait((dma_const, 32))

            xt_ready = {}

            def norm_batch(b):
                xn_ready = normalise_four(range(4 * b, 4 * b + 4))
                cols = slice(b * SEQ, (b + 1) * SEQ)
                for f in range(KT):
                    k = core.take()
                    m = transpose_half(f, k, xn_ready)
                    xt_ready[b] = split_from(bank[k][:, :], XT_hi[:, f, cols], XT_lo[:, f, cols], m)
                    core.give(k, xt_ready[b])

            norm_batch(0)
            w_ready, qkv_read, o_read = {}, {}, {}
            act.wait((dma_w[0], 16), consts)
            m = act.counted(lambda e: e.activation(W_hi[:, 0, :], raw[:, 0:GWORDS], ACT.Copy))
            dve.wait(m, consts, (dma_const, 32))
            w_ready[0] = dve.counted(lambda e: e.tensor_tensor(
                W_lo[:, 0, :], raw[:, 0:GWORDS], W_hi[:, 0, :].bitcast(F32), ALU.subtract))
            sp.wait(w_ready[0])
            sp.dma(raw[:, 0:GWORDS], wa[1], dma_w[1])
            act.wait((dma_b, 32))
            for b in range(1, BATCH):
                m = tile_stats(range(4 * b, 4 * b + 4), (dma_x[b], 16))
            inverse_std(4, NT)

            bias_in = {}

            def add_output_bias(b):
                pool.wait(xt_ready[b], (dma_b, 32), pool.last())
                bias_in[b] = pool.counted(lambda e: e.tensor_tensor(
                    X[:, 4 * b:4 * b + 4, :], X[:, 4 * b:4 * b + 4, :],
                    bo_bc[:, :].unsqueeze(1).to_broadcast([P, 4, DM]), ALU.add))

            def split_weights(g, part):
                s, cols = g % 2, slice(512 * part, 512 * part + 512)
                pool.wait((dma_w[g], 16), *before(o_read if part == 3 else qkv_read, g - 2))
                if part == 0:
                    pool.wait(pool.counted(lambda e: e.tensor_scalar(raw[:, cols], raw[:, cols], SCALE_A,
                                                                     None, ALU.mult)))
                pool.wait(pool.counted(lambda e: e.tensor_scalar(W_hi[:, s, cols], raw[:, cols], 1.0, None,
                                                                 ALU.mult)))
                w_ready[g] = pool.counted(lambda e: e.tensor_tensor(
                    W_lo[:, s, cols], raw[:, cols], W_hi[:, s, cols].bitcast(F32), ALU.subtract))
                if part == 3:
                    if g + 1 < NG:
                        sp.wait(w_ready[g])
                        sp.dma(raw[:, 0:GWORDS], wa[g + 1], dma_w[g + 1])
                    else:
                        load_mix(0, w_ready[g])

            units = NG * BATCH * GH
            qk_ready, s_done, v_ready, av_done, z_ready, o_done = {}, {}, {}, {}, {}, {}

            def place(n):
                return n // 8, (n % 8) // 2, n % 2

            def project(n, which):
                g, b, hh = place(n)
                s, cols = g % 2, slice(b * SEQ, (b + 1) * SEQ)
                view = (wq, wk)[which]
                hi, lo = ((Q_hi, Q_lo), (K_hi, K_lo))[which]
                k = core.take()
                pe.wait(w_ready[g], xt_ready[b])
                for kt in range(KT):
                    step = three_pass(pe, bank[k][:, :], view(W_hi, s)[:, kt, hh, :],
                                      view(W_lo, s)[:, kt, hh, :], XT_hi[:, kt, cols],
                                      XT_lo[:, kt, cols], kt == 0, kt == KT - 1)
                    if kt < KT - 1:
                        pe.do(step)
                m = pe.counted(step)
                h = g * GH + hh
                lo_step = split_from(bank[k][:, :], hi[:, n % 2, :], lo[:, n % 2, :], m,
                                     before(s_done, n - 2), bias=bias[:, which, h:h + 1], later=True)

                def finish():
                    qk_ready[n, which] = lo_step()
                    core.give(k, qk_ready[n, which])
                core.after(1, finish)

            def project_v(u, half):
                g, b = u // BATCH, u % BATCH
                s = g % 2
                k = core.take()
                pe.wait(w_ready[g], xt_ready[b])
                for tt in range(2):
                    cols = slice(b * SEQ + (2 * half + tt) * P, b * SEQ + (2 * half + tt + 1) * P)
                    for kt in range(KT):
                        step = three_pass(pe, bank[k][:, tt * GW:(tt + 1) * GW], XT_hi[:, kt, cols],
                                          XT_lo[:, kt, cols], wv(W_hi, s)[:, kt, :],
                                          wv(W_lo, s)[:, kt, :], kt == 0, kt == KT - 1)
                        if tt == 0 or kt < KT - 1:
                            pe.do(step)
                m = pe.counted(step)
                if b == BATCH - 1 and half == 1:
                    qkv_read[g] = (m,)
                src = bank[k][:, :].rearrange("p (t n) -> p t n", t=2)
                tts = slice(2 * half, 2 * half + 2)
                lo_step = split_from(src, V_hi[:, u % 2, tts, :], V_lo[:, u % 2, tts, :], m,
                                     before(av_done, 2 * (u - 2) + 1), later=True)

                def finish():
                    v_ready[u, half] = lo_step()
                    core.give(k, v_ready[u, half])
                core.after(1, finish)

            def scores(n, i):
                q = n % 2
                m = core.scores(n, i, Q_hi[:, q, :], Q_lo[:, q, :], K_hi[:, q, :], K_lo[:, q, :],
                                [qk_ready[n, 0], qk_ready[n, 1]])
                s_done[n] = (m,)
                return core.pending

            def values(n):
                g, b, hh = place(n)
                u, q = n // 2, n % 2
                k = core.take()
                pe.wait(v_ready[u, 0], v_ready[u, 1], core.pt[n, TPB - 1])
                for i in range(TPB):
                    pe.wait(core.pt[n, i])
                hs = slice(hh * DH, (hh + 1) * DH)
                for j in range(TPB):
                    qs = slice(P * j, SEQ)
                    step = three_pass(pe, bank[k][:, qs], V_hi[:, u % 2, j, hs], V_lo[:, u % 2, j, hs],
                                      PT_hi[:, q, j, qs], PT_lo[:, q, j, qs], j == 0, j == TPB - 1)
                    if j < TPB - 1:
                        pe.do(step)
                m = pe.counted(step)
                av_done[n] = (m,)
                h = g * GH + hh
                lo_step = split_from(bank[k][:, :], Z_hi[:, u % 2, hh, :], Z_lo[:, u % 2, hh, :], m,
                                     before(o_done, u - 2), bias=bias[:, 2, h:h + 1], later=True)

                def finish():
                    z_ready[u, hh] = lo_step()
                    core.give(k, z_ready[u, hh])
                core.after(1, finish)

            def output(u, half):
                g, b = u // BATCH, u % BATCH
                s = g % 2
                k = core.take()
                pe.wait(z_ready[u, 0], z_ready[u, 1])
                for tt in range(2):
                    cols = slice((2 * half + tt) * P, (2 * half + tt + 1) * P)
                    for hh in range(GH):
                        step = three_pass(pe, bank[k][:, tt * DM:(tt + 1) * DM],
                                          Z_hi[:, u % 2, hh, cols], Z_lo[:, u % 2, hh, cols],
                                          wo(W_hi, s)[:, hh, :], wo(W_lo, s)[:, hh, :],
                                          hh == 0, hh == GH - 1)
                        if tt == 0 or hh < GH - 1:
                            pe.do(step)
                m = pe.counted(step)
                if half == 1:
                    o_done[u] = (m,)
                    if b == BATCH - 1:
                        o_read[g] = (m,)
                t0 = 4 * b + 2 * half

                def finish():
                    dve.wait(m, bias_in[b], *x_added.get(t0, ()))
                    done = dve.counted(lambda e: e.tensor_tensor(
                        X[:, t0:t0 + 2, :], X[:, t0:t0 + 2, :],
                        bank[k][:, :].rearrange("p (t d) -> p t d", t=2), ALU.add))
                    x_added[t0] = (done,)
                    core.give(k, done)
                    if g == NG - 1:
                        tile_stats((t0, t0 + 1), done)
                core.after(1, finish)

            x_added = {}
            pool_todo = []
            project(0, 0)
            project(0, 1)
            core.flush()
            for n in range(units + 4):
                g, b, hh = place(n)
                if n in (0, 1, 2):
                    norm_batch(n + 1)
                if n < BATCH:
                    add_output_bias(n)
                if n % 8 in (1, 2, 3, 4) and g + 1 < NG:
                    split_weights(g + 1, n % 8 - 1)
                if n == units - 4:
                    mix_ready = prepare_mix(0, core.take, core.give)
                if n == units:
                    w_mix = split_mix(mix_ready, qkv_read[NG - 1][0])
                u = n // 2
                for i in range(TPB):
                    if 1 <= n <= units:
                        pt_lo = core.transposes(
                            n - 1, i, (PT_hi[:, (n - 1) % 2, :, :], PT_lo[:, (n - 1) % 2, :, :]),
                            before(av_done, n - 3))
                    core.flush()
                    pend = scores(n, i) if n < units else None
                    if 1 <= n <= units:
                        pt_lo()
                    if pool_todo:
                        core.normalise(pool_todo.pop())
                    if pend:
                        pool_todo.append(pend)
                    if i == 0 and n + 1 < units:
                        project(n + 1, 0)
                    if i == 1 and n + 1 < units:
                        project(n + 1, 1)
                    if i == 2 and n < units:
                        project_v(u, hh)
                    if i == 3 and n >= 2 and n - 2 < units:
                        values(n - 2)
                    if i == 2 and n >= 4 and (n - 4) // 2 < units // 2:
                        output((n - 4) // 2, hh)
            barrier()
            ctx.close()
            return w_mix

        def mixture(tag, w_ready, last, between=lambda c, free: None):
            ctx = ExitStack()
            al0 = allocator(ctx)
            al = lambda name, shape, dt=F32: al0(f"{tag}_{name}", shape, dt)
            FIRST = [0, 4, 7, 9]
            QG = MIX_LOGIT
            xt = al("xt", [P, KT, SEQ])
            conv = al("conv", [P, KT, SEQ])
            C_hi, C_lo = (al(n, [P, 2, KT, SEQ], F32R) for n in ("C_hi", "C_lo"))
            RING = 3
            qg = al("qg", [P, RING, BATCH, QG])
            vv = al("vv", [P, RING, BATCH, MIX_DV])
            lg = al("lg", [P, RING, BATCH, 2 * MIX_H])
            prod = al("prod", [P, PAIRS, MIX_DK])
            dots = al("dots", [P, RING, PAIRS, MIX_H])
            small = [al(f"sm{i}", [P, BATCH, MIX_H]) for i in range(12)]
            same = al("same", [P, BATCH, BATCH, MIX_H])
            coef = al("coef", [P, PAIRS, MIX_H])
            ov = al("ov", [P, 6, MIX_DV])
            oo = al("oo", [P, BATCH, MIX_DV])
            sq = ov[:, 0:BATCH, :]
            yy = al("yy", [P, BATCH, MIX_DV])
            Y_hi, Y_lo = (t[:, MIX_WORDS:MIX_WORDS + KT * SEQ].rearrange("p (k n) -> p k n", k=KT)
                          for t in (OP_hi, OP_lo))
            tri = al("tri", [P, BATCH, BATCH, MIX_H])

            small_loaded = (dma_small, 64)
            pool.wait(pool.counted(lambda e: e.memset(tri[:, :, :, :], 0.0)))
            for l in range(BATCH):
                tri_ready = pool.counted(lambda e, l=l: e.memset(tri[:, l, 0:l + 1, :], 1.0))
            inverse_std(0, NT)

            free = {k: () for k in range(8)}
            marks, used = {}, [0]

            def earlier(kind, c):
                return marks[kind, c] if c >= 0 else ()

            def front_a(c):
                ready = normalise_four([4 * l + c for l in range(BATCH)])
                act.wait(small_loaded)
                dve.wait(small_loaded)
                for f in range(KT):
                    m = transpose_half(f, f, ready, *free[f])
                    act.wait(m, *earlier("conv", c - 1))
                    act.do(lambda e, f=f: e.activation(xt[:, f, :], bank[f][:, :], ACT.Copy))
                    m = act.counted(lambda e, f=f: e.activation(conv[:, f, :], bank[f][:, :], ACT.Copy,
                                                                scale=conv_sb[:, f, 1:2]))
                    free[f] = (m,)
                    marks["taps", c, f] = m

            def front_b(c):
                for f in range(KT):
                    dve.wait(marks["taps", c, f])
                    m = dve.counted(lambda e, f=f: e.scalar_tensor_tensor(
                        out=conv[:, f, P:SEQ], in0=xt[:, f, 0:SEQ - P], scalar=conv_sb[:, f, 0:1],
                        in1=conv[:, f, P:SEQ], op0=ALU.mult, op1=ALU.add))
                act.wait(m, *earlier("proj", c - 2))
                m = act.counted(lambda e: e.activation(conv[:, :, :], conv[:, :, :], ACT.Silu))
                act.wait(m)
                m = act.counted(lambda e: e.activation(C_hi[:, c % 2, :, :], conv[:, :, :], ACT.Copy))
                pool.wait(m, pool.last())
                m = pool.counted(lambda e: e.tensor_tensor(C_lo[:, c % 2, :, :], conv[:, :, :],
                                                           C_hi[:, c % 2, :, :].bitcast(F32), ALU.subtract))
                marks["conv", c] = marks["lo", c] = (m,)

            def columns(c, l, a, z, at=0, k=None):
                if k is None:
                    k = 4 + used[0] % 4
                    used[0] += 1
                    pe.wait(*marks["lo", c], w_ready, *free[k])
                cols, q = slice(l * P, (l + 1) * P), c % 2
                for kt in range(KT):
                    step = three_pass(pe, bank[k][:, at:at + z - a], C_hi[:, q, kt, cols],
                                      C_lo[:, q, kt, cols], mix_cols(OP_hi, a, z)[:, kt, :],
                                      mix_cols(OP_lo, a, z)[:, kt, :], kt == 0, kt == KT - 1)
                    if kt < KT - 1:
                        pe.do(step)
                return k, pe.counted(step)

            def project_gates(c):
                r = c % RING
                for l in range(BATCH):
                    k, m = columns(c, l, 0, MIX_K)
                    act.wait(m, *earlier("mix", c - RING))
                    act.do(lambda e, l=l, k=k: e.activation(qg[:, r, l, :], bank[k][:, 0:QG], ACT.Silu))
                    m = act.counted(lambda e, l=l, k=k: e.activation(
                        lg[:, r, l, :], bank[k][:, QG:QG + 2 * MIX_H], ACT.Copy))
                    free[k] = (m,)
                marks["qg", c] = (m,)

            def project_kv(c):
                r = c % RING
                for m_ in range(BATCH):
                    n = BATCH - m_
                    k, kv = columns(c, m_, MIX_K, MIX_K + n * MIX_DK)
                    at = 0
                    v_bank = k
                    if n <= 2:
                        at = n * MIX_DK
                        _, vd = columns(c, m_, MIX_V, MIX_COLS, at, k)
                        kv = vd
                    else:
                        v_bank, vd = columns(c, m_, MIX_V, MIX_COLS)
                    dve.wait(kv, *marks["qg", c], *earlier("dots", c - 1))
                    mp = dve.counted(lambda e, m_=m_, n=n, k=k: e.tensor_tensor(
                        prod[:, FIRST[m_]:FIRST[m_] + n, :],
                        bank[k][:, 0:n * MIX_DK].rearrange("p (n f) -> p n f", n=n),
                        qg[:, r, m_:BATCH, 0:MIX_DK], ALU.mult))
                    free[k] = (mp,)
                    act.wait(vd, *((mp,) if v_bank == k else ()))
                    mv = act.counted(lambda e, m_=m_, v_bank=v_bank, at=at: e.activation(
                        vv[:, r, m_, :], bank[v_bank][:, at:at + MIX_DV], ACT.Copy))
                    free[v_bank] = (mv,)
                marks["proj", c] = (pe.last(),)
                marks["v", c] = (mv,)
                dve.wait(mp)
                m = dve.counted(lambda e: e.tensor_reduce(
                    dots[:, r, :, :].rearrange("p n h -> p (n h)"),
                    prod[:, :, :].rearrange("p n (h f) -> p (n h) f", f=MIX_HDK), AX.X, ALU.add))
                marks["dots", c] = (m,)

            def chain(step):
                m = dve.counted(step)
                dve.wait(m)
                return m

            (diff, first, mag, prob, cnt, rcnt, tmp, pw, var, dev, inv_dev, neg) = (
                t[:, :, :] for t in small)

            def route(c):
                r = c % RING
                LG = lg[:, r, :, :]
                dve.wait(*marks["qg", c], tri_ready)
                chain(lambda e: e.tensor_tensor(diff, LG[:, :, 0:MIX_H], LG[:, :, MIX_H:2 * MIX_H],
                                                ALU.subtract))
                dve.do(lambda e: e.tensor_scalar(neg, diff, -1.0, None, ALU.mult))
                chain(lambda e: e.tensor_scalar(first, diff, 0.0, None, ALU.is_ge))
                m = dve.counted(lambda e: e.tensor_tensor(mag, diff, neg, ALU.max))
                act.wait(m)
                marks["prob", c] = (act.counted(lambda e: e.activation(prob, mag, ACT.Tanh, scale=0.5)),)
                chain(lambda e: e.tensor_tensor(same[:, :, :, :],
                                                first.unsqueeze(2).to_broadcast([P, BATCH, BATCH, MIX_H]),
                                                first.unsqueeze(1).to_broadcast([P, BATCH, BATCH, MIX_H]),
                                                ALU.is_equal))
                chain(lambda e: e.tensor_tensor(same[:, :, :, :], same[:, :, :, :], tri[:, :, :, :],
                                                ALU.mult))
                chain(lambda e: e.tensor_reduce(cnt, same[:, :, :, :].rearrange("p l m h -> p l h m"),
                                                AX.X, ALU.add))
                dve.do(lambda e: e.reciprocal(rcnt, cnt))

            def coefficients(c):
                r = c % RING
                dve.wait(*marks["prob", c])
                chain(lambda e: e.tensor_scalar(tmp, prob, 0.5 * MIX_HDK ** -0.5, 0.5 * MIX_HDK ** -0.5,
                                                ALU.mult, ALU.add))
                chain(lambda e: e.tensor_tensor(pw, tmp, rcnt, ALU.mult))
                dve.wait(*earlier("weighted", c - 1))
                for m_ in range(BATCH):
                    n = BATCH - m_
                    mm = dve.counted(lambda e, m_=m_, n=n: e.tensor_tensor(
                        coef[:, FIRST[m_]:FIRST[m_] + n, :], same[:, m_:BATCH, m_, :],
                        pw[:, m_:BATCH, :], ALU.mult))
                dve.wait(mm, *marks["dots", c])
                marks["coef", c] = (chain(lambda e: e.tensor_tensor(coef[:, :, :], coef[:, :, :],
                                                                    dots[:, r, :, :], ALU.mult)),)

            heads = lambda ap: ap.rearrange("p m (h d) -> p m h d", d=MIX_HDV)

            def weighted(m_, dst, r):
                n = BATCH - m_
                v = vv[:, r, m_, :].rearrange("p (h d) -> p h d", d=MIX_HDV)
                w = coef[:, FIRST[m_]:FIRST[m_] + n, :]
                shape = [P, n, MIX_H, MIX_HDV]
                return lambda e: e.tensor_tensor(heads(dst), v.unsqueeze(1).to_broadcast(shape),
                                                 w.unsqueeze(3).to_broadcast(shape), ALU.mult)

            parts = {}

            def products(c):
                r = c % RING
                pool.wait(*marks["coef", c], *marks["v", c], *earlier("squares", c - 1), pool.last())
                at = 0
                for m_ in range(1, BATCH):
                    dst = ov[:, at:at + BATCH - m_, :]
                    parts[m_] = (dst, pool.counted(weighted(m_, dst, r)))
                    at += BATCH - m_
                marks["weighted", c] = (pool.last(),)
                dve.wait(*marks["v", c], *earlier("gated", c - 1), *earlier("squared", c - 1))
                marks["first", c] = dve.counted(weighted(0, oo[:, :, :], r))

            def total(c):
                r = c % RING
                m = marks["first", c]
                for m_ in range(1, BATCH):
                    dst, ready = parts[m_]
                    dve.wait(m, ready)
                    m = dve.counted(lambda e, m_=m_, dst=dst: e.tensor_tensor(
                        oo[:, m_:BATCH, :], oo[:, m_:BATCH, :], dst, ALU.add))
                act.wait(m)
                marks["squared", c] = (act.counted(lambda e: e.activation(sq, oo[:, :, :], ACT.Square)),)
                pool.wait(m, *earlier("yt", c - 1))
                marks["gated", c] = (pool.counted(lambda e: e.tensor_tensor(
                    yy[:, :, :], oo[:, :, :], qg[:, r, :, MIX_DK:QG], ALU.mult)),)

            def variance(c):
                dve.wait(*marks["squared", c])
                marks["squares", c] = (chain(lambda e: e.tensor_reduce(
                    var.rearrange("p l h -> p (l h)"), sq.rearrange("p l (h d) -> p (l h) d", d=MIX_HDV),
                    AX.X, ALU.add)),)
                m = dve.counted(lambda e: e.tensor_scalar(var, var, 1.0 / MIX_HDV, EPS, ALU.mult, ALU.add))
                act.wait(m)
                marks["root", c] = (act.counted(lambda e: e.activation(dev, var, ACT.Sqrt)),)

            def scale(c):
                dve.wait(*marks["root", c])
                chain(lambda e: e.reciprocal(inv_dev, dev))
                dve.wait(*marks["gated", c])
                m = dve.counted(lambda e: e.tensor_tensor(
                    yy[:, :, :].rearrange("p l (h d) -> p (l h) d", d=MIX_HDV),
                    yy[:, :, :].rearrange("p l (h d) -> p (l h) d", d=MIX_HDV),
                    inv_dev.rearrange("p l h -> p (l h)").unsqueeze(2)
                    .to_broadcast([P, BATCH * MIX_H, MIX_HDV]), ALU.mult))
                marks["mix", c] = marks["y", c] = (m,)

            def turn(c):
                pe.wait(*marks["y", c])
                for f in range(KT):
                    k = 2 + f
                    pe.wait(*free[k])
                    for l in range(BATCH):
                        step = (lambda e, l=l, f=f, k=k: e.transpose(
                            bank[k][:, l * P:(l + 1) * P], yy[:, l, f * P:(f + 1) * P], ident_f[:, :]))
                        if l < BATCH - 1:
                            pe.do(step)
                    m = pe.counted(step)
                    lo = split_from(bank[k][:, :], Y_hi[:, f, :], Y_lo[:, f, :], m, earlier("out", c - 1))
                    free[k] = (lo,)
                marks["yt", c] = (pe.last(),)
                marks["ysplit", c] = (lo,)

            def output(c):
                for half in range(2):
                    k = 2 + half
                    pe.wait(*marks["ysplit", c], *free[k])
                    for a in range(2):
                        l = 2 * half + a
                        cols = slice(l * P, (l + 1) * P)
                        for kt in range(KT):
                            step = three_pass(pe, bank[k][:, a * DM:(a + 1) * DM], Y_hi[:, kt, cols],
                                              Y_lo[:, kt, cols], mix_out_w(OP_hi)[:, kt, :],
                                              mix_out_w(OP_lo)[:, kt, :], kt == 0, kt == KT - 1)
                            if a == 0 or kt < KT - 1:
                                pe.do(step)
                    m = pe.counted(step)
                    tiles = X[:, 8 * half:8 * half + 8, :].rearrange("p (a r) d -> p a r d", r=4)[:, :, c, :]
                    dve.wait(m)
                    m = dve.counted(lambda e, tiles=tiles, k=k: e.tensor_tensor(
                        tiles, tiles, bank[k][:, :].rearrange("p (a d) -> p a d", a=2), ALU.add))
                    free[k] = (m,)
                    if last:
                        sp.wait(m)
                        for a in range(2):
                            t = 4 * (2 * half + a) + c
                            sp.dma(out_tiles[:, t, :], X[:, t, :], dma_out)
                marks["out", c] = (pe.last(),)
                if not last:
                    tile_stats([4 * l + c for l in range(BATCH)], m)

            stages = [front_a, front_b, project_gates, lambda c: (project_kv(c), route(c)),
                      lambda c: (coefficients(c), products(c)), total, variance,
                      lambda c: (scale(c), turn(c)), lambda c: (output(c), between(c, free))]
            for slot in range(len(stages) + SKEW * (TPB - 1)):
                for c in range(TPB):
                    if 0 <= slot - SKEW * c < len(stages):
                        stages[slot - SKEW * c](c)
            if not last:
                barrier()
            ctx.close()

        class LatentAttention:

            def __init__(self):
                self.ctx = ExitStack()
                al = allocator(self.ctx)
                self.Wq = al("b_Wq", [P, HEADS, P], F32R)
                self.Wsw = al("b_Wsw", [P, HEADS // 2, P], F32R)
                self.N_hi, self.N_lo = (al(f"b_{n}", [P, HEADS // 2, DM], F32R) for n in ("Nh", "Nl"))
                self.Wc_hi, self.Wc_lo = (al(f"b_{n}", [P, KT, 4, P], F32R) for n in ("Wch", "Wcl"))
                self.pro = ExitStack()
                ap_ = allocator(self.pro)
                self.wsrc = ap_("b_wsrc", [P, KT, 4, P])
                self.qbt = ap_("b_qbt", [P, 4, 2, RANK])
                self.kbt = ap_("b_kbt", [P, 4, RANK])
                self.vbt = ap_("b_vbt", [P, 4, RANK])
                self.wo = ap_("b_wo", [P, 4, DM])
                self.wq_raw = ap_("b_wqraw", [P, 4, P])
                self.wsw_raw = ap_("b_wswraw", [P, HEADS // 2, P])
                self.dma_w, self.dma_heads = sem("dma_b_w"), sem("dma_b_heads")
                sp.dma(self.wsrc[:, :, 0, :], wqa, self.dma_w)
                sp.dma(self.wsrc[:, :, 1:4, :].rearrange("p k j n -> p k (j n)"), wkva, self.dma_w)
                for half in range(2):
                    sp.dma(self.wsw_raw[64 * half:64 * half + 64, :, :], wqb_sw, self.dma_w)
                self.loaded = (self.dma_w, 16 * 4)
                self.sent = 0
                self.load_heads(0)

            def load_heads(self, r):
                hs = slice(4 * r, 4 * r + 4)
                for rep in range(2):
                    sp.dma(self.qbt[:, :, rep, :], wqb_t[:, hs, :], self.dma_heads)
                sp.dma(self.kbt[:, :, :], wkvbk_t[:, hs, :], self.dma_heads)
                sp.dma(self.vbt[:, :, :], wkvbv_t[:, hs, :], self.dma_heads)
                sp.dma(self.wo[:, :, :], wout_b[:, hs, :], self.dma_heads)
                for half in range(2):
                    sp.dma(self.wq_raw[64 * half:64 * half + 64, :, :], wqb_pe[:, hs, :], self.dma_heads)
                self.sent += 7
                self.heads_loaded = (self.dma_heads, 16 * self.sent)

            def prepare(self, r, free):
                hs = slice(4 * r, 4 * r + 4)
                Wq, wq_raw = self.Wq, self.wq_raw
                pe.wait(self.heads_loaded, *free[0])
                for j in range(4):
                    step = (lambda e, j=j: e.matmul(bank[0][:, j * 64:(j + 1) * 64],
                                                    self.qbt[:, j, :, :].rearrange("p a r -> p (a r)"),
                                                    self.kbt[:, j, :], start=True, stop=True))
                    if j < 3:
                        pe.do(step)
                m = pe.counted(step)
                dve.wait(m, self.heads_loaded)
                absv = bank[0][:, 0:256].rearrange("p (j c) -> p j c", c=64)
                for par in range(2):
                    c0 = 0 if par == 0 else 64
                    m = dve.counted(lambda e, par=par, c0=c0: e.tensor_copy(
                        wq_raw[:, par:4:2, c0:c0 + 64], absv[:, par:4:2, :]))
                free[0] = (m,)
                dve.wait(m)
                dve.wait(dve.counted(lambda e: e.tensor_scalar(wq_raw[:, :, :], wq_raw[:, :, :], SCALE_B,
                                                               None, ALU.mult)))
                dve.wait(dve.counted(lambda e: e.tensor_copy(Wq[:, hs, :], wq_raw[:, :, :])))
                self.w_ready = dve.counted(lambda e: e.tensor_tensor(
                    Wq[64:128, hs, :], wq_raw[64:128, :, :], Wq[64:128, hs, :].bitcast(F32), ALU.subtract))
                pe.wait(*free[1])
                for pr in range(2):
                    for par in range(2):
                        j = 2 * pr + par
                        step = (lambda e, j=j, pr=pr, par=par: e.matmul(
                            bank[1][64 * par:64 * par + 64, pr * DM:(pr + 1) * DM], self.vbt[:, j, :],
                            self.wo[:, j, :], start=True, stop=True))
                        if j < 3:
                            pe.do(step)
                m = pe.counted(step)
                pair = slice(2 * r, 2 * r + 2)
                lo = split_from(bank[1][:, :].rearrange("p (a d) -> p a d", a=2),
                                self.N_hi[:, pair, :], self.N_lo[:, pair, :], m)
                free[1] = (lo,)
                self.n_ready = lo
                if r < 3:
                    sp.wait(m, self.w_ready)
                    self.load_heads(r + 1)
                else:
                    self.prepare_rest()

            def prepare_rest(self):
                pool.wait(self.loaded, pool.last())
                pool.wait(pool.counted(lambda e: e.tensor_scalar(self.Wc_hi[:, :, :, :],
                                                                 self.wsrc[:, :, :, :], 1.0, None, ALU.mult)))
                self.wc_ready = pool.counted(lambda e: e.tensor_tensor(
                    self.Wc_lo[:, :, :, :], self.wsrc[:, :, :, :], self.Wc_hi[:, :, :, :].bitcast(F32),
                    ALU.subtract))
                dve.wait(self.loaded)
                dve.wait(dve.counted(lambda e: e.tensor_scalar(
                    self.wsw_raw[:, :, :], self.wsw_raw[:, :, :], SCALE_B, None, ALU.mult)))
                dve.wait(dve.counted(lambda e: e.tensor_copy(self.Wsw[:, :, :], self.wsw_raw[:, :, :])))
                self.w_ready = dve.counted(lambda e: e.tensor_tensor(
                    self.Wsw[64:128, :, :], self.wsw_raw[64:128, :, :],
                    self.Wsw[64:128, :, :].bitcast(F32), ALU.subtract))

            def run(self):
                Wq, Wsw, N_hi, N_lo = self.Wq, self.Wsw, self.N_hi, self.N_lo
                Wc_hi, Wc_lo = self.Wc_hi, self.Wc_lo
                self.pro.close()
                al = allocator(self.ctx)
                view = lambda a, z, pat, **kw: [t[:, a:z].rearrange(pat, **kw) for t in (OP_hi, OP_lo)]
                XT_hi, XT_lo = view(0, KT * SEQ, "p (k n) -> p k n", k=KT)
                QA_hi, QA_lo = view(2 * SEQ, 4 * SEQ, "p (s n) -> p s n", s=2)
                KC_hi, KC_lo = view(4 * SEQ, 8 * SEQ, "p (s v n) -> p s v n", s=2, v=2)
                tabs = al("b_tabs", [P, 3, SEQ])
                CT = al("b_CT", [P, 2, TPB, RANK])
                kk = al("b_kk", [P, 2, SEQ])
                kt_ = al("b_kt", [P, SEQ])
                qt = al("b_qt", [P, 2, SEQ])
                qr = al("b_qr", [P, 2, SEQ])
                Q_hi, Q_lo = (al(f"b_{n}", [P, 2, SEQ], F32R) for n in ("Qh", "Ql"))
                PT = al("b_PT", [P, 4, TPB, SEQ])
                U_hi, U_lo = (al(f"b_{n}", [P, 2, SEQ], F32R) for n in ("Uh", "Ul"))
                core = Core(al, "b", split=False, ring=2)
                per_b = HEADS
                pairs, units = BATCH * HEADS // 2, BATCH * HEADS
                s_done, av_done, u_ready, o_done = {}, {}, {}, {}
                q_ready, sw_ready, sw_read, x_added = {}, {}, {}, {}
                xt_ready, qa_ready, kc_ready, ct_ready, kk_read, xt_read = {}, {}, {}, {}, {}, {}

                dma_tabs = sem("dma_b_tabs")
                sp.dma(tabs[:, :, :], rope_tab, dma_tabs)
                dve.wait((dma_tabs, 16))
                load_mix(1)
                inverse_std(0, NT)
                for s in (pe, dve, act, pool):
                    s.wait(self.w_ready, self.n_ready, self.wc_ready)

                def latent_norm(b):
                    xn_ready = normalise_four(range(4 * b, 4 * b + 4))
                    for f in range(KT):
                        k = core.take()
                        m = transpose_half(f, k, xn_ready)
                        xt_ready[b] = split_from(bank[k][:, :], XT_hi[:, f, :], XT_lo[:, f, :], m,
                                                 before(xt_read, b - 1))
                        core.give(k, xt_ready[b])

                def latent_project(b, j):
                    k = core.take()
                    pe.wait(xt_ready[b])
                    for kt in range(KT):
                        step = three_pass(pe, bank[k][:, :], Wc_hi[:, kt, j, :], Wc_lo[:, kt, j, :],
                                          XT_hi[:, kt, :], XT_lo[:, kt, :], kt == 0, kt == KT - 1)
                        if kt < KT - 1:
                            pe.do(step)
                    m = pe.counted(step)
                    xt_read[b] = (m,)
                    if j == 0:
                        m = split_from(bank[k][:, :], QA_hi[:, b % 2, :], QA_lo[:, b % 2, :], m,
                                       before(s_done, per_b * (b - 1) - 1))
                        qa_ready[b] = m
                    else:
                        dve.wait(m, *before(kk_read, b - 1))
                        dst = kt_[:, :] if j == 3 else kk[:, j - 1, :]
                        m = dve.counted(lambda e: e.tensor_tensor(dst, bank[k][:, :], tabs[:, j - 1, :],
                                                                  ALU.mult))
                    core.give(k, m)
                    return m

                def latent_keys(b, v, ready):
                    rows = slice(64, 128) if v == 0 else slice(0, 64)
                    dve.wait(ready)
                    m = dve.counted(lambda e: e.tensor_tensor(kk[rows, v, :], kk[rows, v, :],
                                                              kt_[rows, :], ALU.add))
                    act.wait(m, *before(s_done, per_b * (b - 1) - 1))
                    m = act.counted(lambda e: e.activation(KC_hi[:, b % 2, v, :], kk[:, v, :], ACT.Copy))
                    dve.wait(m)
                    return dve.counted(lambda e: e.tensor_tensor(
                        KC_lo[:, b % 2, v, :], kk[:, v, :], KC_hi[:, b % 2, v, :].bitcast(F32),
                        ALU.subtract))

                def latent_values(b):
                    k = core.take()
                    pe.wait(kc_ready[b])
                    for t in range(TPB):
                        step = (lambda e, t=t: e.transpose(bank[k][:, t * RANK:(t + 1) * RANK],
                                                           kk[0:64, 0, t * P:(t + 1) * P],
                                                           ident_f[0:64, 0:64]))
                        if t < TPB - 1:
                            pe.do(step)
                    m = pe.counted(step)
                    kk_read[b] = (m, kc_ready[b])
                    act.wait(m, *before(av_done, per_b * (b - 1) - 1))
                    m = act.counted(lambda e: e.activation(
                        CT[:, b % 2, :, :],
                        bank[k][:, 0:TPB * RANK].rearrange("p (t c) -> p t c", c=RANK), ACT.Copy))
                    ct_ready[b] = m
                    core.give(k, m)

                def latent(b, part):
                    if part == 0:
                        latent_norm(b)
                    elif part == 1:
                        latent_project(b, 0)
                        latent_project(b, 3)
                    elif part == 2:
                        kk_ready[b] = [latent_project(b, 1), latent_project(b, 2)]
                    elif part == 3:
                        latent_keys(b, 0, kk_ready[b][0])
                        kc_ready[b] = latent_keys(b, 1, kk_ready[b][1])
                    else:
                        latent_values(b)

                kk_ready = {}

                def two_pass(out, w, b):
                    pe.do(lambda e: e.matmul(out, w, QA_hi[:, b % 2, :], start=True, stop=False))
                    return pe.counted(lambda e: e.matmul(out, w, QA_lo[:, b % 2, :], start=False, stop=True))

                def swapped(p):
                    b, hp = p // 8, p % 8
                    k = core.take()
                    pe.wait(qa_ready[b])
                    m = two_pass(bank[k][:, :], Wsw[:, hp, :], b)

                    def finish():
                        dve.wait(m, *before(sw_read, p - 2))
                        sw_ready[p] = dve.counted(lambda e: e.tensor_tensor(
                            qt[:, p % 2, :], bank[k][:, :], tabs[:, 2, :], ALU.mult))
                        core.give(k, sw_ready[p])
                    core.after(1, finish)

                def query(n):
                    p, par = n // 2, n % 2
                    b, h = p // 8, 2 * (p % 8) + par
                    q = n % 2
                    k = core.take()
                    pe.wait(qa_ready[b])
                    m = two_pass(bank[k][:, :], Wq[:, h, :], b)
                    rows = slice(64, 128) if par == 0 else slice(0, 64)

                    def rotate():
                        dve.wait(m, *before(q_ready, n - 2))
                        cos_part = dve.counted(lambda e: e.tensor_tensor(
                            qr[:, q, :], bank[k][:, :], tabs[:, par, :], ALU.mult))
                        core.give(k, cos_part)
                        pool.wait(cos_part, sw_ready[p], pool.last())
                        summed = pool.counted(lambda e: e.tensor_tensor(
                            qr[rows, q, :], qr[rows, q, :], qt[rows, p % 2, :], ALU.add))
                        sw_read[p] = (summed,)
                        core.after(1, lambda: high(summed))

                    def high(summed):
                        act.wait(summed, *before(s_done, n - 2))
                        hi = act.counted(lambda e: e.activation(Q_hi[:, q, :], qr[:, q, :], ACT.Copy))
                        core.after(1, lambda: low(hi))

                    def low(hi):
                        dve.wait(hi)
                        q_ready[n] = (dve.counted(lambda e: e.tensor_tensor(
                            Q_lo[:, q, :], qr[:, q, :], Q_hi[:, q, :].bitcast(F32), ALU.subtract)),)
                    core.after(1, rotate)

                def scores(n, i):
                    b, par, q = n // per_b, n % 2, n % 2
                    m = core.scores(n, i, Q_hi[:, q, :], Q_lo[:, q, :], KC_hi[:, b % 2, par, :],
                                    KC_lo[:, b % 2, par, :], [*q_ready[n], kc_ready[b]])
                    s_done[n] = (m,)
                    return core.pending

                def values(p):
                    b = p // 8
                    k = core.take()
                    pe.wait(ct_ready[b])
                    for n in (2 * p, 2 * p + 1):
                        for i in range(TPB):
                            pe.wait(core.pt[n, i])
                    for j in range(TPB):
                        for par in range(2):
                            qs = slice(P * j, SEQ)
                            step = (lambda e, j=j, par=par, qs=qs: e.matmul(
                                bank[k][64 * par:64 * par + 64, qs], CT[:, b % 2, j, :],
                                PT[:, (2 * p + par) % 4, j, qs], start=(j == 0), stop=(j == TPB - 1)))
                            if j < TPB - 1 or par == 0:
                                pe.do(step)
                    m = pe.counted(step)
                    av_done[2 * p] = av_done[2 * p + 1] = (m,)
                    lo_step = split_from(bank[k][:, :], U_hi[:, p % 2, :], U_lo[:, p % 2, :], m,
                                         before(o_done, p - 2), later=True)

                    def finish():
                        u_ready[p] = lo_step()
                        core.give(k, u_ready[p])
                    core.after(1, finish)

                def output(p, half):
                    b, hp = p // 8, p % 8
                    k = core.take()
                    pe.wait(u_ready[p])
                    for tt in range(2):
                        cols = slice((2 * half + tt) * P, (2 * half + tt + 1) * P)
                        step = three_pass(pe, bank[k][:, tt * DM:(tt + 1) * DM], U_hi[:, p % 2, cols],
                                          U_lo[:, p % 2, cols], N_hi[:, hp, :], N_lo[:, hp, :], True, True)
                        if tt == 0:
                            pe.do(step)
                    m = pe.counted(step)
                    if half == 1:
                        o_done[p] = (m,)
                    t0 = 4 * b + 2 * half

                    def finish():
                        dve.wait(m, *x_added.get(t0, ()))
                        done = dve.counted(lambda e: e.tensor_tensor(
                            X[:, t0:t0 + 2, :], X[:, t0:t0 + 2, :],
                            bank[k][:, :].rearrange("p (t d) -> p t d", t=2), ALU.add))
                        x_added[t0] = (done,)
                        core.give(k, done)
                        if hp == 7:
                            tile_stats((t0, t0 + 1), done)
                    core.after(1, finish)

                pool_todo = []
                for part in range(5):
                    latent(0, part)
                swapped(0)
                query(0)
                for _ in range(3):
                    core.flush()
                for n in range(units + 5):
                    b, j = n // per_b, n % per_b
                    if b + 1 < BATCH and j in (6, 7, 8, 9, 10):
                        latent(b + 1, j - 6)
                    if n == units - 4:
                        mix_ready = prepare_mix(1, core.take, core.give)
                    if n == units:
                        w_mix = split_mix(mix_ready, s_done[units - 1][0])
                    for i in range(TPB):
                        if 1 <= n <= units:
                            core.transposes(n - 1, i, PT[:, (n - 1) % 4, :, :], before(av_done, n - 5))
                        core.flush()
                        pend = scores(n, i) if n < units else None
                        if pool_todo:
                            core.normalise(pool_todo.pop())
                        if pend:
                            pool_todo.append(pend)
                        if i == 0 and n + 1 < units:
                            if (n + 1) % 2 == 0:
                                swapped((n + 1) // 2)
                            query(n + 1)
                        if i == 2 and n % 2 == 1 and 3 <= n and (n - 3) // 2 < pairs:
                            values((n - 3) // 2)
                        if i == 3 and n >= 4 and (n - 4) // 2 < pairs:
                            output((n - 4) // 2, n % 2)
                barrier()
                self.ctx.close()
                return w_mix

        w_mix = attention_a()
        attention_b = LatentAttention()
        mixture("m1", w_mix, last=False, between=attention_b.prepare)
        w_mix = attention_b.run()
        mixture("m2", w_mix, last=True)
        sp.wait((dma_out, 16 * NT))

        block = top.enter_context(nc.Block())

        @block.sync
        def _(e):
            sp.play(e)

        @block.tensor
        def _(e):
            pe.play(e)

        @block.scalar
        def _(e):
            act.play(e)

        @block.vector
        def _(e):
            dve.play(e)

        @block.gpsimd
        def _(e):
            pool.play(e)


def kernel(**inputs):
    from concourse import bacc
    from concourse.bass_utils import run_bass_kernel_spmd

    f = {n.removeprefix("L0_"): np.asarray(a) for n, a in inputs.items()}

    def rows(a):
        return a.reshape(-1, P, a.shape[-1]).transpose(1, 0, 2)

    def group(w):
        return w.reshape(NG, GH, KT, P, DH).transpose(0, 3, 2, 1, 4).reshape(NG, P, KT * GH * DH)

    wo = f["attn_a_W_O"].reshape(NG, GH, DH, DM).transpose(0, 2, 1, 3).reshape(NG, P, GH * DM)
    swap = np.arange(ROPE) ^ 1
    wqb = f["attn_b_Wqb"].reshape(RANK, HEADS, NOPE + ROPE)
    wkvb = f["attn_b_Wkvb"].reshape(RANK, HEADS, 2 * NOPE)
    pe_sw = wqb[:, :, NOPE:][:, :, swap].reshape(RANK, HEADS // 2, 2, ROPE)
    wkva = rows(f["attn_b_Wkva"])
    c_, pe_ = wkva[:, :, :RANK], wkva[:, :, RANK:]
    wqa = rows(f["attn_b_Wqa"])
    router = np.zeros((MIX_DV, 2, MIX_H), f["ffn_router_w"].dtype)
    for h in range(MIX_H):
        router[h * MIX_HDV:(h + 1) * MIX_HDV, :, h] = f["ffn_router_w"][h]

    theta = (np.float32(10000.0) ** (-2.0 * np.arange(ROPE // 2, dtype=np.float32) / ROPE)).astype(np.float32)
    angle = np.repeat(theta, 2)[:, None] * np.arange(SEQ, dtype=np.float32)[None, :]
    cos, sin = np.cos(angle), np.sin(angle)
    sin[0::2] *= -1
    one = np.ones_like(cos)
    rope_tab = np.stack([np.concatenate([one, cos]), np.concatenate([cos, one]),
                         np.concatenate([sin, sin])], axis=1).astype(np.float32)
    inv = (1.0 / np.float32(10000.0) ** (np.arange(0, MIX_HDK, 2, dtype=np.float32) / MIX_HDK)).astype(np.float32)
    fr = np.arange(1, BATCH, dtype=np.float32)[:, None] * inv[None, :]
    rot_tab = np.stack([np.concatenate([np.cos(fr), np.cos(fr)], 1),
                        np.concatenate([np.sin(fr), -np.sin(fr)], 1)], axis=1).astype(np.float32)
    wqb_pe = np.zeros((RANK, HEADS, P), wqb.dtype)
    wqb_pe[:, 0::2, 64:] = wqb[:, 0::2, NOPE:]
    wqb_pe[:, 1::2, :64] = wqb[:, 1::2, NOPE:]
    arrays = {
        "x": f["attn_a_x"].reshape(TOK, DM),
        "wa": np.concatenate([group(f["attn_a_W_Q"]), group(f["attn_a_W_K"]), group(f["attn_a_W_V"]), wo], 2),
        "ba": np.stack([f["attn_a_b_Q"].T, f["attn_a_b_K"].T, f["attn_a_b_V"].T], axis=1),
        "bo": f["attn_a_b_O"].reshape(1, DM),
        "ident": np.eye(P, dtype=np.float32),
        "mask_tri": np.triu(np.full((P, P), MASKED, np.float32), 1),
        "wqa": np.concatenate([wqa, wqa], 2),
        "wqb_t": wqb[:, :, :NOPE].transpose(2, 1, 0),
        "wqb_pe": wqb_pe,
        "wqb_sw": pe_sw[:, :, ::-1, :].reshape(RANK, HEADS // 2, P),
        "wkva": np.concatenate([c_, pe_, pe_, c_, pe_[:, :, swap], pe_[:, :, swap]], 2),
        "wkvbk_t": wkvb[:, :, :NOPE].transpose(2, 1, 0),
        "wkvbv_t": wkvb[:, :, NOPE:].transpose(2, 1, 0),
        "wout_b": f["attn_b_Wout"].reshape(HEADS, NOPE, DM).transpose(1, 0, 2),
        "rope_tab": rope_tab,
        "conv_w": rows(f["ffn_conv_w"]),
        "wmix": np.concatenate([rows(f[f"ffn_{n}"]) for n in ("Wq", "Wg", "Wk", "Wv")], 2),
        "wv_t": rows(f["ffn_Wv"].T),
        "router": rows(router.reshape(MIX_DV, 2 * MIX_H)),
        "wmix_out": rows(f["ffn_Wout"]),
        "rot_tab": np.broadcast_to(rot_tab[None], (P, *rot_tab.shape)),
    }
    arrays = {n: np.ascontiguousarray(a) for n, a in arrays.items()}
    nc = bacc.Bacc("TRN2", target_bir_lowering=False, num_devices=1)
    args = [nc.dram_tensor(n, a.shape, mybir.dt.from_np(a.dtype), kind="ExternalInput").ap()
            for n, a in arrays.items()]
    out = nc.dram_tensor("out", [TOK, DM], F32, kind="ExternalOutput").ap()
    hybrid_program(nc, *args, out)
    result = run_bass_kernel_spmd(nc, [arrays], core_ids=[0])
    return result.results[0]["out"].reshape(BATCH, SEQ, DM)
```

```python
from contextlib import ExitStack

import numpy as np
import concourse.bass as bass
from concourse import mybir

F32 = mybir.dt.float32
F32R = mybir.dt.float32r
BF16 = mybir.dt.bfloat16
ALU = mybir.AluOpType
ACT = mybir.ActivationFunctionType
AX = mybir.AxisListType

P = 128
BATCH, SEQ, DM = 4, 512, 256
TOK = BATCH * SEQ
NT = TOK // P
TPB = SEQ // P
KT = DM // P
HEADS = 16
DH = 128
GH = 2
NG = HEADS // GH
GW = GH * DH
ROPE = 64
RANK = 64
NOPE = 128
MIX_DK, MIX_DV, MIX_H = 128, 256, 16
MIX_HDK, MIX_HDV = MIX_DK // MIX_H, MIX_DV // MIX_H
EPS = 1e-5
MASKED = -1.0e30
SCALE_A = float(DH) ** -0.5
SCALE_B = float(NOPE + ROPE) ** -0.5
MIX_LOGIT = MIX_DK + MIX_DV
MIX_K = MIX_LOGIT + 2 * MIX_H
MIX_V = MIX_K + BATCH * MIX_DK
MIX_COLS = MIX_V + MIX_DV
MIX_WORDS = KT * MIX_COLS + KT * DM
MIX_ORDER_1 = (
    ("norm", 0), ("conv0", 0), ("conv1", 0), ("norm", 1), ("gates", 0), ("conv0", 1), ("kv0", 0),
    ("qk0", 0), ("conv1", 1), ("between", 0), ("kv1", 0), ("qk1", 0), ("route", 0), ("kv2", 0), ("kv3", 0),
    ("qk3", 0), ("qk2", 0), ("sums", 0), ("gates", 1), ("norm", 2), ("coef", 0), ("route", 1), ("kv0", 1),
    ("products", 0), ("conv0", 2), ("conv1", 2), ("kv1", 1), ("qk0", 1), ("kv2", 1), ("qk1", 1), ("kv3", 1),
    ("total", 0), ("norm", 3), ("qk2", 1), ("qk3", 1), ("variance", 0), ("sums", 1), ("gates", 2),
    ("scale", 0), ("coef", 1), ("conv0", 3), ("kv0", 2), ("qk0", 2), ("products", 1), ("turn", 0),
    ("kv1", 2), ("conv1", 3), ("kv2", 2), ("qk1", 2), ("total", 1), ("qk2", 2), ("kv3", 2), ("route", 2),
    ("qk3", 2), ("sums", 2), ("between", 1), ("gates", 3), ("variance", 1), ("coef", 2), ("kv0", 3),
    ("qk0", 3), ("scale", 1), ("products", 2), ("out", 0), ("kv1", 3), ("qk1", 3), ("turn", 1), ("kv2", 3),
    ("kv3", 3), ("total", 2), ("qk3", 3), ("qk2", 3), ("route", 3), ("sums", 3), ("between", 2),
    ("variance", 2), ("coef", 3), ("scale", 2), ("out", 1), ("products", 3), ("turn", 2), ("total", 3),
    ("variance", 3), ("scale", 3), ("out", 2), ("between", 3), ("turn", 3), ("out", 3),
)
MIX_ORDER_2 = (
    ("norm", 0), ("conv0", 0), ("conv1", 0), ("norm", 1), ("gates", 0), ("conv0", 1), ("kv0", 0),
    ("conv1", 1), ("kv1", 0), ("qk0", 0), ("route", 0), ("kv2", 0), ("kv3", 0), ("norm", 2), ("qk1", 0),
    ("qk3", 0), ("qk2", 0), ("gates", 1), ("sums", 0), ("coef", 0), ("products", 0), ("conv0", 2),
    ("total", 0), ("conv1", 2), ("kv0", 1), ("kv1", 1), ("qk0", 1), ("variance", 0), ("kv2", 1), ("kv3", 1),
    ("qk1", 1), ("norm", 3), ("scale", 0), ("qk2", 1), ("qk3", 1), ("route", 1), ("sums", 1), ("coef", 1),
    ("products", 1), ("turn", 0), ("gates", 2), ("total", 1), ("kv0", 2), ("qk0", 2), ("kv1", 2),
    ("conv0", 3), ("kv2", 2), ("conv1", 3), ("qk1", 2), ("route", 2), ("kv3", 2), ("variance", 1),
    ("qk3", 2), ("out", 0), ("qk2", 2), ("gates", 3), ("scale", 1), ("sums", 2), ("coef", 2),
    ("products", 2), ("turn", 1), ("kv0", 3), ("kv1", 3), ("qk0", 3), ("kv2", 3), ("total", 2),
    ("route", 3), ("variance", 2), ("qk1", 3), ("out", 1), ("scale", 2), ("qk2", 3), ("kv3", 3), ("qk3", 3),
    ("sums", 3), ("coef", 3), ("products", 3), ("turn", 2), ("total", 3), ("variance", 3), ("scale", 3),
    ("out", 2), ("turn", 3), ("out", 3),
)
PAIRS = BATCH * (BATCH + 1) // 2
NORM_A_ACT, RING_A, LAG_A, ORD_A, PA0, PA1, PAV, VAT_A, OAT_A = (), 2, 6, False, 0, 0, 3, 13, 19
LAG, ORD, VAT, OAT, EVAC_ACT, NORM_ACT, QUERY_AT = 6, False, 15, 22, (0, 1, 2, 3), (0,), 1


class Stream:

    def __init__(self, sem):
        self.sem, self.count, self.steps, self.passed = sem, 0, [], {}

    def wait(self, *marks):
        for sem, value in marks:
            if self.passed.get(id(sem), 0) < value:
                self.passed[id(sem)] = value
                self.steps.append(lambda e, s=sem, v=value: e.wait_ge(s, v))

    def do(self, step):
        self.steps.append(step)

    def counted(self, step):
        self.steps.append(lambda e: step(e).then_inc(self.sem, 1))
        self.count += 1
        return (self.sem, self.count)

    def last(self):
        return (self.sem, self.count)

    def dma(self, out, in_, sem):
        self.steps.append(lambda e: e.dma_start(out, in_).then_inc(sem, 16))

    def play(self, engine):
        for step in self.steps:
            step(engine)


def before(marks, n, *rest):
    return marks[(n, *rest) if rest else n] if n >= 0 else ()


def three_pass(pe, out, w_hi, w_lo, x_hi, x_lo, start, stop, skip=False):
    pe.do(lambda e: e.matmul(out, w_hi, x_hi, start=start, stop=False, skip_group_check=skip))
    pe.do(lambda e: e.matmul(out, w_hi, x_lo, start=False, stop=False, skip_group_check=skip))
    return lambda e: e.matmul(out, w_lo, x_hi, start=False, stop=stop, skip_group_check=skip)


def hybrid_program(nc, x, wa, ba, bo, ident, mask_tri, wqa, wqb_t, wqb_pe, wqb_sw, wkva, wkvbk_t, wkvbv_t,
                   wout_b, rope_tab, conv_w, wmix, wv_t, router, wmix_out, rot_tab, out):
    top = ExitStack()
    with top:
        def sem(name):
            return top.enter_context(nc.semaphore(name))

        def allocator(stack):
            return lambda name, shape, dt=F32: stack.enter_context(nc.sbuf_tensor(name, shape, dt))

        keep = allocator(top)
        pe, act, dve, pool, sp = (Stream(sem(n)) for n in
                                  ("pe_steps", "act_steps", "dve_steps", "pool_steps", "sp_steps"))
        engines = (pe, act, dve, pool)
        bank = [top.enter_context(nc.psum_tensor(f"bank{i}", [P, 512], F32)) for i in range(8)]

        X = keep("X", [P, NT, DM])
        OP_hi = keep("OP_hi", [P, KT * TOK], F32R)
        OP_lo = keep("OP_lo", [P, KT * TOK], F32R)
        ident_f = keep("ident_f", [P, P])
        mask = keep("mask", [P, SEQ])
        stats = keep("stats", [P, NT, 6])
        moments = keep("moments", [P, NT, 2])
        std = keep("std", [P, NT])
        rstd = keep("rstd", [P, NT])
        xn = keep("xn", [P, 4, DM])
        raw = keep("raw", [P, MIX_WORDS])
        wv_t_sb = keep("wv_t_sb", [P, KT, DM])
        router_sb = keep("router_sb", [P, KT, 2 * MIX_H])
        conv_sb = keep("conv_sb", [P, KT, 2])
        rot_sb = keep("rot_sb", [P, BATCH - 1, 2, MIX_HDK])
        k_tmp = keep("k_tmp", [P, KT, MIX_DK])
        v_mean = keep("v_mean", [P, KT, MIX_H])

        dma_x = [sem(f"dma_x{b}") for b in range(BATCH)]
        dma_const = sem("dma_const")
        dma_small = sem("dma_small")
        dma_mix = [sem("dma_mix0"), sem("dma_mix1")]
        dma_out = sem("dma_out")

        x_tiles = x.rearrange("(t p) d -> p t d", p=P)
        out_tiles = out.rearrange("(t p) d -> p t d", p=P)

        def load_x(b):
            sp.dma(X[:, 4 * b:4 * b + 4, :], x_tiles[:, 4 * b:4 * b + 4, :], dma_x[b])

        def barrier():
            marks = [s.last() for s in engines if s.count]
            for s in (*engines, sp):
                s.wait(*marks)

        def tile_stats(tiles, *ready):
            dve.wait(*ready)
            for t in tiles:
                m = dve.counted(lambda e, t=t: e.bn_stats(stats[:, t, :], X[:, t, :]))
            dve.wait(m)
            for t in tiles:
                m = dve.counted(lambda e, t=t: e.bn_aggr(moments[:, t, :], stats[:, t, :]))
            return m

        def inverse_std(a, z):
            dve.wait(dve.last())
            m = dve.counted(lambda e: e.tensor_scalar(std[:, a:z], moments[:, a:z, 1], EPS, None, ALU.add))
            act.wait(m)
            m = act.counted(lambda e: e.activation(std[:, a:z], std[:, a:z], ACT.Sqrt))
            dve.wait(m)
            m = dve.counted(lambda e: e.reciprocal(rstd[:, a:z], std[:, a:z]))
            dve.wait(m)

        xn_read = [()]

        def normalise_four(tiles):
            dve.wait(*xn_read[0])
            for k, t in enumerate(tiles):
                m = dve.counted(lambda e, k=k, t=t: e.tensor_scalar(
                    xn[:, k, :], X[:, t, :], moments[:, t, 0:1], rstd[:, t:t + 1],
                    ALU.subtract, ALU.mult))
            return m

        def transpose_half(f, k, ready, *free):
            pe.wait(ready, *free)
            for j in range(4):
                step = (lambda e, j=j: e.transpose(bank[k][:, j * P:(j + 1) * P],
                                                   xn[:, j, f * P:(f + 1) * P], ident_f[:, :]))
                if j < 3:
                    pe.do(step)
            m = pe.counted(step)
            xn_read[0] = (m,)
            return m

        def split_from(psum_ap, hi, lo, ready, free=(), bias=None, later=None):
            act.wait(ready, *free)
            if bias is None:
                m = act.counted(lambda e: e.activation(hi, psum_ap, ACT.Copy))
            else:
                m = act.counted(lambda e: e.activation(hi, psum_ap, ACT.Identity, bias=bias))

            def remainder():
                dve.wait(m)
                if bias is None:
                    return dve.counted(lambda e: e.tensor_tensor(lo, psum_ap, hi.bitcast(F32),
                                                                 ALU.subtract))
                return dve.counted(lambda e: e.scalar_tensor_tensor(
                    out=lo, in0=psum_ap, scalar=bias, in1=hi.bitcast(F32), op0=ALU.add,
                    op1=ALU.subtract))

            return remainder if later else remainder()

        def mix_cols(t, a, z):
            return t[:, 0:KT * MIX_COLS].rearrange("p (k n) -> p k n", k=KT)[:, :, a:z]

        def mix_out_w(t):
            return t[:, KT * MIX_COLS:MIX_WORDS].rearrange("p (k n) -> p k n", k=KT)

        def load_mix(which, *free):
            sp.wait(*free)
            sp.dma(mix_cols(raw, 0, MIX_LOGIT), wmix[:, :, 0:MIX_LOGIT], dma_mix[which])
            sp.dma(mix_cols(raw, MIX_K, MIX_K + MIX_DK), wmix[:, :, MIX_LOGIT:MIX_LOGIT + MIX_DK],
                   dma_mix[which])
            sp.dma(mix_cols(raw, MIX_V, MIX_COLS), wmix[:, :, MIX_LOGIT + MIX_DK:], dma_mix[which])
            sp.dma(mix_out_w(raw), wmix_out, dma_mix[which])

        def prepare_mix(which, take, give):
            loaded = ((dma_mix[which], 64), (dma_small, 64))
            k = take()
            pe.wait(*loaded)
            for f in range(KT):
                for kt in range(KT):
                    step = (lambda e, f=f, kt=kt: e.matmul(
                        bank[k][:, f * 32:(f + 1) * 32], wv_t_sb[:, kt, f * P:(f + 1) * P],
                        router_sb[:, kt, :], start=(kt == 0), stop=(kt == KT - 1)))
                    if f < KT - 1 or kt < KT - 1:
                        pe.do(step)
            m = pe.counted(step)
            act.wait(m, *loaded)
            m_logit = act.counted(lambda e: e.activation(
                mix_cols(raw, MIX_LOGIT, MIX_K),
                bank[k][:, 0:KT * 32].rearrange("p (f n) -> p f n", f=KT), ACT.Copy))
            give(k, m_logit)
            dve.wait(*loaded)
            vh = mix_cols(raw, MIX_V, MIX_COLS).rearrange("p k (h d) -> p k h d", d=MIX_HDV)
            m_v = dve.counted(lambda e: e.tensor_reduce(v_mean[:, :, :], vh, AX.X, ALU.add))
            dve.wait(m_v)
            m_v = dve.counted(lambda e: e.tensor_scalar(v_mean[:, :, :], v_mean[:, :, :], 1.0 / MIX_HDV,
                                                        None, ALU.mult))
            dve.wait(m_v)
            for kt in range(KT):
                m_v = dve.counted(lambda e, kt=kt: e.tensor_tensor(
                    vh[:, kt], vh[:, kt],
                    v_mean[:, kt, :].unsqueeze(2).to_broadcast([P, MIX_H, MIX_HDV]), ALU.subtract))
            return (m_v, m_logit, *loaded)

        def turn_keys(which, d):
            pool.wait((dma_mix[which], 64), (dma_small, 64), pool.last())
            heads = lambda ap: ap.rearrange("p k (h f) -> p k h f", f=MIX_HDK)
            k0 = heads(mix_cols(raw, MIX_K, MIX_K + MIX_DK))
            half = MIX_HDK // 2
            kd = heads(mix_cols(raw, MIX_K + d * MIX_DK, MIX_K + (d + 1) * MIX_DK))

            def table(j, a, z):
                return rot_sb[:, d - 1, j, a:z].unsqueeze(1).to_broadcast([P, MIX_H, z - a])

            for kt in range(KT):
                for a in range(2):
                    o, i = slice(a * half, (a + 1) * half), slice((1 - a) * half, (2 - a) * half)
                    pool.do(lambda e, o=o, i=i, kt=kt: e.tensor_tensor(
                        kd[:, kt, :, o], k0[:, kt, :, i], table(1, o.start, o.stop), ALU.mult))
                m = pool.counted(lambda e, kt=kt: e.tensor_tensor(
                    heads(k_tmp[:, :, :])[:, kt], k0[:, kt], table(0, 0, MIX_HDK), ALU.mult))
            pool.wait(m)
            return pool.counted(lambda e: e.tensor_tensor(kd, kd, heads(k_tmp[:, :, :]), ALU.add))

        def split_mix(ready, *free):
            act.wait(*ready, *free)
            m = act.counted(lambda e: e.activation(OP_hi[:, 0:MIX_WORDS], raw[:, :], ACT.Copy))
            pool.wait(m, pool.last(), *ready)
            return pool.counted(lambda e: e.tensor_tensor(
                OP_lo[:, 0:MIX_WORDS], raw[:, :], OP_hi[:, 0:MIX_WORDS].bitcast(F32), ALU.subtract))

        class Core:

            def __init__(self, al, tag, split, ring):
                self.split, self.ring = split, ring
                self.negmax = al(f"{tag}_negmax", [P, 8, TPB])
                self.rowsum = al(f"{tag}_rowsum", [P, 8, TPB])
                self.rinv = al(f"{tag}_rinv", [P, 8, TPB])
                self.probs = al(f"{tag}_probs", [P, ring, TPB, SEQ])
                self.s_banks, self.t_banks, self.acc_banks = (0, 1, 2), (3, 4), (5, 6, 7)
                self.free = {k: () for k in range(8)}
                self.n_s = self.n_t = self.n_acc = 0
                self.norm, self.transposed, self.pt = {}, {}, {}
                self.substep, self.due = 0, []

            def after(self, delay, step):
                self.due.append((self.substep + delay, step))

            def flush(self):
                self.substep += 1
                now = [f for t, f in self.due if t <= self.substep]
                self.due = [(t, f) for t, f in self.due if t > self.substep]
                for step in now:
                    step()

            def take(self):
                k = self.acc_banks[self.n_acc % 3]
                self.n_acc += 1
                pe.wait(*self.free[k])
                return k

            def give(self, k, mark):
                self.free[k] = (mark,)

            def scores(self, n, i, q_hi, q_lo, k_hi, k_lo, ready):
                k = self.s_banks[self.n_s % 3]
                self.n_s += 1
                cols = P * (i + 1)
                s_ap = bank[k][:, 0:cols]
                slot = n % 8
                pe.wait(*ready, *self.free[k])
                qs = slice(P * i, P * i + P)
                done = pe.counted(three_pass(pe, s_ap, q_hi[:, qs], q_lo[:, qs], k_hi[:, 0:cols],
                                             k_lo[:, 0:cols], True, True))
                nm = self.negmax[:, slot, i:i + 1]
                rs = self.rowsum[:, slot, i:i + 1]
                ri = self.rinv[:, slot, i:i + 1]
                pr = self.probs[:, n % self.ring, i, 0:cols]
                dve.wait(done)
                m = dve.counted(lambda e: e.tensor_tensor_reduce(
                    s_ap, s_ap, mask[:, SEQ - cols:SEQ], -1.0, 3.0e38, ALU.add, ALU.min, nm))
                act.wait(m, *before(self.transposed, n - self.ring, i))
                m = act.counted(lambda e: e.activation(pr, s_ap, ACT.Exp, bias=nm, scale=-1.0,
                                                       accum_out=rs))
                self.free[k] = (m,)
                self.pending = (n, i, m, ri, rs, pr, cols)
                return done

            def normalise(self, pending):
                n, i, m, ri, rs, pr, cols = pending
                dve.wait(m)
                m = dve.counted(lambda e: e.reciprocal(ri, rs))
                if i in (NORM_A_ACT if self.split else NORM_ACT):
                    act.wait(m)
                    self.norm[n, i] = act.counted(lambda e: e.activation(pr, pr, ACT.Copy, scale=ri))
                    return
                pool.wait(m, pool.last())
                self.norm[n, i] = pool.counted(
                    lambda e: e.tensor_tensor(pr, pr, ri.to_broadcast([P, cols]), ALU.mult))

            def transposes(self, n, i, dst, free):
                k = self.t_banks[self.n_t % 2]
                self.n_t += 1
                pe.wait(self.norm[n, i], *self.free[k])
                for j in range(i + 1):
                    step = (lambda e, j=j: e.transpose(bank[k][:, P * j:P * j + P],
                                                       self.probs[:, n % self.ring, i, P * j:P * j + P], ident_f[:, :]))
                    if j < i:
                        pe.do(step)
                done = pe.counted(step)
                self.transposed[n, i] = (done,)
                src = bank[k][:, 0:P * (i + 1)].rearrange("p (j q) -> p j q", q=P)
                qs = slice(P * i, P * i + P)
                if self.split:
                    hi, lo = dst
                    lo_step = split_from(src, hi[:, 0:i + 1, qs], lo[:, 0:i + 1, qs], done, free,
                                         later=True)

                    def finish():
                        self.pt[n, i] = lo_step()
                        self.free[k] = (self.pt[n, i],)
                    return finish
                elif i in EVAC_ACT:
                    act.wait(done, *free)
                    m = act.counted(lambda e: e.activation(dst[:, 0:i + 1, qs], src, ACT.Copy))
                else:
                    dve.wait(done, *free)
                    m = dve.counted(lambda e: e.tensor_copy(dst[:, 0:i + 1, qs], src))
                self.free[k] = (m,)
                self.pt[n, i] = m
                return lambda: None

        def attention_a():
            ctx = ExitStack()
            al = allocator(ctx)
            GWORDS = 2048
            XT_hi, XT_lo = (t[:, :].rearrange("p (k n) -> p k n", k=KT) for t in (OP_hi, OP_lo))
            W_hi = al("a_W_hi", [P, 2, GWORDS], F32R)
            W_lo = al("a_W_lo", [P, 2, GWORDS], F32R)
            bias = al("a_bias", [P, 3, HEADS])
            bo_bc = al("a_bo", [P, DM])
            Q_hi, Q_lo, K_hi, K_lo = (al(f"a_{n}", [P, 2, SEQ], F32R) for n in ("Qh", "Ql", "Kh", "Kl"))
            V_hi, V_lo = (al(f"a_{n}", [P, 2, TPB, GW], F32R) for n in ("Vh", "Vl"))
            PT_hi, PT_lo = (al(f"a_{n}", [P, 2, TPB, SEQ], F32R) for n in ("PTh", "PTl"))
            Z_hi, Z_lo = (al(f"a_{n}", [P, 2, GH, SEQ], F32R) for n in ("Zh", "Zl"))
            core = Core(al, "a", split=True, ring=RING_A)
            dma_w = [sem(f"dma_wa{g}") for g in range(NG)]
            dma_b = sem("dma_ba")

            def wq(t, s): return t[:, s, 0:512].rearrange("p (k h e) -> p k h e", k=KT, h=GH)
            def wk(t, s): return t[:, s, 512:1024].rearrange("p (k h e) -> p k h e", k=KT, h=GH)
            def wv(t, s): return t[:, s, 1024:1536].rearrange("p (k n) -> p k n", k=KT)
            def wo(t, s): return t[:, s, 1536:2048].rearrange("p (h d) -> p h d", h=GH)

            load_x(0)
            sp.dma(ident_f[:, :], ident, dma_const)
            sp.dma(mask[:, SEQ - P:SEQ], mask_tri, dma_const)
            sp.dma(raw[:, 0:GWORDS], wa[0], dma_w[0])
            sp.dma(bias[:, :, :], ba, dma_b)
            for b in range(1, BATCH):
                load_x(b)
            sp.dma(bo_bc[:, :], bo.to_broadcast([P, DM]), dma_b)
            for dst, src in ((wv_t_sb, wv_t), (router_sb, router), (conv_sb, conv_w)):
                sp.dma(dst[:, :, :], src, dma_small)
            sp.dma(rot_sb[:, :, :, :], rot_tab, dma_small)

            pool.do(lambda e: e.memset(mask[:, 0:SEQ - P], 0.0))
            pool.wait((dma_b, 32), (dma_w[0], 16))
            pool.do(lambda e: e.tensor_scalar(bias[:, 0, :], bias[:, 0, :], SCALE_A, None, ALU.mult))
            consts = pool.counted(lambda e: e.tensor_scalar(raw[:, 0:512], raw[:, 0:512], SCALE_A, None,
                                                            ALU.mult))
            tile_stats(range(0, 4), (dma_x[0], 16))
            inverse_std(0, 4)
            pe.wait((dma_const, 32))

            xt_ready = {}

            def transpose_batch(b, xn_ready):
                cols = slice(b * SEQ, (b + 1) * SEQ)
                for f in range(KT):
                    k = core.take()
                    m = transpose_half(f, k, xn_ready)
                    xt_ready[b] = split_from(bank[k][:, :], XT_hi[:, f, cols], XT_lo[:, f, cols], m)
                    core.give(k, xt_ready[b])

            xn_ready = normalise_four(range(0, 4))
            for b in range(1, BATCH):
                tile_stats(range(4 * b, 4 * b + 4), (dma_x[b], 16))
            inverse_std(4, NT)
            transpose_batch(0, xn_ready)
            w_ready, qkv_read, o_read = {}, {}, {}
            act.wait((dma_w[0], 16), consts)
            m = act.counted(lambda e: e.activation(W_hi[:, 0, :], raw[:, 0:GWORDS], ACT.Copy))
            dve.wait(m, consts, (dma_const, 32))
            w_ready[0] = dve.counted(lambda e: e.tensor_tensor(
                W_lo[:, 0, :], raw[:, 0:GWORDS], W_hi[:, 0, :].bitcast(F32), ALU.subtract))
            sp.wait(w_ready[0])
            sp.dma(raw[:, 0:GWORDS], wa[1], dma_w[1])
            act.wait((dma_b, 32))

            bias_in = {}

            def add_output_bias(b):
                pool.wait(xt_ready[b], (dma_b, 32), pool.last())
                bias_in[b] = pool.counted(lambda e: e.tensor_tensor(
                    X[:, 4 * b:4 * b + 4, :], X[:, 4 * b:4 * b + 4, :],
                    bo_bc[:, :].unsqueeze(1).to_broadcast([P, 4, DM]), ALU.add))

            def split_weights(g, part):
                s, cols = g % 2, slice(512 * part, 512 * part + 512)
                pool.wait((dma_w[g], 16), *before(o_read if part == 3 else qkv_read, g - 2))
                if part == 0:
                    pool.wait(pool.counted(lambda e: e.tensor_scalar(raw[:, cols], raw[:, cols], SCALE_A,
                                                                     None, ALU.mult)))
                pool.wait(pool.counted(lambda e: e.tensor_scalar(W_hi[:, s, cols], raw[:, cols], 1.0, None,
                                                                 ALU.mult)))
                w_ready[g] = pool.counted(lambda e: e.tensor_tensor(
                    W_lo[:, s, cols], raw[:, cols], W_hi[:, s, cols].bitcast(F32), ALU.subtract))
                if part == 3:
                    if g + 1 < NG:
                        sp.wait(w_ready[g])
                        sp.dma(raw[:, 0:GWORDS], wa[g + 1], dma_w[g + 1])
                    else:
                        load_mix(0, w_ready[g])

            units = NG * BATCH * GH
            qk_ready, s_done, v_ready, av_done, z_ready, o_done = {}, {}, {}, {}, {}, {}

            def place(n):
                return n // 8, (n % 8) // 2, n % 2

            def project(n, which):
                g, b, hh = place(n)
                s, cols = g % 2, slice(b * SEQ, (b + 1) * SEQ)
                view = (wq, wk)[which]
                hi, lo = ((Q_hi, Q_lo), (K_hi, K_lo))[which]
                k = core.take()
                pe.wait(w_ready[g], xt_ready[b])
                for kt in range(KT):
                    step = three_pass(pe, bank[k][:, :], view(W_hi, s)[:, kt, hh, :],
                                      view(W_lo, s)[:, kt, hh, :], XT_hi[:, kt, cols],
                                      XT_lo[:, kt, cols], kt == 0, kt == KT - 1)
                    if kt < KT - 1:
                        pe.do(step)
                m = pe.counted(step)
                h = g * GH + hh
                lo_step = split_from(bank[k][:, :], hi[:, n % 2, :], lo[:, n % 2, :], m,
                                     before(s_done, n - 2), bias=bias[:, which, h:h + 1], later=True)

                def finish():
                    qk_ready[n, which] = lo_step()
                    core.give(k, qk_ready[n, which])
                core.after(1, finish)

            def project_v(u, half):
                g, b = u // BATCH, u % BATCH
                s = g % 2
                k = core.take()
                pe.wait(w_ready[g], xt_ready[b])
                for tt in range(2):
                    cols = slice(b * SEQ + (2 * half + tt) * P, b * SEQ + (2 * half + tt + 1) * P)
                    for kt in range(KT):
                        step = three_pass(pe, bank[k][:, tt * GW:(tt + 1) * GW], XT_hi[:, kt, cols],
                                          XT_lo[:, kt, cols], wv(W_hi, s)[:, kt, :],
                                          wv(W_lo, s)[:, kt, :], kt == 0, kt == KT - 1)
                        if tt == 0 or kt < KT - 1:
                            pe.do(step)
                m = pe.counted(step)
                if b == BATCH - 1 and half == 1:
                    qkv_read[g] = (m,)
                src = bank[k][:, :].rearrange("p (t n) -> p t n", t=2)
                tts = slice(2 * half, 2 * half + 2)
                lo_step = split_from(src, V_hi[:, u % 2, tts, :], V_lo[:, u % 2, tts, :], m,
                                     before(av_done, 2 * (u - 2) + 1), later=True)

                def finish():
                    v_ready[u, half] = lo_step()
                    core.give(k, v_ready[u, half])
                core.after(1, finish)

            def scores(n, i):
                q = n % 2
                m = core.scores(n, i, Q_hi[:, q, :], Q_lo[:, q, :], K_hi[:, q, :], K_lo[:, q, :],
                                [qk_ready[n, 0], qk_ready[n, 1]])
                s_done[n] = (m,)
                return core.pending

            def values(n):
                g, b, hh = place(n)
                u, q = n // 2, n % 2
                k = core.take()
                pe.wait(v_ready[u, 0], v_ready[u, 1], core.pt[n, TPB - 1])
                for i in range(TPB):
                    pe.wait(core.pt[n, i])
                hs = slice(hh * DH, (hh + 1) * DH)
                for j in range(TPB):
                    qs = slice(P * j, SEQ)
                    step = three_pass(pe, bank[k][:, qs], V_hi[:, u % 2, j, hs], V_lo[:, u % 2, j, hs],
                                      PT_hi[:, q, j, qs], PT_lo[:, q, j, qs], j == 0, j == TPB - 1)
                    if j < TPB - 1:
                        pe.do(step)
                m = pe.counted(step)
                av_done[n] = (m,)
                h = g * GH + hh
                lo_step = split_from(bank[k][:, :], Z_hi[:, u % 2, hh, :], Z_lo[:, u % 2, hh, :], m,
                                     before(o_done, u - 2), bias=bias[:, 2, h:h + 1], later=True)

                def finish():
                    z_ready[u, hh] = lo_step()
                    core.give(k, z_ready[u, hh])
                core.after(1, finish)

            def output(u, half):
                g, b = u // BATCH, u % BATCH
                s = g % 2
                k = core.take()
                pe.wait(z_ready[u, 0], z_ready[u, 1])
                for tt in range(2):
                    cols = slice((2 * half + tt) * P, (2 * half + tt + 1) * P)
                    for hh in range(GH):
                        step = three_pass(pe, bank[k][:, tt * DM:(tt + 1) * DM],
                                          Z_hi[:, u % 2, hh, cols], Z_lo[:, u % 2, hh, cols],
                                          wo(W_hi, s)[:, hh, :], wo(W_lo, s)[:, hh, :],
                                          hh == 0, hh == GH - 1)
                        if tt == 0 or hh < GH - 1:
                            pe.do(step)
                m = pe.counted(step)
                if half == 1:
                    o_done[u] = (m,)
                    if b == BATCH - 1:
                        o_read[g] = (m,)
                t0 = 4 * b + 2 * half

                def finish():
                    dve.wait(m, bias_in[b], *x_added.get(t0, ()))
                    done = dve.counted(lambda e: e.tensor_tensor(
                        X[:, t0:t0 + 2, :], X[:, t0:t0 + 2, :],
                        bank[k][:, :].rearrange("p (t d) -> p t d", t=2), ALU.add))
                    x_added[t0] = (done,)
                    core.give(k, done)
                    if g == NG - 1:
                        tile_stats((t0, t0 + 1), done)
                core.after(1, finish)

            x_added = {}
            pool_todo = []
            project(0, 0)
            project(0, 1)
            core.flush()
            for n in range(units + 5):
                g, b, hh = place(n)
                if n in (0, 1, 3, 5):
                    add_output_bias((n + 1) // 2)
                if n % 8 in (1, 2, 3, 4) and g + 1 < NG:
                    split_weights(g + 1, n % 8 - 1)
                if n == units - 4:
                    mix_ready = prepare_mix(0, core.take, core.give)
                if units - 4 <= n < units - 1:
                    keys_ready = turn_keys(0, n - units + 5)
                if n == units + 1:
                    w_mix = split_mix((*mix_ready, keys_ready), qkv_read[NG - 1][0])
                u = n // 2
                for i in range(TPB):
                    if n in (0, 2, 4) and i == 1:
                        xn_ready = normalise_four(range(2 * n + 4, 2 * n + 8))
                    turned = 0 <= TPB * n + i - LAG_A < TPB * units
                    if turned:
                        m, t = divmod(TPB * n + i - LAG_A, TPB)
                        pt_lo = core.transposes(m, t, (PT_hi[:, m % 2, :, :], PT_lo[:, m % 2, :, :]),
                                                before(av_done, m - 2))
                    core.flush()
                    if n in (0, 2, 4) and i == 3:
                        transpose_batch(n // 2 + 1, xn_ready)
                    if pool_todo and ORD_A:
                        core.normalise(pool_todo.pop())
                    pend = scores(n, i) if n < units else None
                    if turned:
                        pt_lo()
                    if pool_todo and not ORD_A:
                        core.normalise(pool_todo.pop())
                    if pend:
                        pool_todo.append(pend)
                    if i == PA0 and n + 1 < units:
                        project(n + 1, 0)
                    if i == PA1 and n + 1 < units:
                        project(n + 1, 1)
                    if i == PAV and n < units:
                        project_v(u, hh)
                    at = TPB * n + i - VAT_A
                    if at >= 0 and at % TPB == 0 and at // TPB < units:
                        values(at // TPB)
                    at = TPB * n + i - OAT_A
                    if at >= 0 and at % TPB == 0 and at // TPB < units:
                        output(at // TPB // 2, at // TPB % 2)
            barrier()
            ctx.close()
            return w_mix

        def mixture(tag, order, w_ready, last, between=None):
            ctx = ExitStack()
            al0 = allocator(ctx)
            al = lambda name, shape, dt=F32: al0(f"{tag}_{name}", shape, dt)
            FIRST = [0, 4, 7, 9]
            CRING, RING = 3, 2
            QG = MIX_LOGIT
            conv = al("conv", [P, KT, SEQ])
            shift = al("shift", [P, NT])
            C_hi, C_lo = (al(n, [P, CRING, KT, SEQ], F32R) for n in ("C_hi", "C_lo"))
            qg = al("qg", [P, RING, BATCH, QG])
            vv = al("vv", [P, RING, BATCH, MIX_DV])
            lg = al("lg", [P, RING, BATCH, 2 * MIX_H])
            prod = al("prod", [P, PAIRS, MIX_DK])
            dots = al("dots", [P, RING, PAIRS, MIX_H])
            small = [al(f"sm{i}", [P, BATCH, MIX_H]) for i in range(12)]
            same = al("same", [P, BATCH, BATCH, MIX_H])
            coef = al("coef", [P, PAIRS, MIX_H])
            ov = al("ov", [P, 6, MIX_DV])
            oo = al("oo", [P, BATCH, MIX_DV])
            sq = ov[:, 0:BATCH, :]
            yy = al("yy", [P, BATCH, MIX_DV])
            Y_hi, Y_lo = (t[:, MIX_WORDS:MIX_WORDS + KT * SEQ].rearrange("p (k n) -> p k n", k=KT)
                          for t in (OP_hi, OP_lo))
            tri = al("tri", [P, BATCH, BATCH, MIX_H])

            small_loaded = (dma_small, 64)
            pool.wait(pool.counted(lambda e: e.memset(tri[:, :, :, :], 0.0)))
            for l in range(BATCH):
                tri_ready = pool.counted(lambda e, l=l: e.memset(tri[:, l, 0:l + 1, :], 1.0))
            inverse_std(0, NT)
            centre = dve.counted(lambda e: e.scalar_tensor_tensor(
                out=shift[:, :], in0=moments[:, :, 0], scalar=-1.0, in1=rstd[:, :], op0=ALU.mult,
                op1=ALU.mult))

            free = {k: () for k in range(8)}
            marks, used = {}, [0]

            def earlier(kind, c):
                return marks[kind, c] if c >= 0 else ()

            def front_a(c):
                act.wait(*xn_read[0], centre)
                for l in range(BATCH // 2, BATCH):
                    t = 4 * l + c
                    act_part = act.counted(lambda e, l=l, t=t: e.activation(
                        xn[:, l, :], X[:, t, :], ACT.Identity, bias=shift[:, t:t + 1],
                        scale=rstd[:, t:t + 1]))
                ready = normalise_four([4 * l + c for l in range(BATCH // 2)])
                pe.wait(act_part)
                act.wait(small_loaded)
                dve.wait(small_loaded)
                for f in range(KT):
                    m = transpose_half(f, f, ready, *free[f])
                    free[f] = None
                    act.wait(m, *earlier("conv", c - 1))
                    m = act.counted(lambda e, f=f: e.activation(conv[:, f, :], bank[f][:, :], ACT.Copy,
                                                                scale=conv_sb[:, f, 1:2]))
                    marks["taps", c, f] = m

            def front_b(c, f):
                dve.wait(marks["taps", c, f])
                m = dve.counted(lambda e: e.scalar_tensor_tensor(
                    out=conv[:, f, P:SEQ], in0=bank[f][:, 0:SEQ - P], scalar=conv_sb[:, f, 0:1],
                    in1=conv[:, f, P:SEQ], op0=ALU.mult, op1=ALU.add))
                free[f] = (m,)
                act.wait(m, *earlier("proj", c - CRING))
                m = act.counted(lambda e: e.activation(conv[:, f, :], conv[:, f, :], ACT.Silu))
                act.wait(m)
                m = act.counted(lambda e: e.activation(C_hi[:, c % CRING, f, :], conv[:, f, :], ACT.Copy))
                pool.wait(m, pool.last())
                m = pool.counted(lambda e: e.tensor_tensor(C_lo[:, c % CRING, f, :], conv[:, f, :],
                                                           C_hi[:, c % CRING, f, :].bitcast(F32),
                                                           ALU.subtract))
                marks["conv", c] = marks["lo", c] = (m,)

            def columns(c, l, a, z, at=0, k=None):
                if k is None:
                    k = 4 + used[0] % 4
                    used[0] += 1
                    pe.wait(*marks["lo", c], w_ready, *free[k])
                    free[k] = None
                cols, q = slice(l * P, (l + 1) * P), c % CRING
                for kt in range(KT):
                    step = three_pass(pe, bank[k][:, at:at + z - a], C_hi[:, q, kt, cols],
                                      C_lo[:, q, kt, cols], mix_cols(OP_hi, a, z)[:, kt, :],
                                      mix_cols(OP_lo, a, z)[:, kt, :], kt == 0, kt == KT - 1)
                    if kt < KT - 1:
                        pe.do(step)
                return k, pe.counted(step)

            def project_gates(c):
                r = c % RING
                for l in range(BATCH):
                    k, m = columns(c, l, 0, MIX_K)
                    act.wait(m, *earlier("gated", c - RING))
                    act.do(lambda e, l=l, k=k: e.activation(qg[:, r, l, :], bank[k][:, 0:QG], ACT.Silu))
                    m = act.counted(lambda e, l=l, k=k: e.activation(
                        lg[:, r, l, :], bank[k][:, QG:QG + 2 * MIX_H], ACT.Copy))
                    free[k] = (m,)
                marks["qg", c] = (m,)

            def project_kv(c, m_):
                n, r = BATCH - m_, c % RING
                k, kv = columns(c, m_, MIX_K, MIX_K + n * MIX_DK)
                if n <= 2:
                    at, v_bank = n * MIX_DK, k
                    _, vd = columns(c, m_, MIX_V, MIX_COLS, at, k)
                else:
                    at = 0
                    v_bank, vd = columns(c, m_, MIX_V, MIX_COLS)
                act.wait(vd, *marks["qg", c], *earlier("weighted", c - RING))
                mv = act.counted(lambda e: e.activation(
                    vv[:, r, m_, :], bank[v_bank][:, at:at + MIX_DV], ACT.Copy))
                if v_bank != k:
                    free[v_bank] = (mv,)
                marks["v", c] = (mv,)
                marks["k", c, m_] = (k, mv if v_bank == k else kv)
                marks["proj", c] = (pe.last(),)

            def products_qk(c, m_):
                n, r = BATCH - m_, c % RING
                k, ready = marks["k", c, m_]
                dve.wait(ready, *marks["qg", c], *earlier("dots", c - 1))
                mp = dve.counted(lambda e: e.tensor_tensor(
                    prod[:, FIRST[m_]:FIRST[m_] + n, :],
                    bank[k][:, 0:n * MIX_DK].rearrange("p (n f) -> p n f", n=n),
                    qg[:, r, m_:BATCH, 0:MIX_DK], ALU.mult))
                free[k] = (mp,)
                return mp

            def sums_qk(c):
                r = c % RING
                dve.wait(dve.last())
                m = dve.counted(lambda e: e.tensor_reduce(
                    dots[:, r, :, :].rearrange("p n h -> p (n h)"),
                    prod[:, :, :].rearrange("p n (h f) -> p (n h) f", f=MIX_HDK), AX.X, ALU.add))
                marks["dots", c] = (m,)

            def chain(step):
                m = dve.counted(step)
                dve.wait(m)
                return m

            (diff, first, mag, prob, cnt, rcnt, tmp, pw, var, dev, inv_dev, neg) = (
                t[:, :, :] for t in small)

            def route(c):
                r = c % RING
                LG = lg[:, r, :, :]
                dve.wait(*marks["qg", c], tri_ready)
                chain(lambda e: e.tensor_tensor(diff, LG[:, :, 0:MIX_H], LG[:, :, MIX_H:2 * MIX_H],
                                                ALU.subtract))
                dve.do(lambda e: e.tensor_scalar(neg, diff, -1.0, None, ALU.mult))
                chain(lambda e: e.tensor_scalar(first, diff, 0.0, None, ALU.is_ge))
                m = dve.counted(lambda e: e.tensor_tensor(mag, diff, neg, ALU.max))
                act.wait(m)
                marks["prob", c] = (act.counted(lambda e: e.activation(prob, mag, ACT.Tanh, scale=0.5)),)
                chain(lambda e: e.tensor_tensor(same[:, :, :, :],
                                                first.unsqueeze(2).to_broadcast([P, BATCH, BATCH, MIX_H]),
                                                first.unsqueeze(1).to_broadcast([P, BATCH, BATCH, MIX_H]),
                                                ALU.is_equal))
                chain(lambda e: e.tensor_tensor(same[:, :, :, :], same[:, :, :, :], tri[:, :, :, :],
                                                ALU.mult))
                chain(lambda e: e.tensor_reduce(cnt, same[:, :, :, :].rearrange("p l m h -> p l h m"),
                                                AX.X, ALU.add))
                dve.do(lambda e: e.reciprocal(rcnt, cnt))

            def coefficients(c):
                r = c % RING
                dve.wait(*marks["prob", c])
                chain(lambda e: e.tensor_scalar(tmp, prob, 0.5 * MIX_HDK ** -0.5, 0.5 * MIX_HDK ** -0.5,
                                                ALU.mult, ALU.add))
                chain(lambda e: e.tensor_tensor(pw, tmp, rcnt, ALU.mult))
                dve.wait(*earlier("weighted", c - 1))
                for m_ in range(BATCH):
                    n = BATCH - m_
                    mm = dve.counted(lambda e, m_=m_, n=n: e.tensor_tensor(
                        coef[:, FIRST[m_]:FIRST[m_] + n, :], same[:, m_:BATCH, m_, :],
                        pw[:, m_:BATCH, :], ALU.mult))
                dve.wait(mm, *marks["dots", c])
                marks["coef", c] = (chain(lambda e: e.tensor_tensor(coef[:, :, :], coef[:, :, :],
                                                                    dots[:, r, :, :], ALU.mult)),)

            heads = lambda ap: ap.rearrange("p m (h d) -> p m h d", d=MIX_HDV)

            def weighted(m_, dst, r):
                n = BATCH - m_
                v = vv[:, r, m_, :].rearrange("p (h d) -> p h d", d=MIX_HDV)
                w = coef[:, FIRST[m_]:FIRST[m_] + n, :]
                shape = [P, n, MIX_H, MIX_HDV]
                return lambda e: e.tensor_tensor(heads(dst), v.unsqueeze(1).to_broadcast(shape),
                                                 w.unsqueeze(3).to_broadcast(shape), ALU.mult)

            parts = {}

            def products(c):
                r = c % RING
                pool.wait(*marks["coef", c], *marks["v", c], *earlier("squares", c - 1), pool.last())
                at = 0
                for m_ in range(1, BATCH):
                    dst = ov[:, at:at + BATCH - m_, :]
                    parts[m_] = (dst, pool.counted(weighted(m_, dst, r)))
                    at += BATCH - m_
                marks["weighted", c] = (pool.last(),)
                dve.wait(*marks["v", c], *earlier("gated", c - 1), *earlier("squared", c - 1))
                marks["first", c] = dve.counted(weighted(0, oo[:, :, :], r))

            def total(c):
                r = c % RING
                m = marks["first", c]
                for m_ in range(1, BATCH):
                    dst, ready = parts[m_]
                    dve.wait(m, ready)
                    m = dve.counted(lambda e, m_=m_, dst=dst: e.tensor_tensor(
                        oo[:, m_:BATCH, :], oo[:, m_:BATCH, :], dst, ALU.add))
                act.wait(m)
                marks["squared", c] = (act.counted(lambda e: e.activation(sq, oo[:, :, :], ACT.Square)),)
                pool.wait(m, pool.last(), *earlier("yt", c - 1))
                marks["gated", c] = (pool.counted(lambda e: e.tensor_tensor(
                    yy[:, :, :], oo[:, :, :], qg[:, r, :, MIX_DK:QG], ALU.mult)),)

            def variance(c):
                dve.wait(*marks["squared", c])
                marks["squares", c] = (chain(lambda e: e.tensor_reduce(
                    var.rearrange("p l h -> p (l h)"), sq.rearrange("p l (h d) -> p (l h) d", d=MIX_HDV),
                    AX.X, ALU.add)),)
                m = dve.counted(lambda e: e.tensor_scalar(var, var, 1.0 / MIX_HDV, EPS, ALU.mult, ALU.add))
                act.wait(m)
                marks["root", c] = (act.counted(lambda e: e.activation(dev, var, ACT.Sqrt)),)

            def scale(c):
                dve.wait(*marks["root", c])
                chain(lambda e: e.reciprocal(inv_dev, dev))
                pool.wait(dve.last(), pool.last(), *marks["gated", c])
                m = pool.counted(lambda e: e.tensor_tensor(
                    yy[:, :, :].rearrange("p l (h d) -> p (l h) d", d=MIX_HDV),
                    yy[:, :, :].rearrange("p l (h d) -> p (l h) d", d=MIX_HDV),
                    inv_dev.rearrange("p l h -> p (l h)").unsqueeze(2)
                    .to_broadcast([P, BATCH * MIX_H, MIX_HDV]), ALU.mult))
                marks["mix", c] = marks["y", c] = (m,)

            def turn(c):
                pe.wait(*marks["y", c])
                for f in range(KT):
                    k = 2 + f
                    pe.wait(*free[k])
                    for l in range(BATCH):
                        step = (lambda e, l=l, f=f, k=k: e.transpose(
                            bank[k][:, l * P:(l + 1) * P], yy[:, l, f * P:(f + 1) * P], ident_f[:, :]))
                        if l < BATCH - 1:
                            pe.do(step)
                    m = pe.counted(step)
                    lo = split_from(bank[k][:, :], Y_hi[:, f, :], Y_lo[:, f, :], m, earlier("out", c - 1))
                    free[k] = (lo,)
                marks["yt", c] = (pe.last(),)
                marks["ysplit", c] = (lo,)

            def output(c):
                for half in range(2):
                    k = 2 + half
                    pe.wait(*marks["ysplit", c], *free[k])
                    for a in range(2):
                        l = 2 * half + a
                        cols = slice(l * P, (l + 1) * P)
                        for kt in range(KT):
                            step = three_pass(pe, bank[k][:, a * DM:(a + 1) * DM], Y_hi[:, kt, cols],
                                              Y_lo[:, kt, cols], mix_out_w(OP_hi)[:, kt, :],
                                              mix_out_w(OP_lo)[:, kt, :], kt == 0, kt == KT - 1)
                            if a == 0 or kt < KT - 1:
                                pe.do(step)
                    m = pe.counted(step)
                    tiles = X[:, 8 * half:8 * half + 8, :].rearrange("p (a r) d -> p a r d", r=4)[:, :, c, :]
                    dve.wait(m)
                    m = dve.counted(lambda e, tiles=tiles, k=k: e.tensor_tensor(
                        tiles, tiles, bank[k][:, :].rearrange("p (a d) -> p a d", a=2), ALU.add))
                    free[k] = (m,)
                    if last:
                        sp.wait(m)
                        for a in range(2):
                            t = 4 * (2 * half + a) + c
                            sp.dma(out_tiles[:, t, :], X[:, t, :], dma_out)
                marks["out", c] = (pe.last(),)
                if not last:
                    tile_stats([4 * l + c for l in range(BATCH)], m)

            steps = {"norm": front_a, "gates": project_gates, "route": route,
                     "sums": sums_qk, "coef": coefficients, "products": products, "total": total,
                     "variance": variance, "scale": scale, "turn": turn, "out": output,
                     "between": lambda c: between(c, free)}
            for f in range(KT):
                steps[f"conv{f}"] = lambda c, f=f: front_b(c, f)
            for m_ in range(BATCH):
                steps[f"kv{m_}"] = lambda c, m_=m_: project_kv(c, m_)
                steps[f"qk{m_}"] = lambda c, m_=m_: products_qk(c, m_)
            for name, c in order:
                steps[name](c)
            if not last:
                barrier()
            ctx.close()

        class LatentAttention:

            def __init__(self):
                self.ctx = ExitStack()
                al = allocator(self.ctx)
                self.Wq = al("b_Wq", [P, HEADS, P], F32R)
                self.Wsw = al("b_Wsw", [P, HEADS // 2, P], F32R)
                self.N_hi, self.N_lo = (al(f"b_{n}", [P, HEADS // 2, DM], F32R) for n in ("Nh", "Nl"))
                self.Wc_hi, self.Wc_lo = (al(f"b_{n}", [P, KT, 4, P], F32R) for n in ("Wch", "Wcl"))
                self.pro = ExitStack()
                ap_ = allocator(self.pro)
                self.wsrc = ap_("b_wsrc", [P, KT, 4, P])
                self.qbt = ap_("b_qbt", [P, 4, 2, RANK])
                self.kbt = ap_("b_kbt", [P, 4, RANK])
                self.vbt = ap_("b_vbt", [P, 4, RANK])
                self.wo = ap_("b_wo", [P, 4, DM])
                self.wq_raw = ap_("b_wqraw", [P, 4, P])
                self.wsw_raw = ap_("b_wswraw", [P, HEADS // 2, P])
                self.dma_w, self.dma_heads = sem("dma_b_w"), sem("dma_b_heads")
                sp.dma(self.wsrc[:, :, 0, :], wqa, self.dma_w)
                sp.dma(self.wsrc[:, :, 1:4, :].rearrange("p k j n -> p k (j n)"), wkva, self.dma_w)
                for half in range(2):
                    sp.dma(self.wsw_raw[64 * half:64 * half + 64, :, :], wqb_sw, self.dma_w)
                self.loaded = (self.dma_w, 16 * 4)
                self.sent = 0
                self.load_heads(0)

            def load_heads(self, r):
                hs = slice(4 * r, 4 * r + 4)
                for rep in range(2):
                    sp.dma(self.qbt[:, :, rep, :], wqb_t[:, hs, :], self.dma_heads)
                sp.dma(self.kbt[:, :, :], wkvbk_t[:, hs, :], self.dma_heads)
                sp.dma(self.vbt[:, :, :], wkvbv_t[:, hs, :], self.dma_heads)
                sp.dma(self.wo[:, :, :], wout_b[:, hs, :], self.dma_heads)
                for half in range(2):
                    sp.dma(self.wq_raw[64 * half:64 * half + 64, :, :], wqb_pe[:, hs, :], self.dma_heads)
                self.sent += 7
                self.heads_loaded = (self.dma_heads, 16 * self.sent)

            def prepare(self, r, free):
                if r == 0:
                    self.prepare_rest()
                hs = slice(4 * r, 4 * r + 4)
                Wq, wq_raw = self.Wq, self.wq_raw
                pe.wait(self.heads_loaded, *free[0])
                for j in range(4):
                    step = (lambda e, j=j: e.matmul(bank[0][:, j * 64:(j + 1) * 64],
                                                    self.qbt[:, j, :, :].rearrange("p a r -> p (a r)"),
                                                    self.kbt[:, j, :], start=True, stop=True))
                    if j < 3:
                        pe.do(step)
                m = pe.counted(step)
                act.wait(m, self.heads_loaded)
                absv = bank[0][:, 0:256].rearrange("p (j c) -> p j c", c=64)
                for par in range(2):
                    c0 = 0 if par == 0 else 64
                    m = act.counted(lambda e, par=par, c0=c0: e.activation(
                        wq_raw[:, par:4:2, c0:c0 + 64], absv[:, par:4:2, :], ACT.Copy))
                free[0] = (m,)
                self.scale_and_split(wq_raw, Wq[:, hs, :], m)
                pe.wait(*free[1])
                for pr in range(2):
                    for par in range(2):
                        j = 2 * pr + par
                        step = (lambda e, j=j, pr=pr, par=par: e.matmul(
                            bank[1][64 * par:64 * par + 64, pr * DM:(pr + 1) * DM], self.vbt[:, j, :],
                            self.wo[:, j, :], start=True, stop=True))
                        if j < 3:
                            pe.do(step)
                m = pe.counted(step)
                pair = slice(2 * r, 2 * r + 2)
                lo = split_from(bank[1][:, :].rearrange("p (a d) -> p a d", a=2),
                                self.N_hi[:, pair, :], self.N_lo[:, pair, :], m)
                free[1] = (lo,)
                self.n_ready = lo
                if r < 3:
                    sp.wait(m, self.w_ready)
                    self.load_heads(r + 1)

            def prepare_rest(self):
                pool.wait(self.loaded, pool.last())
                pool.wait(pool.counted(lambda e: e.tensor_scalar(self.Wc_hi[:, :, :, :],
                                                                 self.wsrc[:, :, :, :], 1.0, None, ALU.mult)))
                self.wc_ready = pool.counted(lambda e: e.tensor_tensor(
                    self.Wc_lo[:, :, :, :], self.wsrc[:, :, :, :], self.Wc_hi[:, :, :, :].bitcast(F32),
                    ALU.subtract))
                self.scale_and_split(self.wsw_raw, self.Wsw[:, :, :])

            def scale_and_split(self, raw_w, split, *ready):
                pool.wait(*ready, self.loaded, pool.last())
                pool.wait(pool.counted(lambda e: e.tensor_scalar(raw_w[:, :, :], raw_w[:, :, :], SCALE_B,
                                                                 None, ALU.mult)))
                pool.wait(pool.counted(lambda e: e.tensor_scalar(split, raw_w[:, :, :], 1.0, None,
                                                                 ALU.mult)))
                self.w_ready = pool.counted(lambda e: e.tensor_tensor(
                    split[64:128], raw_w[64:128, :, :], split[64:128].bitcast(F32), ALU.subtract))

            def run(self):
                Wq, Wsw, N_hi, N_lo = self.Wq, self.Wsw, self.N_hi, self.N_lo
                Wc_hi, Wc_lo = self.Wc_hi, self.Wc_lo
                self.pro.close()
                al = allocator(self.ctx)
                view = lambda a, z, pat, **kw: [t[:, a:z].rearrange(pat, **kw) for t in (OP_hi, OP_lo)]
                XT_hi, XT_lo = view(0, KT * SEQ, "p (k n) -> p k n", k=KT)
                QA_hi, QA_lo = view(2 * SEQ, 4 * SEQ, "p (s n) -> p s n", s=2)
                KC_hi, KC_lo = view(4 * SEQ, 8 * SEQ, "p (s v n) -> p s v n", s=2, v=2)
                tabs = al("b_tabs", [P, 3, SEQ])
                CT = al("b_CT", [P, 2, TPB, RANK])
                kk = al("b_kk", [P, 2, SEQ])
                kt_ = al("b_kt", [P, SEQ])
                qt = al("b_qt", [P, 2, SEQ])
                qr = al("b_qr", [P, 3, SEQ])
                Q_hi, Q_lo = (al(f"b_{n}", [P, 3, SEQ], F32R) for n in ("Qh", "Ql"))
                PT = al("b_PT", [P, 4, TPB, SEQ])
                U_hi, U_lo = (al(f"b_{n}", [P, 2, SEQ], F32R) for n in ("Uh", "Ul"))
                core = Core(al, "b", split=False, ring=2)
                per_b = HEADS
                pairs, units = BATCH * HEADS // 2, BATCH * HEADS
                s_done, av_done, u_ready, o_done = {}, {}, {}, {}
                q_ready, sw_ready, sw_read, x_added = {}, {}, {}, {}
                xt_ready, qa_ready, kc_ready, ct_ready, kk_read, xt_read = {}, {}, {}, {}, {}, {}

                dma_tabs = sem("dma_b_tabs")
                sp.dma(tabs[:, :, :], rope_tab, dma_tabs)
                load_mix(1)
                inverse_std(0, NT)
                for s in (pe, dve, act, pool):
                    s.wait(self.w_ready, self.n_ready, self.wc_ready)

                def latent_norm(b):
                    xn_ready = normalise_four(range(4 * b, 4 * b + 4))
                    for f in range(KT):
                        k = core.take()
                        m = transpose_half(f, k, xn_ready)
                        xt_ready[b] = split_from(bank[k][:, :], XT_hi[:, f, :], XT_lo[:, f, :], m,
                                                 before(xt_read, b - 1))
                        core.give(k, xt_ready[b])

                def latent_project(b, j):
                    k = core.take()
                    pe.wait(xt_ready[b])
                    for kt in range(KT):
                        step = three_pass(pe, bank[k][:, :], Wc_hi[:, kt, j, :], Wc_lo[:, kt, j, :],
                                          XT_hi[:, kt, :], XT_lo[:, kt, :], kt == 0, kt == KT - 1)
                        if kt < KT - 1:
                            pe.do(step)
                    m = pe.counted(step)
                    xt_read[b] = (m,)
                    if j == 0:
                        m = split_from(bank[k][:, :], QA_hi[:, b % 2, :], QA_lo[:, b % 2, :], m,
                                       before(s_done, per_b * (b - 1) - 1))
                        qa_ready[b] = m
                    else:
                        dve.wait(m, (dma_tabs, 16), *before(kk_read, b - 1))
                        dst = kt_[:, :] if j == 3 else kk[:, j - 1, :]
                        m = dve.counted(lambda e: e.tensor_tensor(dst, bank[k][:, :], tabs[:, j - 1, :],
                                                                  ALU.mult))
                    core.give(k, m)
                    return m

                def latent_keys(b, v, ready):
                    rows = slice(64, 128) if v == 0 else slice(0, 64)
                    dve.wait(ready)
                    m = dve.counted(lambda e: e.tensor_tensor(kk[rows, v, :], kk[rows, v, :],
                                                              kt_[rows, :], ALU.add))
                    act.wait(m, *before(s_done, per_b * (b - 1) - 1))
                    m = act.counted(lambda e: e.activation(KC_hi[:, b % 2, v, :], kk[:, v, :], ACT.Copy))
                    dve.wait(m)
                    return dve.counted(lambda e: e.tensor_tensor(
                        KC_lo[:, b % 2, v, :], kk[:, v, :], KC_hi[:, b % 2, v, :].bitcast(F32),
                        ALU.subtract))

                def latent_values(b):
                    k = core.take()
                    pe.wait(kc_ready[b])
                    for t in range(TPB):
                        step = (lambda e, t=t: e.transpose(bank[k][:, t * RANK:(t + 1) * RANK],
                                                           kk[0:64, 0, t * P:(t + 1) * P],
                                                           ident_f[0:64, 0:64]))
                        if t < TPB - 1:
                            pe.do(step)
                    m = pe.counted(step)
                    kk_read[b] = (m, kc_ready[b])
                    act.wait(m, *before(av_done, per_b * (b - 1) - 1))
                    m = act.counted(lambda e: e.activation(
                        CT[:, b % 2, :, :],
                        bank[k][:, 0:TPB * RANK].rearrange("p (t c) -> p t c", c=RANK), ACT.Copy))
                    ct_ready[b] = m
                    core.give(k, m)

                def latent(b, part):
                    if part == 0:
                        latent_norm(b)
                    elif part == 1:
                        latent_project(b, 0)
                        latent_project(b, 3)
                    elif part == 2:
                        kk_ready[b] = [latent_project(b, 1), latent_project(b, 2)]
                    elif part == 3:
                        latent_keys(b, 0, kk_ready[b][0])
                        kc_ready[b] = latent_keys(b, 1, kk_ready[b][1])
                    else:
                        latent_values(b)

                kk_ready = {}

                def two_pass(out, w, b):
                    pe.do(lambda e: e.matmul(out, w, QA_hi[:, b % 2, :], start=True, stop=False))
                    return pe.counted(lambda e: e.matmul(out, w, QA_lo[:, b % 2, :], start=False, stop=True))

                def swapped(p):
                    b, hp = p // 8, p % 8
                    k = core.take()
                    pe.wait(qa_ready[b])
                    m = two_pass(bank[k][:, :], Wsw[:, hp, :], b)

                    def finish():
                        dve.wait(m, *before(sw_read, p - 2))
                        sw_ready[p] = dve.counted(lambda e: e.tensor_tensor(
                            qt[:, p % 2, :], bank[k][:, :], tabs[:, 2, :], ALU.mult))
                        core.give(k, sw_ready[p])
                    core.after(1, finish)

                def query(n):
                    p, par = n // 2, n % 2
                    b, h = p // 8, 2 * (p % 8) + par
                    q = n % 3
                    k = core.take()
                    pe.wait(qa_ready[b])
                    m = two_pass(bank[k][:, :], Wq[:, h, :], b)
                    rows = slice(64, 128) if par == 0 else slice(0, 64)

                    def rotate():
                        dve.wait(m, *before(q_ready, n - 3))
                        cos_part = dve.counted(lambda e: e.tensor_tensor(
                            qr[:, q, :], bank[k][:, :], tabs[:, par, :], ALU.mult))
                        core.give(k, cos_part)
                        pool.wait(cos_part, sw_ready[p], pool.last())
                        summed = pool.counted(lambda e: e.tensor_tensor(
                            qr[rows, q, :], qr[rows, q, :], qt[rows, p % 2, :], ALU.add))
                        sw_read[p] = (summed,)
                        core.after(1, lambda: high(summed))

                    def high(summed):
                        act.wait(summed, *before(s_done, n - 3))
                        hi = act.counted(lambda e: e.activation(Q_hi[:, q, :], qr[:, q, :], ACT.Copy))
                        core.after(1, lambda: low(hi))

                    def low(hi):
                        dve.wait(hi)
                        q_ready[n] = (dve.counted(lambda e: e.tensor_tensor(
                            Q_lo[:, q, :], qr[:, q, :], Q_hi[:, q, :].bitcast(F32), ALU.subtract)),)
                    core.after(1, rotate)

                def scores(n, i):
                    b, par, q = n // per_b, n % 2, n % 3
                    m = core.scores(n, i, Q_hi[:, q, :], Q_lo[:, q, :], KC_hi[:, b % 2, par, :],
                                    KC_lo[:, b % 2, par, :], [*q_ready[n], kc_ready[b]])
                    s_done[n] = (m,)
                    return core.pending

                def values(p):
                    b = p // 8
                    k = core.take()
                    pe.wait(ct_ready[b])
                    for n in (2 * p, 2 * p + 1):
                        for i in range(TPB):
                            pe.wait(core.pt[n, i])
                    for j in range(TPB):
                        for par in range(2):
                            qs = slice(P * j, SEQ)
                            step = (lambda e, j=j, par=par, qs=qs: e.matmul(
                                bank[k][64 * par:64 * par + 64, qs], CT[:, b % 2, j, :],
                                PT[:, (2 * p + par) % 4, j, qs], start=(j == 0), stop=(j == TPB - 1)))
                            if j < TPB - 1 or par == 0:
                                pe.do(step)
                    m = pe.counted(step)
                    av_done[2 * p] = av_done[2 * p + 1] = (m,)
                    lo_step = split_from(bank[k][:, :], U_hi[:, p % 2, :], U_lo[:, p % 2, :], m,
                                         before(o_done, p - 2), later=True)

                    def finish():
                        u_ready[p] = lo_step()
                        core.give(k, u_ready[p])
                    core.after(1, finish)

                def output(p, half):
                    b, hp = p // 8, p % 8
                    k = core.take()
                    pe.wait(u_ready[p])
                    for tt in range(2):
                        cols = slice((2 * half + tt) * P, (2 * half + tt + 1) * P)
                        step = three_pass(pe, bank[k][:, tt * DM:(tt + 1) * DM], U_hi[:, p % 2, cols],
                                          U_lo[:, p % 2, cols], N_hi[:, hp, :], N_lo[:, hp, :], True, True)
                        if tt == 0:
                            pe.do(step)
                    m = pe.counted(step)
                    if half == 1:
                        o_done[p] = (m,)
                    t0 = 4 * b + 2 * half

                    def finish():
                        dve.wait(m, *x_added.get(t0, ()))
                        done = dve.counted(lambda e: e.tensor_tensor(
                            X[:, t0:t0 + 2, :], X[:, t0:t0 + 2, :],
                            bank[k][:, :].rearrange("p (t d) -> p t d", t=2), ALU.add))
                        x_added[t0] = (done,)
                        core.give(k, done)
                        if hp == 7:
                            tile_stats((t0, t0 + 1), done)
                    core.after(1, finish)

                pool_todo = []
                for part in range(3):
                    latent(0, part)
                swapped(0)
                query(0)
                latent(0, 3)
                core.flush()
                query(1)
                for _ in range(3):
                    core.flush()
                latent(0, 4)
                for n in range(units + 6):
                    b, j = n // per_b, n % per_b
                    if b + 1 < BATCH and j in (6, 7, 8, 9, 10):
                        latent(b + 1, j - 6)
                    if n == units - 4:
                        mix_ready = prepare_mix(1, core.take, core.give)
                    if n - units + 11 in (1, 4, 7):
                        keys_ready = turn_keys(1, (n - units + 11) // 3 + 1)
                    if n == units + 1:
                        w_mix = split_mix((*mix_ready, keys_ready), s_done[units - 1][0])
                    for i in range(TPB):
                        if 0 <= TPB * n + i - LAG < TPB * units:
                            m, t = divmod(TPB * n + i - LAG, TPB)
                            core.transposes(m, t, PT[:, m % 4, :, :], before(av_done, m - 4))
                        core.flush()
                        if pool_todo and ORD:
                            core.normalise(pool_todo.pop())
                        pend = scores(n, i) if n < units else None
                        if pool_todo and not ORD:
                            core.normalise(pool_todo.pop())
                        if pend:
                            pool_todo.append(pend)
                        if i == QUERY_AT and n + 2 < units:
                            if n % 2 == 0:
                                swapped(n // 2 + 1)
                            query(n + 2)
                        if TPB * n + i >= VAT and (TPB * n + i - VAT) % 8 == 0 and (TPB * n + i - VAT) // 8 < pairs:
                            values((TPB * n + i - VAT) // 8)
                        if TPB * n + i >= OAT and (TPB * n + i - OAT) % 4 == 0 and (TPB * n + i - OAT) // 8 < pairs:
                            output((TPB * n + i - OAT) // 8, (TPB * n + i - OAT) // 4 % 2)
                barrier()
                self.ctx.close()
                return w_mix

        w_mix = attention_a()
        attention_b = LatentAttention()
        mixture("m1", MIX_ORDER_1, w_mix, last=False, between=attention_b.prepare)
        w_mix = attention_b.run()
        mixture("m2", MIX_ORDER_2, w_mix, last=True)
        sp.wait((dma_out, 16 * NT))

        block = top.enter_context(nc.Block())

        @block.sync
        def _(e):
            sp.play(e)

        @block.tensor
        def _(e):
            pe.play(e)

        @block.scalar
        def _(e):
            act.play(e)

        @block.vector
        def _(e):
            dve.play(e)

        @block.gpsimd
        def _(e):
            pool.play(e)


def kernel(**inputs):
    from concourse import bacc
    from concourse.bass_utils import run_bass_kernel_spmd

    f = {n.removeprefix("L0_"): np.asarray(a) for n, a in inputs.items()}

    def rows(a):
        return a.reshape(-1, P, a.shape[-1]).transpose(1, 0, 2)

    def group(w):
        return w.reshape(NG, GH, KT, P, DH).transpose(0, 3, 2, 1, 4).reshape(NG, P, KT * GH * DH)

    wo = f["attn_a_W_O"].reshape(NG, GH, DH, DM).transpose(0, 2, 1, 3).reshape(NG, P, GH * DM)
    swap = np.arange(ROPE) ^ 1
    wqb = f["attn_b_Wqb"].reshape(RANK, HEADS, NOPE + ROPE)
    wkvb = f["attn_b_Wkvb"].reshape(RANK, HEADS, 2 * NOPE)
    pe_sw = wqb[:, :, NOPE:][:, :, swap].reshape(RANK, HEADS // 2, 2, ROPE)
    wkva = rows(f["attn_b_Wkva"])
    c_, pe_ = wkva[:, :, :RANK], wkva[:, :, RANK:]
    wqa = rows(f["attn_b_Wqa"])
    router = np.zeros((MIX_DV, 2, MIX_H), f["ffn_router_w"].dtype)
    for h in range(MIX_H):
        router[h * MIX_HDV:(h + 1) * MIX_HDV, :, h] = f["ffn_router_w"][h]

    theta = (np.float32(10000.0) ** (-2.0 * np.arange(ROPE // 2, dtype=np.float32) / ROPE)).astype(np.float32)
    angle = np.repeat(theta, 2)[:, None] * np.arange(SEQ, dtype=np.float32)[None, :]
    cos, sin = np.cos(angle), np.sin(angle)
    sin[0::2] *= -1
    one = np.ones_like(cos)
    rope_tab = np.stack([np.concatenate([one, cos]), np.concatenate([cos, one]),
                         np.concatenate([sin, sin])], axis=1).astype(np.float32)
    inv = (1.0 / np.float32(10000.0) ** (np.arange(0, MIX_HDK, 2, dtype=np.float32) / MIX_HDK)).astype(np.float32)
    fr = np.arange(1, BATCH, dtype=np.float32)[:, None] * inv[None, :]
    rot_tab = np.stack([np.concatenate([np.cos(fr), np.cos(fr)], 1),
                        np.concatenate([np.sin(fr), -np.sin(fr)], 1)], axis=1).astype(np.float32)
    wqb_pe = np.zeros((RANK, HEADS, P), wqb.dtype)
    wqb_pe[:, 0::2, 64:] = wqb[:, 0::2, NOPE:]
    wqb_pe[:, 1::2, :64] = wqb[:, 1::2, NOPE:]
    arrays = {
        "x": f["attn_a_x"].reshape(TOK, DM),
        "wa": np.concatenate([group(f["attn_a_W_Q"]), group(f["attn_a_W_K"]), group(f["attn_a_W_V"]), wo], 2),
        "ba": np.stack([f["attn_a_b_Q"].T, f["attn_a_b_K"].T, f["attn_a_b_V"].T], axis=1),
        "bo": f["attn_a_b_O"].reshape(1, DM),
        "ident": np.eye(P, dtype=np.float32),
        "mask_tri": np.triu(np.full((P, P), MASKED, np.float32), 1),
        "wqa": np.concatenate([wqa, wqa], 2),
        "wqb_t": wqb[:, :, :NOPE].transpose(2, 1, 0),
        "wqb_pe": wqb_pe,
        "wqb_sw": pe_sw[:, :, ::-1, :].reshape(RANK, HEADS // 2, P),
        "wkva": np.concatenate([c_, pe_, pe_, c_, pe_[:, :, swap], pe_[:, :, swap]], 2),
        "wkvbk_t": wkvb[:, :, :NOPE].transpose(2, 1, 0),
        "wkvbv_t": wkvb[:, :, NOPE:].transpose(2, 1, 0),
        "wout_b": f["attn_b_Wout"].reshape(HEADS, NOPE, DM).transpose(1, 0, 2),
        "rope_tab": rope_tab,
        "conv_w": rows(f["ffn_conv_w"]),
        "wmix": np.concatenate([rows(f[f"ffn_{n}"]) for n in ("Wq", "Wg", "Wk", "Wv")], 2),
        "wv_t": rows(f["ffn_Wv"].T),
        "router": rows(router.reshape(MIX_DV, 2 * MIX_H)),
        "wmix_out": rows(f["ffn_Wout"]),
        "rot_tab": np.broadcast_to(rot_tab[None], (P, *rot_tab.shape)),
    }
    arrays = {n: np.ascontiguousarray(a) for n, a in arrays.items()}
    nc = bacc.Bacc("TRN2", target_bir_lowering=False, num_devices=1)
    args = [nc.dram_tensor(n, a.shape, mybir.dt.from_np(a.dtype), kind="ExternalInput").ap()
            for n, a in arrays.items()]
    out = nc.dram_tensor("out", [TOK, DM], F32, kind="ExternalOutput").ap()
    hybrid_program(nc, *args, out)
    result = run_bass_kernel_spmd(nc, [arrays], core_ids=[0])
    return result.results[0]["out"].reshape(BATCH, SEQ, DM)
```
